# Optimizing a Trainium2 kernel written in Bass

```python
import numpy as np
import jax
import jax.numpy as jnp

def _softmax(x, axis=-1):
    return jax.nn.softmax(x, axis=axis)

def _gelu(x):
    return jax.nn.gelu(x, approximate=True)

def _silu(x):
    return jax.nn.silu(x)

def _sigmoid(x):
    return jax.nn.sigmoid(x)

def _layernorm(x, axis=-1, eps=1e-05):
    m = jnp.mean(x, axis=axis, keepdims=True)
    v = jnp.var(x, axis=axis, keepdims=True)
    return (x - m) / jnp.sqrt(v + eps)

def _scatter_add(tgt, idx, src, axis=0):
    return tgt.at[idx].add(src)

def _segment_sum(src, seg, n):
    return jax.ops.segment_sum(src, seg, n)
kernel_name = 'mk_flamingo_gated_d1_seqx_r4_baa6c3'

def setup_inputs(seed: int=0):
    np.random.seed(seed)
    _w = jnp.asarray

    def _rec_inputs():
        import jax
        import jax.numpy as jnp
        _rk = jax.random.key(seed)
        x = -0.0002928 + 1 * jax.random.normal(jax.random.fold_in(_rk, 1), (64, 128, 256), jnp.float32)
        _lenS = 128 - jax.random.randint(jax.random.fold_in(_rk, 7), (64,), 0, max(1, 128 // 4) + 1, jnp.int32)
        _lenS2 = 128 - jax.random.randint(jax.random.fold_in(_rk, 8), (64,), 0, max(1, 128 // 4) + 1, jnp.int32)
        _ctx_1024P = jax.random.normal(jax.random.fold_in(_rk, 11), (64, 16, 256), jnp.float32)
        _ctx_1024c = jax.random.dirichlet(jax.random.fold_in(_rk, 511), 0.3 * jnp.ones((16,), jnp.float32), (64, 128))
        _ctx_1024t = jnp.einsum('bsk,bkd->bsd', _ctx_1024c, _ctx_1024P)
        _ctx_1024t = _ctx_1024t * jax.lax.rsqrt(jnp.mean(jnp.square(_ctx_1024t)) + 1e-12) * 0.953939
        ctx_1024 = -1.39393e-06 + 0.999914 * (_ctx_1024t + 0.3 * jax.random.normal(jax.random.fold_in(_rk, 611), (64, 128, 256), jnp.float32))
        _validS = jnp.arange(128)[None, :] < _lenS[:, None]
        _validS2 = jnp.arange(128)[None, :] < _lenS2[:, None]
        _causal = jnp.tril(jnp.ones((128, 128), dtype=bool))
        mask_BxS2_bf0 = jnp.logical_not(jnp.ones((64, 128), dtype=bool))
        _g = jax.random.normal(jax.random.fold_in(_rk, 9001), (2, 1), jnp.float32)
        _g = jnp.sign(_g) * jnp.maximum(jnp.abs(_g), 1.0) + (_g == 0) * 1.0
        g_xattn = _g[0]
        g_ffn = _g[1]
        return (x, ctx_1024, mask_BxS2_bf0, g_xattn, g_ffn)
    x, ctx_1024, mask_BxS2_bf0, g_xattn, g_ffn = _rec_inputs()

    def _L0_xattn_setup():
        import jax, jax.numpy as jnp
        import numpy as np
        DIM = 256
        HEADS = 16
        DIM_HEAD = 64
        INNER = HEADS * DIM_HEAD
        B, N = (2, 512)
        SCALE = DIM_HEAD ** (-0.5)
        key = jax.random.key(seed)
        ks = jax.random.split(key, 9)
        s_in = 1.0 / np.sqrt(DIM)
        s_inner = 1.0 / np.sqrt(INNER)
        return {'q': jax.random.normal(ks[0], (B, N, DIM), jnp.float32), 'k': jax.random.normal(ks[1], (B, N, DIM), jnp.float32), 'v': jax.random.normal(ks[2], (B, N, DIM), jnp.float32), 'Wq': jax.random.normal(ks[3], (DIM, INNER), jnp.float32) * s_in, 'Wk': jax.random.normal(ks[4], (DIM, INNER), jnp.float32) * s_in, 'Wv': jax.random.normal(ks[5], (DIM, INNER), jnp.float32) * s_in, 'Wo': jax.random.normal(ks[6], (INNER, DIM), jnp.float32) * s_inner, 'bo': jax.random.normal(ks[7], (DIM,), jnp.float32) * s_inner, 'mask': jnp.zeros((B, N), dtype=bool)}
    _L0_xattn_all = _L0_xattn_setup()
    _L0_xattn_in = {k: v for k, v in _L0_xattn_all.items() if k in ('Wq', 'Wk', 'Wv', 'Wo', 'bo')}
    del _L0_xattn_all

    def _L0_ffn_setup():
        import jax, jax.numpy as jnp
        import numpy as np
        BLOCK = 32
        W_BITS = 4
        ACT_BITS = 16

        def act_qdq(x):
            qmax = 2.0 ** (ACT_BITS - 1) - 1.0
            scale = jnp.maximum(jnp.max(jnp.abs(x)) / qmax, 1e-12)
            return jnp.clip(jnp.round(x / scale), -qmax - 1.0, qmax) * scale

        def fixed_qdq_u16(x):
            scale = 1.0 / 65536.0
            return jnp.clip(jnp.round(x / scale), 0.0, 65535.0) * scale

        def lpbq_dequant(w):
            O, I = w.shape
            qmax = 2.0 ** (W_BITS - 1) - 1.0
            wb = w.reshape(O, I // BLOCK, BLOCK)
            s = jnp.maximum(jnp.max(jnp.abs(wb), axis=-1, keepdims=True) / qmax, 1e-12)
            wq = jnp.clip(jnp.round(wb / s), -qmax - 1.0, qmax) * s
            return wq.reshape(O, I)
        key = jax.random.key(seed)
        k1, k2, k3, k4 = jax.random.split(key, 4)
        B, S, H, I = (2, 1024, 256, 768)
        x = jax.random.normal(k1, (B, S, H), jnp.float32)
        w_gate = jax.random.normal(k2, (I, H), jnp.float32) * 0.02
        w_up = jax.random.normal(k3, (I, H), jnp.float32) * 0.02
        w_down = jax.random.normal(k4, (H, I), jnp.float32) * 0.02
        return {'x': x, 'w_gate': w_gate, 'w_up': w_up, 'w_down': w_down}
    _L0_ffn_all = _L0_ffn_setup()
    _L0_ffn_in = {k: v for k, v in _L0_ffn_all.items() if k in ('w_gate', 'w_up', 'w_down')}
    del _L0_ffn_all
    return {'x': x, 'ctx_1024': ctx_1024, 'mask_BxS2_bf0': mask_BxS2_bf0, 'g_xattn': g_xattn, 'g_ffn': g_ffn, 'L0_xattn_Wq': _L0_xattn_in['Wq'], 'L0_xattn_Wk': _L0_xattn_in['Wk'], 'L0_xattn_Wv': _L0_xattn_in['Wv'], 'L0_xattn_Wo': _L0_xattn_in['Wo'], 'L0_xattn_bo': _L0_xattn_in['bo'], 'L0_ffn_w_gate': _L0_ffn_in['w_gate'], 'L0_ffn_w_up': _L0_ffn_in['w_up'], 'L0_ffn_w_down': _L0_ffn_in['w_down']}

def reference(x, ctx_1024, mask_BxS2_bf0, g_xattn, g_ffn, L0_xattn_Wq, L0_xattn_Wk, L0_xattn_Wv, L0_xattn_Wo, L0_xattn_bo, L0_ffn_w_gate, L0_ffn_w_up, L0_ffn_w_down):
    import jax
    import jax.numpy as jnp

    def _L0_xattn_ref(q, k, v, Wq, Wk, Wv, Wo, bo, mask):
        import jax, jax.numpy as jnp
        import numpy as np
        DIM = 256
        HEADS = 16
        DIM_HEAD = 64
        INNER = HEADS * DIM_HEAD
        B, N = (2, 512)
        SCALE = DIM_HEAD ** (-0.5)
        b, n, _ = q.shape
        h, d = (HEADS, DIM_HEAD)

        def split_heads(x):
            return x.reshape(b, n, h, d).transpose(0, 2, 1, 3)
        qh = split_heads(q @ Wq)
        kh = split_heads(k @ Wk)
        vh = split_heads(v @ Wv)
        dots = jnp.einsum('bhid,bhjd->bhij', qh, kh) * SCALE
        mask_value = -jnp.finfo(dots.dtype).max
        dots = jnp.where(mask[:, None, None, :], mask_value, dots)
        causal = jnp.triu(jnp.ones((n, n), dtype=bool), k=1)
        dots = jnp.where(causal[None, None, :, :], mask_value, dots)
        attn = jax.nn.softmax(dots, axis=-1)
        out = jnp.einsum('bhij,bhjd->bhid', attn, vh)
        out = out.transpose(0, 2, 1, 3).reshape(b, n, h * d)
        return out @ Wo + bo

    def _L0_ffn_ref(x, w_gate, w_up, w_down):
        import jax, jax.numpy as jnp
        import numpy as np
        BLOCK = 32
        W_BITS = 4
        ACT_BITS = 16

        def act_qdq(x):
            qmax = 2.0 ** (ACT_BITS - 1) - 1.0
            scale = jnp.maximum(jnp.max(jnp.abs(x)) / qmax, 1e-12)
            return jnp.clip(jnp.round(x / scale), -qmax - 1.0, qmax) * scale

        def fixed_qdq_u16(x):
            scale = 1.0 / 65536.0
            return jnp.clip(jnp.round(x / scale), 0.0, 65535.0) * scale

        def lpbq_dequant(w):
            O, I = w.shape
            qmax = 2.0 ** (W_BITS - 1) - 1.0
            wb = w.reshape(O, I // BLOCK, BLOCK)
            s = jnp.maximum(jnp.max(jnp.abs(wb), axis=-1, keepdims=True) / qmax, 1e-12)
            wq = jnp.clip(jnp.round(wb / s), -qmax - 1.0, qmax) * s
            return wq.reshape(O, I)
        x = act_qdq(x)
        up = act_qdq(x @ lpbq_dequant(w_up).T)
        gate = act_qdq(x @ lpbq_dequant(w_gate).T)
        sig = fixed_qdq_u16(jax.nn.sigmoid(gate))
        gate = act_qdq(gate * sig)
        o = act_qdq(gate * up)
        return o @ lpbq_dequant(w_down).T
    x = x + jnp.tanh(g_xattn[0]) * _L0_xattn_ref(_layernorm(x, axis=-1), ctx_1024, ctx_1024, L0_xattn_Wq, L0_xattn_Wk, L0_xattn_Wv, L0_xattn_Wo, L0_xattn_bo, mask_BxS2_bf0)
    x = x + jnp.tanh(g_ffn[0]) * _L0_ffn_ref(_layernorm(x, axis=-1), L0_ffn_w_gate, L0_ffn_w_up, L0_ffn_w_down)
    return x

_drawn_inputs = setup_inputs


def setup_inputs(seed=0):
    import zlib

    import numpy as np

    out = dict(_drawn_inputs(seed))
    spreads = {}
    factors = {}
    for name, (base, spread) in spreads.items():
        noise = np.random.default_rng([zlib.crc32(name.encode()), seed]).standard_normal(out[name].shape)
        drawn = base * np.exp(spread * noise) if base else spread * noise
        out[name] = jnp.asarray(drawn.astype(out[name].dtype))
    for name, factor in factors.items():
        out[name] = (out[name] * factor).astype(out[name].dtype)
    return out
```

```python
from contextlib import ExitStack

import concourse.bass as bass
from concourse import mybir

ALU = mybir.AluOpType
ACT = mybir.ActivationFunctionType
F32 = mybir.dt.float32
F32R = mybir.dt.float32r
I16 = mybir.dt.int16
U16 = mybir.dt.uint16
U8 = mybir.dt.uint8
X = mybir.AxisListType.X
ABSMAX = bass.bass_isa.ReduceOp.absmax

P = 128
NB = 4
HD = 64
SCALE = HD ** -0.5
FMAX = 3.4028234663852886e38
EPS = 1e-5
QMAX = 32767.0
TINY = 1e-12
WBLOCK = 32
WQMAX = 7.0


def split(hi, lo):
    return [(hi, hi), (lo, hi), (hi, lo)]


def wait(eng, s, n):
    if not isinstance(n, int) or n > 0:
        eng.wait_ge(s, n)


def attention(nc, x, ctx, mask, g_xattn, wq, wk, wv, wo, bo, x1_d, xn2_d, amax_x):
    B, S, D = x.shape
    INNER = wq.shape[1]
    assert S == P and D == 2 * P and INNER % P == 0 and B % NB == 0
    KC = D // P
    NC = INNER // P
    G = B // NB
    U = G * NC
    T = NB * P
    VH = 512
    assert NC == 8 and INNER == 2 * VH

    jobs = []
    for c in range(NC):
        jobs += [(c, "q", 0), (c, "k", 0)]
        if c < 2:
            jobs += [(c, "v", 2 * c), (c, "v", 2 * c + 1)]
        elif c < 6:
            jobs += [(c, "v", NB + c - 2)]
    jobs += [(NC - 1, "t", n) for n in range(2 * KC)]
    NJ = len(jobs)
    FIRST = 2 * KC
    assert NJ % 2 == 0 and FIRST % 2 == 0

    def jobs_of(c, kind):
        return [(i, n) for i, (cc, k, n) in enumerate(jobs) if cc == c and k == kind]

    def nth(g, i):
        return i % 2, (FIRST + i) // 2 + (NJ // 2) * g

    with ExitStack() as st:
        def sb(name, shape, dt=F32):
            return st.enter_context(nc.sbuf_tensor(name, shape, dt))

        def sem(name):
            return st.enter_context(nc.semaphore(name))

        w_stage = sb("w_stage", [P, KC, INNER])
        w_hi = [sb(f"w{n}_hi", [P, KC, INNER], F32R) for n in "qkv"]
        w_lo = [sb(f"w{n}_lo", [P, KC, INNER], F32R) for n in "qkv"]
        wo_sb = sb("wo_sb", [P, NC, D])
        x_in = sb("x_in", [P, NB, D])
        ctx_in = sb("ctx_in", [P, NB, D])
        xn = sb("xn", [P, NB, D])
        xres = sb("xres", [P, NB, D])
        t_hi = [sb(f"t{n}_hi", [P, KC, T], F32R) for n in "xc"]
        t_lo = [sb(f"t{n}_lo", [P, KC, T], F32R) for n in "xc"]
        qT = sb("qT", [P, T])
        kT = sb("kT", [P, T])
        v_sb = sb("v_sb", [P, NB, INNER])
        masked = sb("masked", [P, 2, NB, P])
        prob = sb("prob", [P, 2, 2, NB, P])
        probT = sb("probT", [P, 2, NB, P])
        neg_max = sb("neg_max", [P, 2, NB])
        psums = sb("psums", [P, 2, NB])
        rsums = sb("rsums", [P, 2, NB])
        outT = sb("outT", [P, T])
        mask_u8 = sb("mask_u8", [P, NB, P], U8)
        mask_add = sb("mask_add", [P, NB, P])
        causal = sb("causal", [P, P])
        ident = sb("ident", [P, P])
        x1 = sb("x1", [P, NB, D])
        xn2 = sb("xn2", [P, NB, D])
        bo_g = sb("bo_g", [P, D])
        tg = sb("tg", [P, 1])
        stats = sb("stats", [P, NB, 6])
        mean = sb("mean", [P, NB])
        stats2 = sb("stats2", [P, NB, 6])
        mean2 = sb("mean2", [P, NB])
        vare = sb("vare", [P, NB])
        vare2 = sb("vare2", [P, NB])
        m_sum, m_dif, v_sum, m_sq, v_eps = (sb(n, [P, NB]) for n in ("m_sum", "m_dif", "v_sum", "m_sq", "v_eps"))
        rstd = sb("rstd", [P, NB])
        rstd2 = sb("rstd2", [P, NB])
        mhalf = sb("mhalf", [P, NB])

        proj = [st.enter_context(nc.psum_tensor(f"proj{b}", [P, T], F32)) for b in range(2)]
        score = [st.enter_context(nc.psum_tensor(f"score{h}", [P, NB, P], F32)) for h in range(2)]
        trans = st.enter_context(nc.psum_tensor("trans", [P, NB, P], F32))
        pv = st.enter_context(nc.psum_tensor("pv", [P, NB, P], F32))
        y = st.enter_context(nc.psum_tensor("y", [P, NB, D], F32))

        w_loaded = sem("w_loaded")
        w_high = sem("w_high")
        w_ready = sem("w_ready")
        wo_loaded = sem("wo_loaded")
        small_loaded = sem("small_loaded")
        x_loaded = sem("x_loaded")
        ctx_loaded = sem("ctx_loaded")
        mask_loaded = sem("mask_loaded")
        ident_zero = sem("ident_zero")
        consts = sem("consts")
        gate_ready = sem("gate_ready")
        bo_ready = sem("bo_ready")
        stats_done = sem("stats_done")
        var_ready = sem("var_ready")
        rstd_ready = sem("rstd_ready")
        xn_ready = sem("xn_ready")
        xres_ready = sem("xres_ready")
        mask_ready = sem("mask_ready")
        projected = [sem(f"projected{b}") for b in range(2)]
        copied = [sem(f"copied{b}") for b in range(2)]
        high_done = sem("high_done")
        scored = sem("scored")
        masked_done = sem("masked_done")
        max_done = sem("max_done")
        exp_done = sem("exp_done")
        recip_done = sem("recip_done")
        normed = sem("normed")
        transposed = sem("transposed")
        probT_copied = [sem(f"probT_copied{h}") for h in range(2)]
        pv_done = sem("pv_done")
        outT_copied = sem("outT_copied")
        wo_done = sem("wo_done")
        x1_ready = sem("x1_ready")
        stats2_done = sem("stats2_done")
        var2_ready = sem("var2_ready")
        rstd2_ready = sem("rstd2_ready")
        xn2_ready = sem("xn2_ready")
        x1_stored = sem("x1_stored")
        xn2_stored = sem("xn2_stored")

        def drive(eng, step):
            for c in range(NC):
                step(0, c)
            with eng.Fori(1, G - 1) as i:
                for c in range(NC):
                    step(i, c)
            for c in range(NC):
                step(G - 1, c)
            for c in range(2):
                step(G, c)

        def parts(g, c):
            u = g * NC + c
            if not isinstance(g, int):
                return u, True, True, True, True
            return u, u < U, 0 < u <= U, 2 <= u < U + 2, g < G - 1

        block = st.enter_context(nc.Block())

        @block.sync
        def _(sp):
            def load_ctx(g):
                sp.dma_start(ctx_in[:], ctx[bass.ds(g * NB, NB)].rearrange("b p d -> p b d")).then_inc(ctx_loaded, 16)

            def load_x(g):
                sp.dma_start(x_in[:], x[bass.ds(g * NB, NB)].rearrange("b p d -> p b d")).then_inc(x_loaded, 16)

            def load_mask(g):
                rows = mask[bass.ds(g * NB, NB)].rearrange("(o b) k -> o b k", o=1)
                sp.dma_start(mask_u8[:], rows.broadcast_to([P, NB, P])).then_inc(mask_loaded, 16)

            load_x(0)
            load_ctx(0)
            sp.dma_start(tg[:], g_xattn.rearrange("(o n) -> o n", o=1).broadcast_to([P, 1])).then_inc(small_loaded, 16)
            sp.dma_start(bo_g[:], bo.rearrange("(o n) -> o n", o=1).broadcast_to([P, D])).then_inc(small_loaded, 16)
            load_mask(0)
            for n, w in enumerate((wq, wk, wv)):
                wait(sp, w_ready, n)
                sp.dma_start(w_stage[:], w.rearrange("(c p) n -> p c n", p=P)).then_inc(w_loaded, 16)
            sp.dma_start(wo_sb[:], wo.rearrange("(c p) n -> p c n", p=P)).then_inc(wo_loaded, 16)

            def store(g):
                sp.wait_ge(x1_ready, g + 1)
                sp.dma_start(x1_d[:, g], x1[:]).then_inc(x1_stored, 16)
                sp.wait_ge(xn2_ready, NB * (g + 1))
                sp.dma_start(xn2_d[:, g], xn2[:]).then_inc(xn2_stored, 16)

            def load_next(g):
                sp.wait_ge(mask_ready, g + 1)
                sp.wait_ge(projected[1], nth(g, 1)[1])
                load_ctx(g + 1)
                load_mask(g + 1)
                sp.wait_ge(xn_ready, g + 1)
                sp.wait_ge(xres_ready, g + 1)
                load_x(g + 1)

            load_next(0)
            with sp.Fori(1, G - 1) as i:
                load_next(i)
                store(i - 1)
            store(G - 2)
            store(G - 1)
            sp.wait_ge(x1_stored, 16 * G)
            sp.wait_ge(xn2_stored, 16 * G)

        @block.gpsimd
        def _(gp):
            gp.memset(ident[:], 0.0).then_inc(ident_zero, 1)
            gp.memset(causal[:], 0.0).then_inc(ident_zero, 1)
            gp.wait_ge(ident_zero, 2)
            gp.affine_select(out=ident[:], in_=ident[:], compare_op=ALU.not_equal, fill=1.0, base=0,
                             pattern=[[-1, P]], channel_multiplier=1).then_inc(consts, 1)
            gp.affine_select(out=causal[:], in_=causal[:], compare_op=ALU.is_ge, fill=-FMAX, base=0,
                             pattern=[[-1, P]], channel_multiplier=1).then_inc(consts, 1)
            gp.memset(mhalf[:], -0.5).then_inc(consts, 1)
            gp.wait_ge(gate_ready, 1)
            gp.tensor_scalar(bo_g[:], bo_g[:], tg[:, 0:1], None, ALU.mult).then_inc(bo_ready, 1)
            gp.wait_ge(bo_ready, 1)
            gp.wait_ge(consts, 3)

            def make_rstd(g):
                gp.wait_ge(var_ready, g + 1)
                gp.tensor_tensor(rstd[:], vare[:], mhalf[:], ALU.pow).then_inc(rstd_ready, 1)

            def make_rstd2(g):
                gp.wait_ge(var2_ready, g + 1)
                gp.tensor_tensor(rstd2[:], vare2[:], mhalf[:], ALU.pow).then_inc(rstd2_ready, 1)

            def step(g, c):
                u, new, soft, old, more = parts(g, c)
                if soft:
                    for h in range(2):
                        gp.wait_ge(recip_done, 2 * (u - 1) + h + 1)
                        pr = prob[:, (c + 1) % 2, h]
                        gp.tensor_tensor(pr, pr, rsums[:, h, :].rearrange("p (b o) -> p b o", o=1).broadcast_to([P, NB, P]),
                                         ALU.mult).then_inc(normed, 1)
                if c == 2 and new:
                    gp.wait_ge(x_loaded, 16 * (g + 1))
                    wait(gp, x1_ready, g)
                    gp.tensor_tensor(xres[:], x_in[:], bo_g[:].rearrange("p (o n) -> p o n", o=1).broadcast_to([P, NB, D]),
                                     ALU.add).then_inc(xres_ready, 1)
                if c == 3 and new and not (isinstance(g, int) and g == 0):
                    make_rstd2(g - 1)
                if c == 5 and new and more:
                    make_rstd(g + 1)

            make_rstd(0)
            drive(gp, step)
            make_rstd2(G - 1)

        @block.scalar
        def _(act):
            act.wait_ge(small_loaded, 32)
            nc.scalar.activation(tg[:], tg[:], ACT.Tanh).then_inc(gate_ready, 1)
            for n in range(3):
                act.wait_ge(w_loaded, 16 * (n + 1))
                nc.scalar.activation(w_hi[n][:], w_stage[:], ACT.Copy).then_inc(w_high, 1)

            def high(g, i, n):
                b, before = nth(g, i)
                act.wait_ge(projected[b], before + 1)
                nc.scalar.activation(t_hi[n // KC][:, n % KC, :], proj[b][:], ACT.Copy).then_inc(high_done, 1)

            def exps(u, c, h):
                wait(act, transposed, 2 * (u - 2) + h + 1)
                act.wait_ge(max_done, 2 * u + h + 1)
                wait(act, normed, 2 * (u - 1) + h + 1)
                for b in range(NB):
                    nc.scalar.activation(prob[:, c % 2, h, b, :], masked[:, h, b, :], ACT.Exp,
                                         bias=neg_max[:, h, b:b + 1],
                                         accum_out=psums[:, h, b:b + 1]).then_inc(exp_done, 1)

            def step(g, c):
                u, new, soft, old, more = parts(g, c)
                if new:
                    (i, _), = jobs_of(c, "q")
                    b, before = nth(g, i)
                    act.wait_ge(projected[b], before + 1)
                    wait(act, scored, 2 * u)
                    nc.scalar.activation(qT[:], proj[b][:], ACT.Copy, scale=SCALE).then_inc(copied[b], 1)
                if old:
                    act.wait_ge(transposed, 2 * (u - 2) + 1)
                    wait(act, pv_done, u - 2)
                    nc.scalar.activation(probT[:, 0], trans[:], ACT.Copy).then_inc(probT_copied[0], 1)
                if soft:
                    exps(u - 1, c + 1, 0)
                if c == NC - 1 and new and more:
                    high(g, jobs_of(c, "t")[0][0], 0)
                if soft:
                    exps(u - 1, c + 1, 1)
                if c == NC - 1 and new and more:
                    high(g, jobs_of(c, "t")[1][0], 1)
                if old:
                    act.wait_ge(pv_done, u - 1)
                    wait(act, wo_done, u - 2)
                    nc.scalar.activation(outT[:], pv[:], ACT.Copy).then_inc(outT_copied, 1)
                if c == NC - 1 and new and more:
                    high(g, jobs_of(c, "t")[2][0], 2)
                    high(g, jobs_of(c, "t")[3][0], 3)

            for n in range(2 * KC):
                high(-1, NJ - FIRST + n, n)
            drive(act, step)

        @block.vector
        def _(dve):
            for n in range(3):
                dve.wait_ge(w_high, n + 1)
                nc.vector.tensor_tensor(w_lo[n][:], w_stage[:], w_hi[n][:].bitcast(F32), ALU.subtract).then_inc(w_ready, 1)

            MOMENTS = NB + 6

            def moments(stats, mean, var_eps, done, n, ready):
                v = nc.vector
                dve.wait_ge(done, n)
                v.tensor_tensor(m_sum[:], stats[:, :, 1], stats[:, :, 4], ALU.add).then_inc(done, 1)
                v.tensor_tensor(m_dif[:], stats[:, :, 1], stats[:, :, 4], ALU.subtract).then_inc(done, 1)
                v.tensor_tensor(v_sum[:], stats[:, :, 2], stats[:, :, 5], ALU.add).then_inc(done, 1)
                dve.wait_ge(done, n + 3)
                v.tensor_scalar(mean[:], m_sum[:], 0.5, None, ALU.mult).then_inc(done, 1)
                v.tensor_tensor(m_sq[:], m_dif[:], m_dif[:], ALU.mult).then_inc(done, 1)
                v.tensor_scalar(v_eps[:], v_sum[:], 1.0 / D, EPS, ALU.mult, ALU.add).then_inc(done, 1)
                dve.wait_ge(done, n + 6)
                v.scalar_tensor_tensor(var_eps[:], m_sq[:], 0.25, v_eps[:], ALU.mult, ALU.add).then_inc(ready, 1)

            def layernorm_stats(g):
                dve.wait_ge(x_loaded, 16 * (g + 1))
                for b in range(NB):
                    nc.vector.bn_stats(stats[:, b, :], x_in[:, b, :]).then_inc(stats_done, 1)
                moments(stats, mean, vare, stats_done, MOMENTS * g + NB, var_ready)

            def normalise(g):
                dve.wait_ge(rstd_ready, g + 1)
                for b in range(NB):
                    last = nc.vector.tensor_scalar(xn[:, b, :], x_in[:, b, :], mean[:, b:b + 1], rstd[:, b:b + 1],
                                                   ALU.subtract, ALU.mult)
                last.then_inc(xn_ready, 1)

            def low(g, i, n, high_before):
                b, before = nth(g, i)
                dve.wait_ge(high_done, high_before + 1)
                nc.vector.tensor_tensor(t_lo[n // KC][:, n % KC, :], proj[b][:], t_hi[n // KC][:, n % KC, :].bitcast(F32),
                                        ALU.subtract).then_inc(copied[b], 1)

            def step(g, c):
                u, new, soft, old, more = parts(g, c)
                if soft:
                    for h in range(2):
                        n = 2 * (u - 1) + h + 1
                        dve.wait_ge(scored, n)
                        wait(dve, exp_done, NB * (n - 2))
                        nc.vector.tensor_tensor(masked[:, h], score[h][:], mask_add[:], ALU.add).then_inc(masked_done, 1)
                        dve.wait_ge(masked_done, n)
                        nc.vector.tensor_reduce(neg_max[:, h, :], masked[:, h], X, ALU.max, negate=True).then_inc(max_done, 1)
                if c == 0 and new:
                    dve.wait_ge(mask_loaded, 16 * (g + 1))
                    if isinstance(g, int) and g == 0:
                        dve.wait_ge(consts, 2)
                    nc.vector.scalar_tensor_tensor(mask_add[:], mask_u8[:], -FMAX,
                                                   causal[:].rearrange("p (o k) -> p o k", o=1).broadcast_to([P, NB, P]),
                                                   ALU.mult, ALU.min).then_inc(mask_ready, 1)
                    dve.wait_ge(mask_ready, g + 1)
                if new:
                    (i, _), = jobs_of(c, "k")
                    b, before = nth(g, i)
                    dve.wait_ge(projected[b], before + 1)
                    wait(dve, scored, 2 * u)
                    nc.vector.tensor_copy(kT[:], proj[b][:]).then_inc(copied[b], 1)
                if old:
                    dve.wait_ge(transposed, 2 * (u - 2) + 2)
                    wait(dve, pv_done, u - 2)
                    nc.vector.tensor_copy(probT[:, 1], trans[:]).then_inc(probT_copied[1], 1)
                if new:
                    for i, n in jobs_of(c, "v"):
                        b, before = nth(g, i)
                        dve.wait_ge(projected[b], before + 1)
                        cols = slice((n // NB) * VH, (n // NB + 1) * VH)
                        nc.vector.tensor_copy(v_sb[:, n % NB, cols], proj[b][:]).then_inc(copied[b], 1)
                if soft:
                    for h in range(2):
                        n = 2 * (u - 1) + h + 1
                        dve.wait_ge(exp_done, NB * n)
                        wait(dve, normed, n - 2)
                        nc.vector.reciprocal(rsums[:, h, :], psums[:, h, :]).then_inc(recip_done, 1)
                if c == NC - 1 and new and more:
                    for i, n in jobs_of(c, "t"):
                        low(g, i, n, 2 * KC * (g + 1) + n)
                if c == 2 and new and not (isinstance(g, int) and g == 0):
                    residual(g - 1)
                if c == 3 and new and not (isinstance(g, int) and g == 0):
                    second_stats(g - 1)
                if c == 4 and new and not (isinstance(g, int) and g == 0):
                    second_norm(g - 1)
                if c == 5 and new and more:
                    layernorm_stats(g + 1)
                if c == 6 and new and more:
                    normalise(g + 1)

            def residual(g):
                dve.wait_ge(wo_done, NC * (g + 1))
                dve.wait_ge(xres_ready, g + 1)
                wait(dve, x1_stored, 16 * g)
                half = NB // 2
                nc.vector.scalar_tensor_tensor(x1[:, 0:half], y[:, 0:half], tg[:, 0:1], xres[:, 0:half], ALU.mult, ALU.add)
                nc.vector.scalar_tensor_tensor(x1[:, half:NB], y[:, half:NB], tg[:, 0:1], xres[:, half:NB],
                                               ALU.mult, ALU.add).then_inc(x1_ready, 1)

            def second_stats(g):
                dve.wait_ge(x1_ready, g + 1)
                for b in range(NB):
                    nc.vector.bn_stats(stats2[:, b, :], x1[:, b, :]).then_inc(stats2_done, 1)
                moments(stats2, mean2, vare2, stats2_done, MOMENTS * g + NB, var2_ready)

            def second_norm(g):
                dve.wait_ge(rstd2_ready, g + 1)
                wait(dve, xn2_stored, 16 * g)
                for b in range(NB):
                    nc.vector.tensor_scalar(xn2[:, b, :], x1[:, b, :], mean2[:, b:b + 1], rstd2[:, b:b + 1],
                                            ALU.subtract, ALU.mult).then_inc(xn2_ready, 1)
                dve.wait_ge(xn2_ready, NB * (g + 1))
                nc.vector.tensor_reduce(amax_x[:, bass.ds(g, 1)],
                                        xn2[:].rearrange("p b d -> p (b d)"), X, ALU.max, apply_absolute_value=True)

            layernorm_stats(0)
            normalise(0)
            for n in range(2 * KC):
                low(-1, NJ - FIRST + n, n, n)
            drive(dve, step)
            residual(G - 1)
            second_stats(G - 1)
            second_norm(G - 1)

        @block.tensor
        def _(pe):
            pe.wait_ge(consts, 1)

            def product(b, before, stat, mov, n=KC):
                wait(pe, copied[b], before)
                passes = [(k, s, m) for k in range(n) for s, m in split(0, 1)]
                for j, (k, s, m) in enumerate(passes):
                    last = nc.tensor.matmul(proj[b][:], stat(s, k), mov(m, k), start=(j == 0), stop=(j == len(passes) - 1))
                last.then_inc(projected[b], 1)

            def weights_left(g, c, i, n):
                b, before = nth(g, i)
                w, t = (w_hi[n], w_lo[n]), (t_hi[n], t_lo[n])
                product(b, before, lambda s, k: w[s][:, k, c * P:(c + 1) * P], lambda m, k: t[m][:, k, :])

            def value(g, i, n):
                b, before = nth(g, i)
                e, half = n % NB, n // NB
                t, w = (t_hi[1], t_lo[1]), (w_hi[2], w_lo[2])
                product(b, before, lambda s, k: t[s][:, k, e * P:(e + 1) * P], lambda m, k: w[m][:, k, half * VH:(half + 1) * VH])

            def transpose_in(g, i, n):
                b, before = nth(g, i)
                if n == 0:
                    pe.wait_ge(xn_ready, g + 2)
                if n == KC:
                    pe.wait_ge(ctx_loaded, 16 * (g + 2))
                wait(pe, copied[b], before)
                src = (xn, ctx_in)[n // KC]
                for e in range(NB):
                    last = nc.tensor.transpose(proj[b][:, e * P:(e + 1) * P], src[:, e, (n % KC) * P:(n % KC + 1) * P], ident[:])
                last.then_inc(projected[b], 1)

            def transpose_prob(u, c, h):
                pe.wait_ge(normed, 2 * u + h + 1)
                wait(pe, probT_copied[1 - h], u + h)
                for b in range(NB):
                    last = nc.tensor.transpose(trans[:, b, :], prob[:, c % 2, h, b, :], ident[:])
                last.then_inc(transposed, 1)

            def times_v(u, c, h):
                pe.wait_ge(probT_copied[h], u + 1)
                if h == 0:
                    wait(pe, outT_copied, u)
                for b in range(NB):
                    last = nc.tensor.matmul(pv[h * HD:(h + 1) * HD, b, :], v_sb[:, b, c * P + h * HD:c * P + (h + 1) * HD],
                                            probT[:, h, b, :], start=True, stop=True)
                if h == 1:
                    last.then_inc(pv_done, 1)

            def scores(g, c, u):
                for kind in "qk":
                    (i, _), = jobs_of(c, kind)
                    b, before = nth(g, i)
                    pe.wait_ge(copied[b], before + 1)
                for h in range(2):
                    wait(pe, masked_done, 2 * (u - 1) + h + 1)
                rows = [slice(h * HD, (h + 1) * HD) for h in range(2)]
                for b in range(NB):
                    for h in range(2):
                        last = nc.tensor.matmul(score[h][:, b, :], qT[rows[h], b * P:(b + 1) * P], kT[rows[h], b * P:(b + 1) * P],
                                                start=True, stop=True)
                        if b == NB - 1:
                            last.then_inc(scored, 1)

            def out_product(u, c):
                pe.wait_ge(outT_copied, u + 1)
                for b in range(NB):
                    last = nc.tensor.matmul(y[:, b, :], outT[:, b * P:(b + 1) * P], wo_sb[:, c, :],
                                            start=(c == 0 and b % 2 == 0), stop=(c == NC - 1), skip_group_check=True)
                    if b == NB - 1:
                        last.then_inc(wo_done, 1)

            def step(g, c):
                u, new, soft, old, more = parts(g, c)
                co = (c - 2) % NC
                nxt = c == NC - 1 and new and more
                ts = jobs_of(c, "t")
                if new:
                    weights_left(g, c, jobs_of(c, "q")[0][0], 0)
                if old:
                    transpose_prob(u - 2, co, 0)
                if new:
                    weights_left(g, c, jobs_of(c, "k")[0][0], 1)
                if old:
                    transpose_prob(u - 2, co, 1)
                if new:
                    for i, n in jobs_of(c, "v"):
                        value(g, i, n)
                if nxt:
                    transpose_in(g, *ts[0])
                if old:
                    times_v(u - 2, co, 0)
                if nxt:
                    transpose_in(g, *ts[1])
                if old:
                    times_v(u - 2, co, 1)
                if nxt:
                    transpose_in(g, *ts[2])
                if new:
                    scores(g, c, u)
                if nxt:
                    transpose_in(g, *ts[3])
                if old:
                    if co == 0 and c == 2:
                        wait(pe, x1_ready, g)
                    out_product(u - 2, co)

            for n in range(2 * KC):
                transpose_in(-1, NJ - FIRST + n, n)
            pe.wait_ge(w_ready, 3)
            pe.wait_ge(wo_loaded, 16)
            drive(pe, step)


def up_and_gate(nc, w_up, w_gate, w_down, xn2_d, up_d, gate_d, wd, amax_x, amax_up, amax_gate, s_x, G):
    I, D = w_up.shape
    KC, IC, T = D // P, I // P, NB * P
    J = 2 * IC
    RING = 6
    W1 = IC * D
    NBLK = 3 * W1 // WBLOCK
    assert J % RING == 0
    with ExitStack() as st:
        def sb(name, shape, dt=F32):
            return st.enter_context(nc.sbuf_tensor(name, shape, dt))

        def sem(name):
            return st.enter_context(nc.semaphore(name))

        w_raw = sb("w_raw", [P, 3 * W1])
        w_int = sb("w_int", [P, 3 * W1], I16)
        w_max = sb("w_max", [P, NBLK])
        w_scale = sb("w_scale", [P, NBLK])
        w_inv = sb("w_inv", [P, NBLK])
        wug = [sb(f"wug_{n}", [P, KC, 2 * I], F32R) for n in ("hi", "lo")]
        ident = sb("ident2", [P, P])
        xin = sb("xin", [P, 2, NB, D])
        n16 = sb("n16", [P, 2, KC, T], I16)
        xT = [[sb(f"xT{n}{b}", [P, KC, T], F32R) for n in ("hi", "lo")] for b in range(2)]
        stage = sb("stage", [P, 2, J, T])
        a1 = sb("a1", [P, 1])
        a2 = sb("a2", [P, 1])
        inv_x = sb("inv_x", [P, 1])
        ring = [st.enter_context(nc.psum_tensor(f"ring{n}", [P, T], F32)) for n in range(RING)]
        tr = [st.enter_context(nc.psum_tensor(f"tr{k}", [P, T], F32)) for k in range(KC)]

        w_loaded = sem("w_loaded2")
        zeroed = sem("zeroed")
        ident_ready = sem("ident_ready")
        quantised = sem("quantised")
        w_transposed = sem("w_transposed")
        w_high = sem("w_high2")
        w_copied = sem("w_copied")
        amax_local = sem("amax_local")
        amax_all = sem("amax_all")
        scale_step = sem("scale_step")
        x_loaded = [sem(f"xn2_loaded{b}") for b in range(2)]
        x_transposed = sem("x_transposed")
        x_int = sem("x_int")
        x_high = sem("x_high")
        x_ready = sem("x_ready")
        product_done = sem("product_done")
        staged = sem("staged")
        reduced = sem("reduced")
        stored = [sem(f"ug_stored{b}") for b in range(2)]
        block = st.enter_context(nc.Block())

        HI = IC // 2
        w_jobs = [("ug", m, k, h) for m in range(2) for k in range(KC) for h in range(2)] + [("d", i, 0, 0) for i in range(HI)]

        @block.sync
        def _(sp):
            for n, w in enumerate((w_up, w_gate, w_down)):
                sp.dma_start(w_raw[:, n * W1:(n + 1) * W1].rearrange("p (c n) -> p c n", n=w.shape[1]),
                             w.rearrange("(c p) n -> p c n", p=P)).then_inc(w_loaded, 16)

            def load(t, b):
                sp.dma_start(xin[:, b], xn2_d[:, t]).then_inc(x_loaded[b], 16)

            def step(t, b, more):
                if more:
                    sp.wait_ge(x_transposed, KC * (t + 1))
                    load(t + 2, b)
                for half, dram in ((0, up_d), (1, gate_d)):
                    sp.wait_ge(staged, J * t + IC * (half + 1))
                    sp.dma_start(dram[:, t], stage[:, b, half * IC:(half + 1) * IC]).then_inc(stored[b], 16)

            load(0, 0)
            load(1, 1)
            with sp.Fori(0, G // 2 - 1) as i:
                for b in range(2):
                    step(2 * i + b, b, True)
            for b in range(2):
                step(G - 2 + b, b, False)
            for b in range(2):
                sp.wait_ge(stored[b], 16 * G)

        @block.gpsimd
        def _(gp):
            gp.memset(ident[:], 0.0).then_inc(zeroed, 1)
            gp.wait_ge(zeroed, 1)
            gp.affine_select(out=ident[:], in_=ident[:], compare_op=ALU.not_equal, fill=1.0, base=0,
                             pattern=[[-1, P]], channel_multiplier=1).then_inc(ident_ready, 1)
            gp.wait_ge(amax_local, 1)
            gp.partition_all_reduce(a2[:], a1[:], P, ABSMAX).then_inc(amax_all, 1)

        @block.scalar
        def _(act):
            for n, (kind, m, k, h) in enumerate(w_jobs):
                act.wait_ge(w_transposed, n + 1)
                if kind == "ug":
                    o = m * I + h * HI * P
                    nc.scalar.activation(wug[0][:, k, o:o + HI * P], ring[n % RING][:, 0:HI * P], ACT.Copy).then_inc(w_high, 1)
                else:
                    nc.scalar.activation(wd[:, 2 * m:2 * m + 2, :], ring[n % RING][:].rearrange("p (c n) -> p c n", n=D),
                                         ACT.Copy).then_inc(w_high, 1)

            def high(t, b):
                for k in range(KC):
                    act.wait_ge(x_int, KC * t + k + 1)
                    wait(act, product_done, J * (t - 1))
                    nc.scalar.activation(xT[b][0][:, k, :], n16[:, b, k, :], ACT.Copy).then_inc(x_high, 1)

            def step(t, b=None, last=False):
                b = t % 2 if isinstance(t, int) else b
                if not last:
                    high(t + 1, 1 - b)
                for n in range(J):
                    act.wait_ge(product_done, J * t + n + 1)
                    if n % IC == 0:
                        wait(act, reduced, 2 * (t - 2) + n // IC + 1)
                        wait(act, stored[b], 16 * (t - b))
                    nc.scalar.activation(stage[:, b, n, :], ring[n % RING][:], ACT.Copy).then_inc(staged, 1)

            high(0, 0)
            step(0)
            step(1)
            with act.Fori(1, G // 2 - 1) as i:
                step(2 * i, 0)
                step(2 * i + 1, 1)
            step(G - 2)
            step(G - 1, last=True)

        @block.vector
        def _(dve):
            v = nc.vector
            v.tensor_reduce(a1[:], amax_x[:], X, ALU.max).then_inc(amax_local, 1)
            dve.wait_ge(w_loaded, 48)
            blocks = w_raw[:].rearrange("p (a b) -> p a b", b=WBLOCK)
            v.tensor_reduce(w_max[:], blocks, X, ALU.max, apply_absolute_value=True).then_inc(quantised, 1)
            dve.wait_ge(quantised, 1)
            v.tensor_scalar(w_scale[:], w_max[:], 1.0 / WQMAX, TINY, ALU.mult, ALU.max).then_inc(quantised, 1)
            dve.wait_ge(quantised, 2)
            v.reciprocal(w_inv[:], w_scale[:]).then_inc(quantised, 1)
            dve.wait_ge(quantised, 3)

            def wide(a):
                return a[:].rearrange("p (a o) -> p a o", o=1).broadcast_to([P, NBLK, WBLOCK])

            ints = w_int[:].rearrange("p (a b) -> p a b", b=WBLOCK)
            v.tensor_tensor(ints, blocks, wide(w_inv), ALU.mult).then_inc(quantised, 1)
            dve.wait_ge(quantised, 4)
            v.tensor_tensor(blocks, ints, wide(w_scale), ALU.mult).then_inc(quantised, 1)
            dve.wait_ge(amax_all, 1)
            v.tensor_scalar(s_x[:], a2[:], 1.0 / QMAX, TINY, ALU.mult, ALU.max).then_inc(scale_step, 1)
            dve.wait_ge(scale_step, 1)
            v.reciprocal(inv_x[:], s_x[:]).then_inc(scale_step, 1)
            dve.wait_ge(scale_step, 2)
            for n, (kind, m, k, h) in enumerate(w_jobs):
                dve.wait_ge(w_high, n + 1)
                if kind == "ug":
                    o = m * I + h * HI * P
                    v.tensor_tensor(wug[1][:, k, o:o + HI * P], ring[n % RING][:, 0:HI * P],
                                    wug[0][:, k, o:o + HI * P].bitcast(F32), ALU.subtract).then_inc(w_copied, 1)

            def quantise_x(t, b):
                for k in range(KC):
                    dve.wait_ge(x_transposed, KC * t + k + 1)
                    wait(dve, x_high, KC * (t - 2) + k + 1)
                    v.tensor_scalar(n16[:, b, k, :], tr[k][:], inv_x[:, 0:1], None, ALU.mult).then_inc(x_int, 1)
                for k in range(KC):
                    dve.wait_ge(x_high, KC * t + k + 1)
                    v.tensor_tensor(xT[b][1][:, k, :], n16[:, b, k, :], xT[b][0][:, k, :].bitcast(F32), ALU.subtract).then_inc(x_ready, 1)

            def step(t, b=None, last=False):
                b = t % 2 if isinstance(t, int) else b
                if not last:
                    quantise_x(t + 1, 1 - b)
                for half, amax in ((0, amax_up), (1, amax_gate)):
                    dve.wait_ge(staged, J * t + IC * (half + 1))
                    v.tensor_reduce(amax[:, bass.ds(t, 1)], stage[:, b, half * IC:(half + 1) * IC].rearrange("p j n -> p (j n)"),
                                    X, ALU.max, apply_absolute_value=True).then_inc(reduced, 1)

            quantise_x(0, 0)
            step(0)
            step(1)
            with dve.Fori(1, G // 2 - 1) as i:
                step(2 * i, 0)
                step(2 * i + 1, 1)
            step(G - 2)
            step(G - 1, last=True)

        @block.tensor
        def _(pe):
            pe.wait_ge(ident_ready, 1)
            pe.wait_ge(quantised, 5)
            nug = sum(j[0] == "ug" for j in w_jobs)
            for n, (kind, m, k, h) in enumerate(w_jobs):
                if n >= RING:
                    pe.wait_ge(w_copied, min(n - RING + 1, nug))
                for e in range(HI if kind == "ug" else 4):
                    if kind == "ug":
                        at = m * W1 + (h * HI + e) * D + k * P
                    else:
                        at = 2 * W1 + (e % 2) * I + (2 * m + e // 2) * P
                    last = nc.tensor.transpose(ring[n % RING][:, e * P:(e + 1) * P], w_raw[:, at:at + P], ident[:])
                last.then_inc(w_transposed, 1)
            pe.wait_ge(w_copied, nug)
            pe.wait_ge(w_high, len(w_jobs))

            def transpose_x(t, b):
                pe.wait_ge(x_loaded[b], 8 * (t - b) + 16)
                for k in range(KC):
                    wait(pe, x_int, KC * (t - 1) + k + 1)
                    for e in range(NB):
                        last = nc.tensor.transpose(tr[k][:, e * P:(e + 1) * P], xin[:, b, e, k * P:(k + 1) * P], ident[:])
                    last.then_inc(x_transposed, 1)

            def step(t, b=None, last=False):
                b = t % 2 if isinstance(t, int) else b
                if not last:
                    transpose_x(t + 1, 1 - b)
                pe.wait_ge(x_ready, KC * (t + 1))
                for n in range(J):
                    wait(pe, staged, J * t + n + 1 - RING)
                    passes = [(k, s, m) for k in range(KC) for s, m in split(0, 1)]
                    for j, (k, s, m) in enumerate(passes):
                        mm = nc.tensor.matmul(ring[n % RING][:], wug[s][:, k, n * P:(n + 1) * P], xT[b][m][:, k, :],
                                              start=(j == 0), stop=(j == len(passes) - 1))
                    mm.then_inc(product_done, 1)

            transpose_x(0, 0)
            step(0)
            step(1)
            with pe.Fori(1, G // 2 - 1) as i:
                step(2 * i, 0)
                step(2 * i + 1, 1)
            step(G - 2)
            step(G - 1, last=True)


def gate_block(nc, gate_d, prod_d, amax_up, amax_gate, amax_prod, s_x, s_g, k_u, s_u, G, N):
    with ExitStack() as st:
        def sb(name, shape, dt=F32):
            return st.enter_context(nc.sbuf_tensor(name, shape, dt))

        def sem(name):
            return st.enter_context(nc.semaphore(name))

        gate = sb("gate", [P, 2, N])
        n_g = sb("n_g", [P, 2, N], I16)
        sig = sb("sig", [P, 2, N])
        n_s = sb("n_s", [P, 2, N], U16)
        prod = sb("prod", [P, 2, N])
        a1 = sb("a1g", [P, 2])
        a2 = sb("a2g", [P, 2])
        a3 = sb("a3g", [P, 2])
        sug = sb("sug", [P, 2])
        rug = sb("rug", [P, 2])
        kug = sb("kug", [P, 2])
        loaded = [sem(f"gate_loaded{b}") for b in range(2)]
        amax_local = sem("amax_local3")
        amax_all = sem("amax_all3")
        scale_step = sem("scale_step3")
        rounded = sem("rounded3")
        sig_done = sem("sig_done")
        sig_int = sem("sig_int")
        prod_done = sem("prod_done")
        reduced = sem("reduced3")
        stored = [sem(f"prod_stored{b}") for b in range(2)]
        block = st.enter_context(nc.Block())

        @block.sync
        def _(sp):
            def load(t, b):
                sp.dma_start(gate[:, b], gate_d[:, t].rearrange("p j n -> p (j n)")).then_inc(loaded[b], 16)

            def step(t, b, more):
                if more:
                    sp.wait_ge(rounded, t + 1)
                    load(t + 2, b)
                sp.wait_ge(prod_done, t + 1)
                sp.dma_start(prod_d[:, t].rearrange("p j n -> p (j n)"), prod[:, b]).then_inc(stored[b], 16)

            load(0, 0)
            load(1, 1)
            with sp.Fori(0, G // 2 - 1) as i:
                for b in range(2):
                    step(2 * i + b, b, True)
            for b in range(2):
                step(G - 2 + b, b, False)
            for b in range(2):
                sp.wait_ge(stored[b], 8 * G)

        @block.gpsimd
        def _(gp):
            gp.wait_ge(amax_local, 2)
            gp.partition_all_reduce(a2[:], a1[:], P, ABSMAX).then_inc(amax_all, 1)

        @block.scalar
        def _(act):
            act.wait_ge(scale_step, 6)

            def step(t, b=None):
                b = t % 2 if isinstance(t, int) else b
                act.wait_ge(loaded[b], 8 * (t - b) + 16)
                wait(act, prod_done, t - 1)
                nc.scalar.activation(n_g[:, b], gate[:, b], ACT.Copy, scale=kug[:, 1:2]).then_inc(rounded, 1)
                act.wait_ge(rounded, t + 1)
                nc.scalar.activation(sig[:, b], n_g[:, b], ACT.Sigmoid, scale=s_g[:, 0:1]).then_inc(sig_done, 1)

            step(0)
            step(1)
            with act.Fori(1, G // 2) as i:
                step(2 * i, 0)
                step(2 * i + 1, 1)

        @block.vector
        def _(dve):
            v = nc.vector
            v.tensor_reduce(a1[:, 0:1], amax_up[:], X, ALU.max).then_inc(amax_local, 1)
            v.tensor_reduce(a1[:, 1:2], amax_gate[:], X, ALU.max).then_inc(amax_local, 1)
            dve.wait_ge(amax_all, 1)
            v.tensor_scalar(a3[:], a2[:], s_x[:, 0:1], 1.0 / QMAX, ALU.mult, ALU.mult).then_inc(scale_step, 1)
            dve.wait_ge(scale_step, 1)
            v.tensor_scalar(sug[:], a3[:], TINY, None, ALU.max).then_inc(scale_step, 1)
            dve.wait_ge(scale_step, 2)
            v.reciprocal(rug[:], sug[:]).then_inc(scale_step, 1)
            v.tensor_copy(s_u[:], sug[:, 0:1])
            v.tensor_copy(s_g[:], sug[:, 1:2]).then_inc(scale_step, 1)
            dve.wait_ge(scale_step, 4)
            v.tensor_scalar(kug[:], rug[:], s_x[:, 0:1], None, ALU.mult).then_inc(scale_step, 1)
            dve.wait_ge(scale_step, 5)
            v.tensor_copy(k_u[:], kug[:, 0:1]).then_inc(scale_step, 1)

            def step(t, b=None):
                b = t % 2 if isinstance(t, int) else b
                dve.wait_ge(sig_done, t + 1)
                v.tensor_scalar(n_s[:, b], sig[:, b], 65536.0, 65535.0, ALU.mult, ALU.min).then_inc(sig_int, 1)
                dve.wait_ge(sig_int, t + 1)
                wait(dve, stored[b], 8 * (t - b))
                v.tensor_tensor(prod[:, b], n_g[:, b], n_s[:, b], ALU.mult).then_inc(prod_done, 1)
                dve.wait_ge(prod_done, t + 1)
                v.tensor_reduce(amax_prod[:, bass.ds(t, 1)], prod[:, b], X, ALU.max, apply_absolute_value=True).then_inc(reduced, 1)

            step(0)
            step(1)
            with dve.Fori(1, G // 2) as i:
                step(2 * i, 0)
                step(2 * i + 1, 1)


def hidden_block(nc, prod_d, up_d, hid_d, amax_prod, amax_hid, s_g, k_u, s_u, s_hid, G, N):
    with ExitStack() as st:
        def sb(name, shape, dt=F32):
            return st.enter_context(nc.sbuf_tensor(name, shape, dt))

        def sem(name):
            return st.enter_context(nc.semaphore(name))

        prod = sb("prod4", [P, 2, N])
        up = sb("up4", [P, 2, N])
        n_p = sb("n_p", [P, 2, N], I16)
        n_u = sb("n_u", [P, 2, N], I16)
        hid = sb("hid", [P, 2, N])
        a1 = sb("a1h", [P, 1])
        a2 = sb("a2h", [P, 1])
        sp_ = sb("s_prod_unit", [P, 1])
        a3 = sb("a3h", [P, 1])
        s_p = sb("s_p", [P, 1])
        r_p = sb("r_p", [P, 1])
        k_p = sb("k_p", [P, 1])
        loaded = [sem(f"pu_loaded{b}") for b in range(2)]
        amax_local = sem("amax_local4")
        amax_all = sem("amax_all4")
        scale_step = sem("scale_step4")
        gate_int = sem("gate_int")
        up_int = sem("up_int")
        hid_done = sem("hid_done")
        stored = [sem(f"hid_stored{b}") for b in range(2)]
        block = st.enter_context(nc.Block())

        @block.sync
        def _(sp):
            def load(t, b):
                sp.dma_start(prod[:, b], prod_d[:, t].rearrange("p j n -> p (j n)")).then_inc(loaded[b], 16)
                sp.dma_start(up[:, b], up_d[:, t].rearrange("p j n -> p (j n)")).then_inc(loaded[b], 16)

            def step(t, b, more):
                if more:
                    sp.wait_ge(gate_int, t + 1)
                    sp.wait_ge(up_int, t + 1)
                    load(t + 2, b)
                sp.wait_ge(hid_done, t + 1)
                sp.dma_start(hid_d[:, t].rearrange("p j n -> p (j n)"), hid[:, b]).then_inc(stored[b], 16)

            load(0, 0)
            load(1, 1)
            with sp.Fori(0, G // 2 - 1) as i:
                for b in range(2):
                    step(2 * i + b, b, True)
            for b in range(2):
                step(G - 2 + b, b, False)
            for b in range(2):
                sp.wait_ge(stored[b], 8 * G)

        @block.gpsimd
        def _(gp):
            gp.wait_ge(amax_local, 1)
            gp.partition_all_reduce(a2[:], a1[:], P, ABSMAX).then_inc(amax_all, 1)

        @block.scalar
        def _(act):
            act.wait_ge(scale_step, 6)

            def step(t, b=None):
                b = t % 2 if isinstance(t, int) else b
                act.wait_ge(loaded[b], 16 * (t - b) + 32)
                wait(act, hid_done, t - 1)
                nc.scalar.activation(n_p[:, b], prod[:, b], ACT.Copy, scale=k_p[:, 0:1]).then_inc(gate_int, 1)

            step(0)
            step(1)
            with act.Fori(1, G // 2) as i:
                step(2 * i, 0)
                step(2 * i + 1, 1)

        @block.vector
        def _(dve):
            v = nc.vector
            v.tensor_reduce(a1[:], amax_prod[:], X, ALU.max).then_inc(amax_local, 1)
            v.tensor_scalar(sp_[:], s_g[:], 1.0 / 65536.0, None, ALU.mult).then_inc(scale_step, 1)
            dve.wait_ge(amax_all, 1)
            dve.wait_ge(scale_step, 1)
            v.tensor_scalar(a3[:], a2[:], sp_[:, 0:1], 1.0 / QMAX, ALU.mult, ALU.mult).then_inc(scale_step, 1)
            dve.wait_ge(scale_step, 2)
            v.tensor_scalar(s_p[:], a3[:], TINY, None, ALU.max).then_inc(scale_step, 1)
            dve.wait_ge(scale_step, 3)
            v.reciprocal(r_p[:], s_p[:]).then_inc(scale_step, 1)
            dve.wait_ge(scale_step, 4)
            v.tensor_scalar(k_p[:], r_p[:], sp_[:, 0:1], None, ALU.mult).then_inc(scale_step, 1)
            v.tensor_tensor(s_hid[:], s_p[:], s_u[:], ALU.mult).then_inc(scale_step, 1)

            def step(t, b=None):
                b = t % 2 if isinstance(t, int) else b
                dve.wait_ge(loaded[b], 16 * (t - b) + 32)
                v.tensor_scalar(n_u[:, b], up[:, b], k_u[:, 0:1], None, ALU.mult).then_inc(up_int, 1)
                dve.wait_ge(up_int, t + 1)
                dve.wait_ge(gate_int, t + 1)
                wait(dve, stored[b], 8 * (t - b))
                v.tensor_tensor(hid[:, b], n_p[:, b], n_u[:, b], ALU.mult).then_inc(hid_done, 1)
                dve.wait_ge(hid_done, t + 1)
                v.tensor_reduce(amax_hid[:, bass.ds(t, 1)], hid[:, b], X, ALU.max, apply_absolute_value=True)

            step(0)
            step(1)
            with dve.Fori(1, G // 2) as i:
                step(2 * i, 0)
                step(2 * i + 1, 1)


def down_block(nc, hid_d, x1_d, g_ffn, wd, out, amax_hid, s_hid, G, IC):
    D = wd.shape[2]
    T = NB * P
    N = IC * T
    with ExitStack() as st:
        def sb(name, shape, dt=F32):
            return st.enter_context(nc.sbuf_tensor(name, shape, dt))

        def sem(name):
            return st.enter_context(nc.semaphore(name))

        hid = sb("hid5", [P, 2, N])
        n_h = sb("n_h", [P, 2, N], I16)
        f_h = sb("f_h", [P, 2, IC, T])
        x1 = sb("x1_5", [P, 2, NB, D])
        res = sb("res", [P, 2, NB, D])
        tg = sb("tg5", [P, 1])
        a1 = sb("a1o", [P, 1])
        a2 = sb("a2o", [P, 1])
        a3 = sb("a3o", [P, 1])
        s_o = sb("s_o", [P, 1])
        r_o = sb("r_o", [P, 1])
        k_o = sb("k_o", [P, 1])
        y_scale = sb("y_scale", [P, 1])
        y = [st.enter_context(nc.psum_tensor(f"y5{b}", [P, NB, D], F32)) for b in range(2)]
        tg_loaded = sem("tg_loaded5")
        tg_ready = sem("tg_ready5")
        hid_loaded = [sem(f"hid_loaded{b}") for b in range(2)]
        x1_loaded = [sem(f"x1_loaded{b}") for b in range(2)]
        amax_local = sem("amax_local5")
        amax_all = sem("amax_all5")
        scale_step = sem("scale_step5")
        rounded = sem("rounded5")
        widened = sem("widened")
        y_done = sem("y_done5")
        res_done = sem("res_done")
        stored = [sem(f"out_stored{b}") for b in range(2)]
        block = st.enter_context(nc.Block())

        @block.sync
        def _(sp):
            sp.dma_start(tg[:], g_ffn.rearrange("(o n) -> o n", o=1).broadcast_to([P, 1])).then_inc(tg_loaded, 16)

            def load(t, b):
                sp.dma_start(hid[:, b], hid_d[:, t].rearrange("p j n -> p (j n)")).then_inc(hid_loaded[b], 16)

            def load_x1(t, b):
                sp.dma_start(x1[:, b], x1_d[:, t]).then_inc(x1_loaded[b], 16)

            def step(t, b, more):
                if more:
                    sp.wait_ge(rounded, t + 1)
                    load(t + 2, b)
                sp.wait_ge(res_done, t + 1)
                sp.dma_start(out[bass.ds(t * NB, NB)].rearrange("b p d -> p b d"), res[:, b]).then_inc(stored[b], 16)
                if more:
                    load_x1(t + 2, b)

            for b in range(2):
                load(b, b)
                load_x1(b, b)
            with sp.Fori(0, G // 2 - 1) as i:
                for b in range(2):
                    step(2 * i + b, b, True)
            for b in range(2):
                step(G - 2 + b, b, False)
            for b in range(2):
                sp.wait_ge(stored[b], 8 * G)

        @block.gpsimd
        def _(gp):
            gp.wait_ge(amax_local, 1)
            gp.partition_all_reduce(a2[:], a1[:], P, ABSMAX).then_inc(amax_all, 1)

        @block.scalar
        def _(act):
            act.wait_ge(tg_loaded, 16)
            nc.scalar.activation(tg[:], tg[:], ACT.Tanh).then_inc(tg_ready, 1)

            def step(t, b=None):
                b = t % 2 if isinstance(t, int) else b
                act.wait_ge(rounded, t + 1)
                wait(act, y_done, t - 1)
                nc.scalar.activation(f_h[:, b].rearrange("p j n -> p (j n)"), n_h[:, b], ACT.Copy).then_inc(widened, 1)

            step(0)
            step(1)
            with act.Fori(1, G // 2) as i:
                step(2 * i, 0)
                step(2 * i + 1, 1)

        @block.vector
        def _(dve):
            v = nc.vector
            v.tensor_reduce(a1[:], amax_hid[:], X, ALU.max).then_inc(amax_local, 1)
            dve.wait_ge(amax_all, 1)
            v.tensor_scalar(a3[:], a2[:], s_hid[:, 0:1], 1.0 / QMAX, ALU.mult, ALU.mult).then_inc(scale_step, 1)
            dve.wait_ge(scale_step, 1)
            v.tensor_scalar(s_o[:], a3[:], TINY, None, ALU.max).then_inc(scale_step, 1)
            dve.wait_ge(scale_step, 2)
            v.reciprocal(r_o[:], s_o[:]).then_inc(scale_step, 1)
            dve.wait_ge(scale_step, 3)
            v.tensor_scalar(k_o[:], r_o[:], s_hid[:, 0:1], None, ALU.mult).then_inc(scale_step, 1)
            dve.wait_ge(tg_ready, 1)
            v.tensor_tensor(y_scale[:], s_o[:], tg[:], ALU.mult).then_inc(scale_step, 1)
            dve.wait_ge(scale_step, 5)

            def quantise(t, b):
                dve.wait_ge(hid_loaded[b], 8 * (t - b) + 16)
                wait(dve, widened, t - 1)
                v.tensor_scalar(n_h[:, b], hid[:, b], k_o[:, 0:1], None, ALU.mult).then_inc(rounded, 1)

            def step(t, b=None, last=False):
                b = t % 2 if isinstance(t, int) else b
                if not last:
                    quantise(t + 1, 1 - b)
                dve.wait_ge(y_done, t + 1)
                dve.wait_ge(x1_loaded[b], 8 * (t - b) + 16)
                wait(dve, stored[b], 8 * (t - b))
                for h in range(2):
                    rows = slice(h * NB // 2, (h + 1) * NB // 2)
                    last_op = v.scalar_tensor_tensor(res[:, b, rows], y[b][:, rows], y_scale[:, 0:1], x1[:, b, rows], ALU.mult, ALU.add)
                last_op.then_inc(res_done, 1)

            quantise(0, 0)
            step(0)
            step(1)
            with dve.Fori(1, G // 2 - 1) as i:
                step(2 * i, 0)
                step(2 * i + 1, 1)
            step(G - 2)
            step(G - 1, last=True)

        @block.tensor
        def _(pe):
            def step(t, b=None):
                b = t % 2 if isinstance(t, int) else b
                pe.wait_ge(widened, t + 1)
                wait(pe, res_done, t - 1)
                for e in range(NB):
                    for j in range(IC):
                        mm = nc.tensor.matmul(y[b][:, e, :], f_h[:, b, j, e * P:(e + 1) * P], wd[:, j, :],
                                              start=(j == 0), stop=(j == IC - 1))
                mm.then_inc(y_done, 1)

            step(0)
            step(1)
            with pe.Fori(1, G // 2) as i:
                step(2 * i, 0)
                step(2 * i + 1, 1)


def program(nc, x, ctx, mask, g_xattn, g_ffn, wq, wk, wv, wo, bo, w_gate, w_up, w_down, out):
    B, S, D = x.shape
    I = w_up.shape[0]
    G, IC, T = B // NB, I // P, NB * P
    assert G % 2 == 0 and G >= 6

    def dram(name, shape):
        return nc.dram_tensor(name, shape, F32, kind="Internal").ap()

    x1_d = dram("x1_d", (P, G, NB, D))
    xn2_d = dram("xn2_d", (P, G, NB, D))
    up_d, gate_d, prod_d, hid_d = (dram(n, (P, G, IC, T)) for n in ("up_d", "gate_d", "prod_d", "hid_d"))

    with ExitStack() as st:
        def sb(name, shape):
            return st.enter_context(nc.sbuf_tensor(name, shape, F32))

        amax_x, amax_up, amax_gate, amax_prod, amax_hid = (sb(f"amax_{n}", [P, G]) for n in ("x", "up", "gate", "prod", "hid"))
        s_x, s_g, s_u, k_u, s_hid = (sb(n, [P, 1]) for n in ("s_x", "s_g", "s_u", "k_u", "s_hid"))
        wd = sb("wd", [P, IC, D])
        attention(nc, x, ctx, mask, g_xattn, wq, wk, wv, wo, bo, x1_d, xn2_d, amax_x)
        up_and_gate(nc, w_up, w_gate, w_down, xn2_d, up_d, gate_d, wd, amax_x, amax_up, amax_gate, s_x, G)
        gate_block(nc, gate_d, prod_d, amax_up, amax_gate, amax_prod, s_x, s_g, k_u, s_u, G, IC * T)
        hidden_block(nc, prod_d, up_d, hid_d, amax_prod, amax_hid, s_g, k_u, s_u, s_hid, G, IC * T)
        down_block(nc, hid_d, x1_d, g_ffn, wd, out, amax_hid, s_hid, G, IC)


INPUTS = ["x", "ctx_1024", "mask_BxS2_bf0", "g_xattn", "g_ffn", "L0_xattn_Wq", "L0_xattn_Wk", "L0_xattn_Wv", "L0_xattn_Wo",
          "L0_xattn_bo", "L0_ffn_w_gate", "L0_ffn_w_up", "L0_ffn_w_down"]


def kernel(**inputs):
    import numpy as np
    import concourse.bacc as bacc
    from concourse.bass_utils import run_bass_kernel_spmd

    nc = bacc.Bacc("TRN2", target_bir_lowering=False, num_devices=1)
    arrays, args = {}, []
    for name in INPUTS:
        a = np.ascontiguousarray(inputs[name])
        arrays[f"in_{name}"] = a
        args.append(nc.dram_tensor(f"in_{name}", a.shape, mybir.dt.from_np(a.dtype), kind="ExternalInput").ap())
    out = nc.dram_tensor("out_x", inputs["x"].shape, F32, kind="ExternalOutput").ap()
    program(nc, *args, out)
    r = run_bass_kernel_spmd(nc, [arrays], core_ids=[0])
    return np.asarray(r.results[0]["out_x"])
```

```python
from contextlib import ExitStack

import concourse.bass as bass
from concourse import mybir

ALU = mybir.AluOpType
ACT = mybir.ActivationFunctionType
F32 = mybir.dt.float32
F32R = mybir.dt.float32r
I16 = mybir.dt.int16
U16 = mybir.dt.uint16
U8 = mybir.dt.uint8
X = mybir.AxisListType.X
ABSMAX = bass.bass_isa.ReduceOp.absmax

P = 128
NB = 4
HD = 64
SCALE = HD ** -0.5
FMAX = 3.4028234663852886e38
EPS = 1e-5
QMAX = 32767.0
TINY = 1e-12
WBLOCK = 32
WQMAX = 7.0


def split(hi, lo):
    return [(hi, hi), (lo, hi), (hi, lo)]


def wait(eng, s, n):
    if not isinstance(n, int) or n > 0:
        eng.wait_ge(s, n)


def attention(nc, x, ctx, mask, g_xattn, wq, wk, wv, wo, bo, x1_d, xn2_d, amax_x):
    B, S, D = x.shape
    INNER = wq.shape[1]
    assert S == P and D == 2 * P and INNER % P == 0 and B % NB == 0
    KC = D // P
    NC = INNER // P
    G = B // NB
    U = G * NC
    T = NB * P
    VH = 512
    assert NC == 8 and INNER == 2 * VH

    jobs = []
    for c in range(NC):
        jobs += [(c, "q", 0), (c, "k", 0)]
        if c < 2:
            jobs += [(c, "v", 2 * c), (c, "v", 2 * c + 1)]
        elif c < 6:
            jobs += [(c, "v", NB + c - 2)]
    jobs += [(NC - 1, "t", n) for n in range(2 * KC)]
    NJ = len(jobs)
    FIRST = 2 * KC
    assert NJ % 2 == 0 and FIRST % 2 == 0

    def jobs_of(c, kind):
        return [(i, n) for i, (cc, k, n) in enumerate(jobs) if cc == c and k == kind]

    def nth(g, i):
        return i % 2, (FIRST + i) // 2 + (NJ // 2) * g

    with ExitStack() as st:
        def sb(name, shape, dt=F32):
            return st.enter_context(nc.sbuf_tensor(name, shape, dt))

        def sem(name):
            return st.enter_context(nc.semaphore(name))

        w_stage = sb("w_stage", [P, KC, INNER])
        w_hi = [sb(f"w{n}_hi", [P, KC, INNER], F32R) for n in "qkv"]
        w_lo = [sb(f"w{n}_lo", [P, KC, INNER], F32R) for n in "qkv"]
        wo_sb = sb("wo_sb", [P, NC, D])
        x_in = sb("x_in", [P, NB, D])
        ctx_in = sb("ctx_in", [P, NB, D])
        xn = sb("xn", [P, NB, D])
        xres = sb("xres", [P, NB, D])
        t_hi = [sb(f"t{n}_hi", [P, KC, T], F32R) for n in "xc"]
        t_lo = [sb(f"t{n}_lo", [P, KC, T], F32R) for n in "xc"]
        qT = sb("qT", [P, T])
        kT = sb("kT", [P, T])
        v_sb = sb("v_sb", [P, NB, INNER])
        masked = sb("masked", [P, 2, NB, P])
        prob = sb("prob", [P, 2, 2, NB, P])
        probT = sb("probT", [P, 2, NB, P])
        neg_max = sb("neg_max", [P, 2, NB])
        psums = sb("psums", [P, 2, NB])
        rsums = sb("rsums", [P, 2, NB])
        outT = sb("outT", [P, T])
        mask_u8 = sb("mask_u8", [P, NB, P], U8)
        mask_add = sb("mask_add", [P, NB, P])
        causal = sb("causal", [P, P])
        ident = sb("ident", [P, P])
        x1 = sb("x1", [P, NB, D])
        xn2 = sb("xn2", [P, NB, D])
        bo_g = sb("bo_g", [P, D])
        tg = sb("tg", [P, 1])
        stats = sb("stats", [P, NB, 6])
        mean = sb("mean", [P, NB])
        stats2 = sb("stats2", [P, NB, 6])
        mean2 = sb("mean2", [P, NB])
        vare = sb("vare", [P, NB])
        vare2 = sb("vare2", [P, NB])
        m_sum, m_dif, v_sum, m_sq, v_eps = (sb(n, [P, NB]) for n in ("m_sum", "m_dif", "v_sum", "m_sq", "v_eps"))
        rstd = sb("rstd", [P, NB])
        rstd2 = sb("rstd2", [P, NB])
        mhalf = sb("mhalf", [P, NB])

        proj = [st.enter_context(nc.psum_tensor(f"proj{b}", [P, T], F32)) for b in range(2)]
        score = [st.enter_context(nc.psum_tensor(f"score{h}", [P, NB, P], F32)) for h in range(2)]
        trans = st.enter_context(nc.psum_tensor("trans", [P, NB, P], F32))
        pv = st.enter_context(nc.psum_tensor("pv", [P, NB, P], F32))
        y = st.enter_context(nc.psum_tensor("y", [P, NB, D], F32))

        w_loaded = sem("w_loaded")
        w_high = sem("w_high")
        w_ready = sem("w_ready")
        wo_loaded = sem("wo_loaded")
        small_loaded = sem("small_loaded")
        x_loaded = sem("x_loaded")
        ctx_loaded = sem("ctx_loaded")
        mask_loaded = sem("mask_loaded")
        ident_zero = sem("ident_zero")
        consts = sem("consts")
        gate_ready = sem("gate_ready")
        bo_ready = sem("bo_ready")
        stats_done = sem("stats_done")
        var_ready = sem("var_ready")
        rstd_ready = sem("rstd_ready")
        xn_ready = sem("xn_ready")
        xres_ready = sem("xres_ready")
        mask_ready = sem("mask_ready")
        projected = [sem(f"projected{b}") for b in range(2)]
        copied = [sem(f"copied{b}") for b in range(2)]
        high_done = sem("high_done")
        scored = sem("scored")
        masked_done = sem("masked_done")
        max_done = sem("max_done")
        exp_done = sem("exp_done")
        recip_done = sem("recip_done")
        normed = sem("normed")
        transposed = sem("transposed")
        probT_copied = [sem(f"probT_copied{h}") for h in range(2)]
        pv_done = sem("pv_done")
        outT_copied = sem("outT_copied")
        wo_done = sem("wo_done")
        x1_ready = sem("x1_ready")
        stats2_done = sem("stats2_done")
        var2_ready = sem("var2_ready")
        rstd2_ready = sem("rstd2_ready")
        xn2_ready = sem("xn2_ready")
        x1_stored = sem("x1_stored")
        xn2_stored = sem("xn2_stored")

        def drive(eng, step):
            for c in range(NC):
                step(0, c)
            with eng.Fori(1, G - 1) as i:
                for c in range(NC):
                    step(i, c)
            for c in range(NC):
                step(G - 1, c)
            for c in range(2):
                step(G, c)

        def parts(g, c):
            u = g * NC + c
            if not isinstance(g, int):
                return u, True, True, True, True
            return u, u < U, 0 < u <= U, 2 <= u < U + 2, g < G - 1

        block = st.enter_context(nc.Block())

        @block.sync
        def _(sp):
            def load_ctx(g):
                sp.dma_start(ctx_in[:], ctx[bass.ds(g * NB, NB)].rearrange("b p d -> p b d")).then_inc(ctx_loaded, 16)

            def load_x(g):
                sp.dma_start(x_in[:], x[bass.ds(g * NB, NB)].rearrange("b p d -> p b d")).then_inc(x_loaded, 16)

            def load_mask(g):
                rows = mask[bass.ds(g * NB, NB)].rearrange("(o b) k -> o b k", o=1)
                sp.dma_start(mask_u8[:], rows.broadcast_to([P, NB, P])).then_inc(mask_loaded, 16)

            load_x(0)
            load_ctx(0)
            sp.dma_start(tg[:], g_xattn.rearrange("(o n) -> o n", o=1).broadcast_to([P, 1])).then_inc(small_loaded, 16)
            sp.dma_start(bo_g[:], bo.rearrange("(o n) -> o n", o=1).broadcast_to([P, D])).then_inc(small_loaded, 16)
            load_mask(0)
            for n, w in enumerate((wq, wk, wv)):
                wait(sp, w_ready, n)
                sp.dma_start(w_stage[:], w.rearrange("(c p) n -> p c n", p=P)).then_inc(w_loaded, 16)
            sp.dma_start(wo_sb[:], wo.rearrange("(c p) n -> p c n", p=P)).then_inc(wo_loaded, 16)

            def store(g):
                sp.wait_ge(x1_ready, g + 1)
                sp.dma_start(x1_d[:, g], x1[:]).then_inc(x1_stored, 16)
                sp.wait_ge(xn2_ready, NB * (g + 1))
                sp.dma_start(xn2_d[:, g], xn2[:]).then_inc(xn2_stored, 16)

            def load_next(g):
                sp.wait_ge(mask_ready, g + 1)
                sp.wait_ge(projected[1], nth(g, 1)[1])
                load_ctx(g + 1)
                load_mask(g + 1)
                sp.wait_ge(xn_ready, g + 1)
                sp.wait_ge(xres_ready, g + 1)
                load_x(g + 1)

            load_next(0)
            with sp.Fori(1, G - 1) as i:
                load_next(i)
                store(i - 1)
            store(G - 2)
            store(G - 1)
            sp.wait_ge(x1_stored, 16 * G)
            sp.wait_ge(xn2_stored, 16 * G)

        @block.gpsimd
        def _(gp):
            gp.memset(ident[:], 0.0).then_inc(ident_zero, 1)
            gp.memset(causal[:], 0.0).then_inc(ident_zero, 1)
            gp.wait_ge(ident_zero, 2)
            gp.affine_select(out=ident[:], in_=ident[:], compare_op=ALU.not_equal, fill=1.0, base=0,
                             pattern=[[-1, P]], channel_multiplier=1).then_inc(consts, 1)
            gp.affine_select(out=causal[:], in_=causal[:], compare_op=ALU.is_ge, fill=-FMAX, base=0,
                             pattern=[[-1, P]], channel_multiplier=1).then_inc(consts, 1)
            gp.memset(mhalf[:], -0.5).then_inc(consts, 1)
            gp.wait_ge(gate_ready, 1)
            gp.tensor_scalar(bo_g[:], bo_g[:], tg[:, 0:1], None, ALU.mult).then_inc(bo_ready, 1)
            gp.wait_ge(bo_ready, 1)
            gp.wait_ge(consts, 3)

            def make_rstd(g):
                gp.wait_ge(var_ready, g + 1)
                gp.tensor_tensor(rstd[:], vare[:], mhalf[:], ALU.pow).then_inc(rstd_ready, 1)

            def make_rstd2(g):
                gp.wait_ge(var2_ready, g + 1)
                gp.tensor_tensor(rstd2[:], vare2[:], mhalf[:], ALU.pow).then_inc(rstd2_ready, 1)

            def step(g, c):
                u, new, soft, old, more = parts(g, c)
                if soft:
                    for h in range(2):
                        gp.wait_ge(recip_done, 2 * (u - 1) + h + 1)
                        pr = prob[:, (c + 1) % 2, h]
                        gp.tensor_tensor(pr, pr, rsums[:, h, :].rearrange("p (b o) -> p b o", o=1).broadcast_to([P, NB, P]),
                                         ALU.mult).then_inc(normed, 1)
                if c == 2 and new:
                    gp.wait_ge(x_loaded, 16 * (g + 1))
                    wait(gp, x1_ready, g)
                    gp.tensor_tensor(xres[:], x_in[:], bo_g[:].rearrange("p (o n) -> p o n", o=1).broadcast_to([P, NB, D]),
                                     ALU.add).then_inc(xres_ready, 1)
                if c == 3 and new and not (isinstance(g, int) and g == 0):
                    make_rstd2(g - 1)
                if c == 5 and new and more:
                    make_rstd(g + 1)

            make_rstd(0)
            drive(gp, step)
            make_rstd2(G - 1)

        @block.scalar
        def _(act):
            act.wait_ge(small_loaded, 32)
            nc.scalar.activation(tg[:], tg[:], ACT.Tanh).then_inc(gate_ready, 1)
            for n in range(3):
                act.wait_ge(w_loaded, 16 * (n + 1))
                nc.scalar.activation(w_hi[n][:], w_stage[:], ACT.Copy).then_inc(w_high, 1)

            def high(g, i, n):
                b, before = nth(g, i)
                act.wait_ge(projected[b], before + 1)
                nc.scalar.activation(t_hi[n // KC][:, n % KC, :], proj[b][:], ACT.Copy).then_inc(high_done, 1)

            def exps(u, c, h):
                wait(act, transposed, 2 * (u - 2) + h + 1)
                act.wait_ge(max_done, 2 * u + h + 1)
                wait(act, normed, 2 * (u - 1) + h + 1)
                for b in range(NB):
                    nc.scalar.activation(prob[:, c % 2, h, b, :], masked[:, h, b, :], ACT.Exp,
                                         bias=neg_max[:, h, b:b + 1],
                                         accum_out=psums[:, h, b:b + 1]).then_inc(exp_done, 1)

            def step(g, c):
                u, new, soft, old, more = parts(g, c)
                if new:
                    (i, _), = jobs_of(c, "q")
                    b, before = nth(g, i)
                    act.wait_ge(projected[b], before + 1)
                    wait(act, scored, 2 * u)
                    nc.scalar.activation(qT[:], proj[b][:], ACT.Copy, scale=SCALE).then_inc(copied[b], 1)
                if old:
                    act.wait_ge(transposed, 2 * (u - 2) + 1)
                    wait(act, pv_done, u - 2)
                    nc.scalar.activation(probT[:, 0], trans[:], ACT.Copy).then_inc(probT_copied[0], 1)
                if soft:
                    exps(u - 1, c + 1, 0)
                if c == NC - 1 and new and more:
                    high(g, jobs_of(c, "t")[0][0], 0)
                if soft:
                    exps(u - 1, c + 1, 1)
                if c == NC - 1 and new and more:
                    high(g, jobs_of(c, "t")[1][0], 1)
                if old:
                    act.wait_ge(pv_done, u - 1)
                    wait(act, wo_done, u - 2)
                    nc.scalar.activation(outT[:], pv[:], ACT.Copy).then_inc(outT_copied, 1)
                if c == NC - 1 and new and more:
                    high(g, jobs_of(c, "t")[2][0], 2)
                    high(g, jobs_of(c, "t")[3][0], 3)

            for n in range(2 * KC):
                high(-1, NJ - FIRST + n, n)
            drive(act, step)

        @block.vector
        def _(dve):
            for n in range(3):
                dve.wait_ge(w_high, n + 1)
                nc.vector.tensor_tensor(w_lo[n][:], w_stage[:], w_hi[n][:].bitcast(F32), ALU.subtract).then_inc(w_ready, 1)

            MOMENTS = NB + 6

            def moments(stats, mean, var_eps, done, n, ready):
                v = nc.vector
                dve.wait_ge(done, n)
                v.tensor_tensor(m_sum[:], stats[:, :, 1], stats[:, :, 4], ALU.add).then_inc(done, 1)
                v.tensor_tensor(m_dif[:], stats[:, :, 1], stats[:, :, 4], ALU.subtract).then_inc(done, 1)
                v.tensor_tensor(v_sum[:], stats[:, :, 2], stats[:, :, 5], ALU.add).then_inc(done, 1)
                dve.wait_ge(done, n + 3)
                v.tensor_scalar(mean[:], m_sum[:], 0.5, None, ALU.mult).then_inc(done, 1)
                v.tensor_tensor(m_sq[:], m_dif[:], m_dif[:], ALU.mult).then_inc(done, 1)
                v.tensor_scalar(v_eps[:], v_sum[:], 1.0 / D, EPS, ALU.mult, ALU.add).then_inc(done, 1)
                dve.wait_ge(done, n + 6)
                v.scalar_tensor_tensor(var_eps[:], m_sq[:], 0.25, v_eps[:], ALU.mult, ALU.add).then_inc(ready, 1)

            def layernorm_stats(g):
                dve.wait_ge(x_loaded, 16 * (g + 1))
                for b in range(NB):
                    nc.vector.bn_stats(stats[:, b, :], x_in[:, b, :]).then_inc(stats_done, 1)
                moments(stats, mean, vare, stats_done, MOMENTS * g + NB, var_ready)

            def normalise(g):
                dve.wait_ge(rstd_ready, g + 1)
                for b in range(NB):
                    last = nc.vector.tensor_scalar(xn[:, b, :], x_in[:, b, :], mean[:, b:b + 1], rstd[:, b:b + 1],
                                                   ALU.subtract, ALU.mult)
                last.then_inc(xn_ready, 1)

            def low(g, i, n, high_before):
                b, before = nth(g, i)
                dve.wait_ge(high_done, high_before + 1)
                nc.vector.tensor_tensor(t_lo[n // KC][:, n % KC, :], proj[b][:], t_hi[n // KC][:, n % KC, :].bitcast(F32),
                                        ALU.subtract).then_inc(copied[b], 1)

            def step(g, c):
                u, new, soft, old, more = parts(g, c)
                if soft:
                    for h in range(2):
                        n = 2 * (u - 1) + h + 1
                        dve.wait_ge(scored, n)
                        wait(dve, exp_done, NB * (n - 2))
                        nc.vector.tensor_tensor(masked[:, h], score[h][:], mask_add[:], ALU.add).then_inc(masked_done, 1)
                        dve.wait_ge(masked_done, n)
                        nc.vector.tensor_reduce(neg_max[:, h, :], masked[:, h], X, ALU.max, negate=True).then_inc(max_done, 1)
                if c == 0 and new:
                    dve.wait_ge(mask_loaded, 16 * (g + 1))
                    if isinstance(g, int) and g == 0:
                        dve.wait_ge(consts, 2)
                    nc.vector.scalar_tensor_tensor(mask_add[:], mask_u8[:], -FMAX,
                                                   causal[:].rearrange("p (o k) -> p o k", o=1).broadcast_to([P, NB, P]),
                                                   ALU.mult, ALU.min).then_inc(mask_ready, 1)
                    dve.wait_ge(mask_ready, g + 1)
                if new:
                    (i, _), = jobs_of(c, "k")
                    b, before = nth(g, i)
                    dve.wait_ge(projected[b], before + 1)
                    wait(dve, scored, 2 * u)
                    nc.vector.tensor_copy(kT[:], proj[b][:]).then_inc(copied[b], 1)
                if old:
                    dve.wait_ge(transposed, 2 * (u - 2) + 2)
                    wait(dve, pv_done, u - 2)
                    nc.vector.tensor_copy(probT[:, 1], trans[:]).then_inc(probT_copied[1], 1)
                if new:
                    for i, n in jobs_of(c, "v"):
                        b, before = nth(g, i)
                        dve.wait_ge(projected[b], before + 1)
                        cols = slice((n // NB) * VH, (n // NB + 1) * VH)
                        nc.vector.tensor_copy(v_sb[:, n % NB, cols], proj[b][:]).then_inc(copied[b], 1)
                if soft:
                    for h in range(2):
                        n = 2 * (u - 1) + h + 1
                        dve.wait_ge(exp_done, NB * n)
                        wait(dve, normed, n - 2)
                        nc.vector.reciprocal(rsums[:, h, :], psums[:, h, :]).then_inc(recip_done, 1)
                if c == NC - 1 and new and more:
                    for i, n in jobs_of(c, "t"):
                        low(g, i, n, 2 * KC * (g + 1) + n)
                if c == 2 and new and not (isinstance(g, int) and g == 0):
                    residual(g - 1)
                if c == 3 and new and not (isinstance(g, int) and g == 0):
                    second_stats(g - 1)
                if c == 4 and new and not (isinstance(g, int) and g == 0):
                    second_norm(g - 1)
                if c == 5 and new and more:
                    layernorm_stats(g + 1)
                if c == 6 and new and more:
                    normalise(g + 1)

            def residual(g):
                dve.wait_ge(wo_done, NC * (g + 1))
                dve.wait_ge(xres_ready, g + 1)
                wait(dve, x1_stored, 16 * g)
                half = NB // 2
                nc.vector.scalar_tensor_tensor(x1[:, 0:half], y[:, 0:half], tg[:, 0:1], xres[:, 0:half], ALU.mult, ALU.add)
                nc.vector.scalar_tensor_tensor(x1[:, half:NB], y[:, half:NB], tg[:, 0:1], xres[:, half:NB],
                                               ALU.mult, ALU.add).then_inc(x1_ready, 1)

            def second_stats(g):
                dve.wait_ge(x1_ready, g + 1)
                for b in range(NB):
                    nc.vector.bn_stats(stats2[:, b, :], x1[:, b, :]).then_inc(stats2_done, 1)
                moments(stats2, mean2, vare2, stats2_done, MOMENTS * g + NB, var2_ready)

            def second_norm(g):
                dve.wait_ge(rstd2_ready, g + 1)
                wait(dve, xn2_stored, 16 * g)
                for b in range(NB):
                    nc.vector.tensor_scalar(xn2[:, b, :], x1[:, b, :], mean2[:, b:b + 1], rstd2[:, b:b + 1],
                                            ALU.subtract, ALU.mult).then_inc(xn2_ready, 1)
                dve.wait_ge(xn2_ready, NB * (g + 1))
                nc.vector.tensor_reduce(amax_x[:, bass.ds(g, 1)],
                                        xn2[:].rearrange("p b d -> p (b d)"), X, ALU.max, apply_absolute_value=True)

            layernorm_stats(0)
            normalise(0)
            for n in range(2 * KC):
                low(-1, NJ - FIRST + n, n, n)
            drive(dve, step)
            residual(G - 1)
            second_stats(G - 1)
            second_norm(G - 1)

        @block.tensor
        def _(pe):
            pe.wait_ge(consts, 1)

            def product(b, before, stat, mov, n=KC):
                wait(pe, copied[b], before)
                passes = [(k, s, m) for k in range(n) for s, m in split(0, 1)]
                for j, (k, s, m) in enumerate(passes):
                    last = nc.tensor.matmul(proj[b][:], stat(s, k), mov(m, k), start=(j == 0), stop=(j == len(passes) - 1))
                last.then_inc(projected[b], 1)

            def weights_left(g, c, i, n):
                b, before = nth(g, i)
                w, t = (w_hi[n], w_lo[n]), (t_hi[n], t_lo[n])
                product(b, before, lambda s, k: w[s][:, k, c * P:(c + 1) * P], lambda m, k: t[m][:, k, :])

            def value(g, i, n):
                b, before = nth(g, i)
                e, half = n % NB, n // NB
                t, w = (t_hi[1], t_lo[1]), (w_hi[2], w_lo[2])
                product(b, before, lambda s, k: t[s][:, k, e * P:(e + 1) * P], lambda m, k: w[m][:, k, half * VH:(half + 1) * VH])

            def transpose_in(g, i, n):
                b, before = nth(g, i)
                if n == 0:
                    pe.wait_ge(xn_ready, g + 2)
                if n == KC:
                    pe.wait_ge(ctx_loaded, 16 * (g + 2))
                wait(pe, copied[b], before)
                src = (xn, ctx_in)[n // KC]
                for e in range(NB):
                    last = nc.tensor.transpose(proj[b][:, e * P:(e + 1) * P], src[:, e, (n % KC) * P:(n % KC + 1) * P], ident[:])
                last.then_inc(projected[b], 1)

            def transpose_prob(u, c, h):
                pe.wait_ge(normed, 2 * u + h + 1)
                wait(pe, probT_copied[1 - h], u + h)
                for b in range(NB):
                    last = nc.tensor.transpose(trans[:, b, :], prob[:, c % 2, h, b, :], ident[:])
                last.then_inc(transposed, 1)

            def times_v(u, c, h):
                pe.wait_ge(probT_copied[h], u + 1)
                if h == 0:
                    wait(pe, outT_copied, u)
                for b in range(NB):
                    last = nc.tensor.matmul(pv[h * HD:(h + 1) * HD, b, :], v_sb[:, b, c * P + h * HD:c * P + (h + 1) * HD],
                                            probT[:, h, b, :], start=True, stop=True)
                if h == 1:
                    last.then_inc(pv_done, 1)

            def scores(g, c, u):
                for kind in "qk":
                    (i, _), = jobs_of(c, kind)
                    b, before = nth(g, i)
                    pe.wait_ge(copied[b], before + 1)
                for h in range(2):
                    wait(pe, masked_done, 2 * (u - 1) + h + 1)
                rows = [slice(h * HD, (h + 1) * HD) for h in range(2)]
                for b in range(NB):
                    for h in range(2):
                        last = nc.tensor.matmul(score[h][:, b, :], qT[rows[h], b * P:(b + 1) * P], kT[rows[h], b * P:(b + 1) * P],
                                                start=True, stop=True)
                        if b == NB - 1:
                            last.then_inc(scored, 1)

            def out_product(u, c):
                pe.wait_ge(outT_copied, u + 1)
                for b in range(NB):
                    last = nc.tensor.matmul(y[:, b, :], outT[:, b * P:(b + 1) * P], wo_sb[:, c, :],
                                            start=(c == 0 and b % 2 == 0), stop=(c == NC - 1), skip_group_check=True)
                    if b == NB - 1:
                        last.then_inc(wo_done, 1)

            def step(g, c):
                u, new, soft, old, more = parts(g, c)
                co = (c - 2) % NC
                nxt = c == NC - 1 and new and more
                ts = jobs_of(c, "t")
                if new:
                    weights_left(g, c, jobs_of(c, "q")[0][0], 0)
                if old:
                    transpose_prob(u - 2, co, 0)
                if new:
                    weights_left(g, c, jobs_of(c, "k")[0][0], 1)
                if old:
                    transpose_prob(u - 2, co, 1)
                if new:
                    for i, n in jobs_of(c, "v"):
                        value(g, i, n)
                if nxt:
                    transpose_in(g, *ts[0])
                if old:
                    times_v(u - 2, co, 0)
                if nxt:
                    transpose_in(g, *ts[1])
                if old:
                    times_v(u - 2, co, 1)
                if nxt:
                    transpose_in(g, *ts[2])
                if new:
                    scores(g, c, u)
                if nxt:
                    transpose_in(g, *ts[3])
                if old:
                    if co == 0 and c == 2:
                        wait(pe, x1_ready, g)
                    out_product(u - 2, co)

            for n in range(2 * KC):
                transpose_in(-1, NJ - FIRST + n, n)
            pe.wait_ge(w_ready, 3)
            pe.wait_ge(wo_loaded, 16)
            drive(pe, step)


def two_buffers(eng, G, step):
    step(0, 0, False)
    step(1, 1, False)
    with eng.Fori(1, G // 2 - 1) as i:
        step(2 * i, 0, False)
        step(2 * i + 1, 1, False)
    step(G - 2, 0, False)
    step(G - 1, 1, True)


def product(nc, bank, stat, mov, KC):
    passes = [(k, s, m) for k in range(KC) for s, m in split(0, 1)]
    for j, (k, s, m) in enumerate(passes):
        last = nc.tensor.matmul(bank, stat(s, k), mov(m, k), start=(j == 0), stop=(j == len(passes) - 1))
    return last


def gate_products(nc, w_up, w_gate, w_down, xn2_d, n_x_d, gate_d, wup, wd, amax_x, ext_gate, s_x, G):
    I, D = w_up.shape
    KC, IC, T = D // P, I // P, NB * P
    RING = IC
    W1 = IC * D
    NBLK = 3 * W1 // WBLOCK
    with ExitStack() as st:
        def sb(name, shape, dt=F32):
            return st.enter_context(nc.sbuf_tensor(name, shape, dt))

        def sem(name):
            return st.enter_context(nc.semaphore(name))

        w_raw = sb("w_raw", [P, 3 * W1])
        w_int = sb("w_int", [P, 3 * W1], I16)
        w_max = sb("w_max", [P, NBLK])
        w_scale = sb("w_scale", [P, NBLK])
        w_inv = sb("w_inv", [P, NBLK])
        wgate = [sb(f"wgate_{n}", [P, KC, I], F32R) for n in ("hi", "lo")]
        ident = sb("ident2", [P, P])
        xin = sb("xin", [P, 2, NB, D])
        n_x = sb("n_x", [P, 2, KC, T], I16)
        xT = [[sb(f"xT{n}{b}", [P, KC, T], F32R) for n in ("hi", "lo")] for b in range(2)]
        stage = sb("stage", [P, 2, IC, T])
        a1 = sb("a1", [P, 1])
        a2 = sb("a2", [P, 1])
        inv_x = sb("inv_x", [P, 1])
        ring = [st.enter_context(nc.psum_tensor(f"ring{n}", [P, T], F32)) for n in range(RING)]
        tr = [st.enter_context(nc.psum_tensor(f"tr{k}", [P, T], F32)) for k in range(KC)]

        w_loaded = sem("w_loaded2")
        zeroed = sem("zeroed")
        ident_ready = sem("ident_ready")
        dequantised = sem("dequantised")
        w_transposed = sem("w_transposed")
        w_high = sem("w_high2")
        w_copied = sem("w_copied")
        amax_local = sem("amax_local")
        amax_all = sem("amax_all")
        scale_step = sem("scale_step")
        x_loaded = [sem(f"xn2_loaded{b}") for b in range(2)]
        x_transposed = sem("x_transposed")
        x_int = sem("x_int")
        x_high = sem("x_high")
        x_ready = sem("x_ready")
        product_done = sem("product_done")
        staged = sem("staged")
        reduced = sem("reduced")
        n_x_stored = [sem(f"n_x_stored{b}") for b in range(2)]
        stored = [sem(f"gate_stored{b}") for b in range(2)]
        block = st.enter_context(nc.Block())

        HI = IC // 2
        targets = (wup, wgate)
        w_jobs = [("ug", m, k, h) for m in (1, 0) for k in range(KC) for h in range(2)] + [("d", i, 0, 0) for i in range(HI)]
        nug = 2 * 2 * KC

        @block.sync
        def _(sp):
            for n, w in enumerate((w_up, w_gate, w_down)):
                sp.dma_start(w_raw[:, n * W1:(n + 1) * W1].rearrange("p (c n) -> p c n", n=w.shape[1]),
                             w.rearrange("(c p) n -> p c n", p=P)).then_inc(w_loaded, 16)

            def load(t, b):
                sp.dma_start(xin[:, b], xn2_d[:, t]).then_inc(x_loaded[b], 16)

            def step(t, b, more):
                if more:
                    sp.wait_ge(x_transposed, KC * (t + 1))
                    load(t + 2, b)
                sp.wait_ge(x_int, KC * (t + 1))
                sp.dma_start(n_x_d[:, t], n_x[:, b]).then_inc(n_x_stored[b], 16)
                sp.wait_ge(staged, IC * (t + 1))
                sp.dma_start(gate_d[:, t], stage[:, b]).then_inc(stored[b], 16)

            load(0, 0)
            load(1, 1)
            with sp.Fori(0, G // 2 - 1) as i:
                for b in range(2):
                    step(2 * i + b, b, True)
            for b in range(2):
                step(G - 2 + b, b, False)
            for b in range(2):
                sp.wait_ge(stored[b], 8 * G)
                sp.wait_ge(n_x_stored[b], 8 * G)

        @block.gpsimd
        def _(gp):
            gp.memset(ident[:], 0.0).then_inc(zeroed, 1)
            gp.wait_ge(zeroed, 1)
            gp.affine_select(out=ident[:], in_=ident[:], compare_op=ALU.not_equal, fill=1.0, base=0,
                             pattern=[[-1, P]], channel_multiplier=1).then_inc(ident_ready, 1)
            gp.wait_ge(amax_local, 1)
            gp.partition_all_reduce(a2[:], a1[:], P, ABSMAX).then_inc(amax_all, 1)

        @block.scalar
        def _(act):
            for n, (kind, m, k, h) in enumerate(w_jobs):
                act.wait_ge(w_transposed, n + 1)
                if kind == "ug":
                    o = h * HI * P
                    nc.scalar.activation(targets[m][0][:, k, o:o + HI * P], ring[n % RING][:, 0:HI * P], ACT.Copy).then_inc(w_high, 1)
                else:
                    nc.scalar.activation(wd[:, 2 * m:2 * m + 2, :], ring[n % RING][:].rearrange("p (c n) -> p c n", n=D),
                                         ACT.Copy).then_inc(w_high, 1)

            def high(t, b):
                for k in range(KC):
                    act.wait_ge(x_int, KC * t + k + 1)
                    wait(act, product_done, IC * (t - 1))
                    nc.scalar.activation(xT[b][0][:, k, :], n_x[:, b, k, :], ACT.Copy).then_inc(x_high, 1)

            def step(t, b, last):
                if not last:
                    high(t + 1, 1 - b)
                for n in range(IC):
                    act.wait_ge(product_done, IC * t + n + 1)
                    if n == 0:
                        wait(act, reduced, 2 * (t - 1))
                        wait(act, stored[b], 8 * (t - b))
                    nc.scalar.activation(stage[:, b, n, :], ring[n][:], ACT.Copy).then_inc(staged, 1)

            high(0, 0)
            two_buffers(act, G, step)

        @block.vector
        def _(dve):
            v = nc.vector
            v.tensor_reduce(a1[:], amax_x[:], X, ALU.max).then_inc(amax_local, 1)
            dve.wait_ge(w_loaded, 48)
            blocks = w_raw[:].rearrange("p (a b) -> p a b", b=WBLOCK)
            v.tensor_reduce(w_max[:], blocks, X, ALU.max, apply_absolute_value=True).then_inc(dequantised, 1)
            dve.wait_ge(dequantised, 1)
            v.tensor_scalar(w_scale[:], w_max[:], 1.0 / WQMAX, TINY, ALU.mult, ALU.max).then_inc(dequantised, 1)
            dve.wait_ge(dequantised, 2)
            v.reciprocal(w_inv[:], w_scale[:]).then_inc(dequantised, 1)
            dve.wait_ge(dequantised, 3)

            def wide(a):
                return a[:].rearrange("p (a o) -> p a o", o=1).broadcast_to([P, NBLK, WBLOCK])

            ints = w_int[:].rearrange("p (a b) -> p a b", b=WBLOCK)
            v.tensor_tensor(ints, blocks, wide(w_inv), ALU.mult).then_inc(dequantised, 1)
            dve.wait_ge(dequantised, 4)
            v.tensor_tensor(blocks, ints, wide(w_scale), ALU.mult).then_inc(dequantised, 1)
            dve.wait_ge(amax_all, 1)
            v.tensor_scalar(s_x[:], a2[:], 1.0 / QMAX, TINY, ALU.mult, ALU.max).then_inc(scale_step, 1)
            dve.wait_ge(scale_step, 1)
            v.reciprocal(inv_x[:], s_x[:]).then_inc(scale_step, 1)
            dve.wait_ge(scale_step, 2)
            for n, (kind, m, k, h) in enumerate(w_jobs[:nug]):
                dve.wait_ge(w_high, n + 1)
                o = h * HI * P
                v.tensor_tensor(targets[m][1][:, k, o:o + HI * P], ring[n % RING][:, 0:HI * P],
                                targets[m][0][:, k, o:o + HI * P].bitcast(F32), ALU.subtract).then_inc(w_copied, 1)

            def quantise_x(t, b):
                for k in range(KC):
                    dve.wait_ge(x_transposed, KC * t + k + 1)
                    wait(dve, n_x_stored[b], 8 * (t - b))
                    wait(dve, x_high, KC * (t - 2) + k + 1)
                    v.tensor_scalar(n_x[:, b, k, :], tr[k][:], inv_x[:, 0:1], None, ALU.mult).then_inc(x_int, 1)
                for k in range(KC):
                    dve.wait_ge(x_high, KC * t + k + 1)
                    v.tensor_tensor(xT[b][1][:, k, :], n_x[:, b, k, :], xT[b][0][:, k, :].bitcast(F32), ALU.subtract).then_inc(x_ready, 1)

            def step(t, b, last):
                if not last:
                    quantise_x(t + 1, 1 - b)
                dve.wait_ge(staged, IC * (t + 1))
                for e, op in enumerate((ALU.max, ALU.min)):
                    v.tensor_reduce(ext_gate[:, e, bass.ds(t, 1)], stage[:, b].rearrange("p j n -> p (j n)"), X, op).then_inc(reduced, 1)

            quantise_x(0, 0)
            two_buffers(dve, G, step)

        @block.tensor
        def _(pe):
            pe.wait_ge(ident_ready, 1)
            pe.wait_ge(dequantised, 5)
            for n, (kind, m, k, h) in enumerate(w_jobs):
                if n >= RING:
                    pe.wait_ge(w_copied, min(n - RING + 1, nug))
                for e in range(HI if kind == "ug" else 4):
                    if kind == "ug":
                        at = m * W1 + (h * HI + e) * D + k * P
                    else:
                        at = 2 * W1 + (e % 2) * I + (2 * m + e // 2) * P
                    last = nc.tensor.transpose(ring[n % RING][:, e * P:(e + 1) * P], w_raw[:, at:at + P], ident[:])
                last.then_inc(w_transposed, 1)

            def transpose_x(t, b):
                pe.wait_ge(x_loaded[b], 8 * (t - b) + 16)
                for k in range(KC):
                    wait(pe, x_int, KC * (t - 1) + k + 1)
                    for e in range(NB):
                        last = nc.tensor.transpose(tr[k][:, e * P:(e + 1) * P], xin[:, b, e, k * P:(k + 1) * P], ident[:])
                    last.then_inc(x_transposed, 1)

            def step(t, b, last):
                if not last:
                    transpose_x(t + 1, 1 - b)
                pe.wait_ge(x_ready, KC * (t + 1))
                for n in range(IC):
                    wait(pe, staged, IC * (t - 1) + n + 1)
                    product(nc, ring[n][:], lambda s, k: wgate[s][:, k, n * P:(n + 1) * P],
                            lambda m, k: xT[b][m][:, k, :], KC).then_inc(product_done, 1)

            transpose_x(0, 0)
            pe.wait_ge(w_copied, nug)
            pe.wait_ge(w_high, len(w_jobs))
            two_buffers(pe, G, step)


NEGATIVE_SILU = 0.279


def gate_scales(nc, gate_d, ext_gate, s_x, s_g, k_g, k_p, s_p, G, N):
    with ExitStack() as st:
        def sb(name, shape, dt=F32):
            return st.enter_context(nc.sbuf_tensor(name, shape, dt))

        def sem(name):
            return st.enter_context(nc.semaphore(name))

        a1 = sb("a1g", [P, 2])
        a2 = sb("a2g", [P, 2])
        a3 = sb("a3g", [P, 1])
        a4 = sb("a4g", [P, 1])
        inv_g = sb("inv_g", [P, 1])
        unit_p = sb("unit_p", [P, 1])
        n_top = sb("n_top", [P, 1], I16)
        sig_top = sb("sig_top", [P, 1])
        n_sig_top = sb("n_sig_top", [P, 1], U16)
        p_top = sb("p_top", [P, 1])
        silu_top = sb("silu_top", [P, 1])
        slow = sb("slow", [P, 1], mybir.dt.int32)
        local = sem("local3")
        overall = sem("overall3")
        step_done = sem("step_done3")
        top_sig = sem("top_sig")
        slow_known = sem("slow_known")

        with ExitStack() as st1:
            block = st1.enter_context(nc.Block())

            @block.gpsimd
            def _(gp):
                gp.wait_ge(local, 2)
                gp.partition_all_reduce(a2[:], a1[:], P, bass.bass_isa.ReduceOp.max).then_inc(overall, 1)

            @block.scalar
            def _(act):
                act.wait_ge(step_done, 7)
                nc.scalar.activation(sig_top[:], n_top[:], ACT.Sigmoid, scale=s_g[:, 0:1]).then_inc(top_sig, 1)

            @block.vector
            def _(dve):
                v = nc.vector
                n = [0]

                def chain(ins):
                    n[0] += 1
                    ins.then_inc(step_done, 1)
                    dve.wait_ge(step_done, n[0])

                v.tensor_reduce(a1[:, 0:1], ext_gate[:, 0, :], X, ALU.max).then_inc(local, 1)
                v.tensor_reduce(a1[:, 1:2], ext_gate[:, 1, :], X, ALU.min, negate=True).then_inc(local, 1)
                dve.wait_ge(overall, 1)
                chain(v.tensor_tensor(a3[:], a2[:, 0:1], a2[:, 1:2], ALU.max))
                chain(v.tensor_scalar(a4[:], a3[:], s_x[:, 0:1], 1.0 / QMAX, ALU.mult, ALU.mult))
                chain(v.tensor_scalar(s_g[:], a4[:], TINY, None, ALU.max))
                chain(v.reciprocal(inv_g[:], s_g[:]))
                chain(v.tensor_scalar(k_g[:], inv_g[:], s_x[:, 0:1], None, ALU.mult))
                chain(v.tensor_scalar(unit_p[:], s_g[:], 1.0 / 65536.0, None, ALU.mult))
                chain(v.tensor_scalar(n_top[:], a2[:, 0:1], k_g[:, 0:1], None, ALU.mult))
                dve.wait_ge(top_sig, 1)
                chain(v.tensor_scalar(n_sig_top[:], sig_top[:], 65536.0, 65535.0, ALU.mult, ALU.min))
                chain(v.tensor_tensor(p_top[:], n_top[:], n_sig_top[:], ALU.mult))
                chain(v.tensor_scalar(silu_top[:], p_top[:], unit_p[:, 0:1], None, ALU.mult))
                v.tensor_scalar(slow[:], silu_top[:], NEGATIVE_SILU, None, ALU.is_lt).then_inc(slow_known, 1)

        with ExitStack() as st2:
            gate = st2.enter_context(nc.sbuf_tensor("gate_all", [P, N], F32))
            n_g = st2.enter_context(nc.sbuf_tensor("n_g_all", [P, N], I16))
            sig = st2.enter_context(nc.sbuf_tensor("sig_all", [P, N], F32))
            n_s = st2.enter_context(nc.sbuf_tensor("n_s_all", [P, N], U16))
            prod = st2.enter_context(nc.sbuf_tensor("prod_all", [P, N], F32))
            amax = st2.enter_context(nc.sbuf_tensor("amax_prod", [P, G], F32))
            am1 = st2.enter_context(nc.sbuf_tensor("am1", [P, 1], F32))
            loaded, rounded, sig_done, sig_int, prod_done, reduced, am_local, am_all = (
                st2.enter_context(nc.semaphore(n)) for n in
                ("gate_all_loaded", "gate_all_rounded", "sig_all_done", "sig_all_int", "prod_all_done", "prod_reduced", "am_local", "am_all"))
            block = st2.enter_context(nc.Block())

            def if_slow(eng):
                return eng.If(eng.value_load(slow[0:1, 0:1], min_val=0, max_val=1) == 1)

            @block.sync
            def _(sp):
                sp.wait_ge(slow_known, 1)
                with if_slow(sp):
                    with sp.Fori(0, G) as t:
                        sp.wait_ge(prod_done, t + 1)
                        sp.dma_start(gate[:], gate_d[:, t].rearrange("p j n -> p (j n)")).then_inc(loaded, 16)

            @block.gpsimd
            def _(gp):
                gp.wait_ge(slow_known, 1)
                with if_slow(gp):
                    gp.wait_ge(am_local, 1)
                    gp.partition_all_reduce(p_top[:], am1[:], P, ABSMAX).then_inc(am_all, 1)

            @block.scalar
            def _(act):
                act.wait_ge(slow_known, 1)
                with if_slow(act):
                    with act.Fori(0, G) as t:
                        act.wait_ge(loaded, 16 * t + 16)
                        nc.scalar.activation(n_g[:], gate[:], ACT.Copy, scale=k_g[:, 0:1]).then_inc(rounded, 1)
                        act.wait_ge(rounded, t + 1)
                        nc.scalar.activation(sig[:], n_g[:], ACT.Sigmoid, scale=s_g[:, 0:1]).then_inc(sig_done, 1)

            @block.vector
            def _(dve):
                v = nc.vector
                dve.wait_ge(slow_known, 1)
                with if_slow(dve):
                    v.memset(prod[:], 0.0).then_inc(prod_done, 1)
                    with dve.Fori(0, G) as t:
                        dve.wait_ge(sig_done, t + 1)
                        v.tensor_scalar(n_s[:], sig[:], 65536.0, 65535.0, ALU.mult, ALU.min).then_inc(sig_int, 1)
                        dve.wait_ge(sig_int, t + 1)
                        v.tensor_tensor(prod[:], n_g[:], n_s[:], ALU.mult).then_inc(prod_done, 1)
                        dve.wait_ge(prod_done, t + 2)
                        v.tensor_reduce(amax[:, bass.ds(t, 1)], prod[:], X, ALU.max, apply_absolute_value=True).then_inc(reduced, 1)
                    dve.wait_ge(reduced, G)
                    v.tensor_reduce(am1[:], amax[:], X, ALU.max).then_inc(am_local, 1)
                    dve.wait_ge(am_all, 1)
                n = [10]

                def chain(ins):
                    n[0] += 1
                    ins.then_inc(step_done, 1)
                    dve.wait_ge(step_done, n[0])

                chain(v.tensor_scalar(a3[:], p_top[:], unit_p[:, 0:1], 1.0 / QMAX, ALU.mult, ALU.mult))
                chain(v.tensor_scalar(s_p[:], a3[:], TINY, None, ALU.max))
                chain(v.reciprocal(a4[:], s_p[:]))
                chain(v.tensor_scalar(k_p[:], a4[:], unit_p[:, 0:1], None, ALU.mult))


def up_products(nc, n_x_d, gate_d, up_d, wup, n_p, amax_up, s_g, k_g, k_p, G, IC):
    T = NB * P
    KC = wup[0].shape[1]
    RING = IC
    HJ = IC // 2
    H = HJ * T
    with ExitStack() as st:
        def sb(name, shape, dt=F32):
            return st.enter_context(nc.sbuf_tensor(name, shape, dt))

        def sem(name):
            return st.enter_context(nc.semaphore(name))

        n_x = sb("n_x2", [P, 2, KC, T], I16)
        x_wide = sb("x_wide", [P, KC, T])
        xT = [[sb(f"xT2{n}{b}", [P, KC, T], F32R) for n in ("hi", "lo")] for b in range(2)]
        stage = sb("stage2", [P, 2, IC, T])
        gate = sb("gate2", [P, 2, H])
        n_g = sb("n_g2", [P, 2, H], I16)
        sig = sb("sig2", [P, 2, H])
        n_s = sb("n_s2", [P, 2, H], U16)
        ring = [st.enter_context(nc.psum_tensor(f"ring2{n}", [P, T], F32)) for n in range(RING)]
        x_loaded = [sem(f"n_x_loaded{b}") for b in range(2)]
        gate_loaded = [sem(f"gate_loaded{h}") for h in range(2)]
        x_widened = sem("x_widened")
        x_high = sem("x_high2")
        x_ready = sem("x_ready2")
        product_done = sem("product_done2")
        staged = sem("staged2")
        reduced = sem("reduced2")
        stored = [sem(f"up_stored{b}") for b in range(2)]
        rounded = [sem(f"gate_rounded{h}") for h in range(2)]
        sig_done = [sem(f"sig_done{h}") for h in range(2)]
        sig_int = [sem(f"sig_int{h}") for h in range(2)]
        silu_int = [sem(f"silu_int{h}") for h in range(2)]
        block = st.enter_context(nc.Block())

        @block.sync
        def _(sp):
            def load_x(t, b):
                sp.dma_start(n_x[:, b], n_x_d[:, t]).then_inc(x_loaded[b], 16)

            def load_gate(t, h):
                sp.dma_start(gate[:, h], gate_d[:, t, h * HJ:(h + 1) * HJ].rearrange("p j n -> p (j n)")).then_inc(gate_loaded[h], 16)

            def step(t, b, more_x, more_gate):
                if more_x:
                    sp.wait_ge(x_ready, KC * (t + 1))
                    load_x(t + 2, b)
                if more_gate:
                    for h in range(2):
                        sp.wait_ge(rounded[h], t + 1)
                        load_gate(t + 1, h)
                sp.wait_ge(staged, IC * (t + 1))
                sp.dma_start(up_d[:, t], stage[:, b]).then_inc(stored[b], 16)

            load_x(0, 0)
            load_gate(0, 0)
            load_gate(0, 1)
            load_x(1, 1)
            with sp.Fori(0, G // 2 - 1) as i:
                for b in range(2):
                    step(2 * i + b, b, True, True)
            step(G - 2, 0, False, True)
            step(G - 1, 1, False, False)
            for b in range(2):
                sp.wait_ge(stored[b], 8 * G)

        @block.gpsimd
        def _(gp):
            def step(t, b, last):
                gp.wait_ge(x_widened, t + 1)
                for k in range(KC):
                    gp.wait_ge(x_high, KC * t + k + 1)
                    gp.tensor_tensor(xT[b][1][:, k, :], x_wide[:, k, :], xT[b][0][:, k, :].bitcast(F32), ALU.subtract).then_inc(x_ready, 1)

            two_buffers(gp, G, step)

        @block.scalar
        def _(act):
            def high(t, b):
                act.wait_ge(x_loaded[b], 8 * (t - b) + 16)
                wait(act, product_done, IC * (t - 1))
                for k in range(KC):
                    nc.scalar.activation(xT[b][0][:, k, :], n_x[:, b, k, :], ACT.Copy).then_inc(x_high, 1)

            def sigmoid(t, h):
                act.wait_ge(rounded[h], t + 1)
                wait(act, sig_int[h], t)
                nc.scalar.activation(sig[:, h], n_g[:, h], ACT.Sigmoid, scale=s_g[:, 0:1]).then_inc(sig_done[h], 1)

            def evacuate(t, b, n):
                act.wait_ge(product_done, IC * t + n + 1)
                if n == 0:
                    wait(act, reduced, t - 1)
                    wait(act, stored[b], 8 * (t - b))
                nc.scalar.activation(stage[:, b, n, :], ring[n][:], ACT.Copy).then_inc(staged, 1)

            def step(t, b, last):
                if not last:
                    high(t + 1, 1 - b)
                act.wait_ge(gate_loaded[0], 16 * t + 16)
                wait(act, silu_int[0], t)
                nc.scalar.activation(n_g[:, 0], gate[:, 0], ACT.Copy, scale=k_g[:, 0:1]).then_inc(rounded[0], 1)
                evacuate(t, b, 0)
                sigmoid(t, 0)
                for n in range(1, HJ):
                    evacuate(t, b, n)
                sigmoid(t, 1)
                for n in range(HJ, IC):
                    evacuate(t, b, n)

            high(0, 0)
            two_buffers(act, G, step)

        @block.vector
        def _(dve):
            v = nc.vector

            def silu(t, h):
                dve.wait_ge(sig_done[h], t + 1)
                wait(dve, silu_int[h], t)
                v.tensor_scalar(n_s[:, h], sig[:, h], 65536.0, 65535.0, ALU.mult, ALU.min).then_inc(sig_int[h], 1)
                dve.wait_ge(sig_int[h], t + 1)
                v.scalar_tensor_tensor(n_p[:, bass.ds(t, 1), h * H:(h + 1) * H].rearrange("p o n -> p (o n)"), n_g[:, h], k_p[:, 0:1],
                                       n_s[:, h], ALU.mult, ALU.mult).then_inc(silu_int[h], 1)

            def widen(t, b):
                dve.wait_ge(x_loaded[b], 8 * (t - b) + 16)
                wait(dve, x_ready, KC * t)
                v.tensor_copy(x_wide[:], n_x[:, b]).then_inc(x_widened, 1)

            def step(t, b, last):
                if not last:
                    widen(t + 1, 1 - b)
                dve.wait_ge(gate_loaded[1], 16 * t + 16)
                wait(dve, silu_int[1], t)
                v.tensor_scalar(n_g[:, 1], gate[:, 1], k_g[:, 0:1], None, ALU.mult).then_inc(rounded[1], 1)
                silu(t, 0)
                silu(t, 1)
                dve.wait_ge(staged, IC * (t + 1))
                v.tensor_reduce(amax_up[:, bass.ds(t, 1)], stage[:, b].rearrange("p j n -> p (j n)"), X, ALU.max,
                                apply_absolute_value=True).then_inc(reduced, 1)

            widen(0, 0)
            two_buffers(dve, G, step)

        @block.tensor
        def _(pe):
            def step(t, b, last):
                pe.wait_ge(x_ready, KC * (t + 1))
                for n in range(IC):
                    wait(pe, staged, IC * (t - 1) + n + 1)
                    product(nc, ring[n][:], lambda s, k: wup[s][:, k, n * P:(n + 1) * P],
                            lambda m, k: xT[b][m][:, k, :], KC).then_inc(product_done, 1)

            two_buffers(pe, G, step)


def hidden_max(nc, up_d, n_u_d, n_p, amax_up, amax_hid, s_x, s_p, s_hid, G, N):
    with ExitStack() as st:
        def sb(name, shape, dt=F32):
            return st.enter_context(nc.sbuf_tensor(name, shape, dt))

        def sem(name):
            return st.enter_context(nc.semaphore(name))

        up = sb("up4", [P, 2, N])
        n_u = sb("n_u4", [P, 2, N], I16)
        hid = sb("hid4", [P, N])
        a1 = sb("a1h", [P, 1])
        a2 = sb("a2h", [P, 1])
        a3 = sb("a3h", [P, 1])
        s_u = sb("s_u", [P, 1])
        r_u = sb("r_u", [P, 1])
        k_u = sb("k_u", [P, 1])
        loaded = [sem(f"up_loaded{b}") for b in range(2)]
        amax_local = sem("amax_local4")
        amax_all = sem("amax_all4")
        scale_step = sem("scale_step4")
        up_int = sem("up_int")
        hid_done = sem("hid_done")
        hid_reduced = sem("hid_reduced")
        stored = [sem(f"n_u_stored{b}") for b in range(2)]
        block = st.enter_context(nc.Block())

        @block.sync
        def _(sp):
            def load(t, b):
                sp.dma_start(up[:, b], up_d[:, t].rearrange("p j n -> p (j n)")).then_inc(loaded[b], 16)

            def step(t, b, more):
                sp.wait_ge(up_int, t + 1)
                if more:
                    load(t + 2, b)
                sp.dma_start(n_u_d[:, t], n_u[:, b]).then_inc(stored[b], 16)

            load(0, 0)
            load(1, 1)
            with sp.Fori(0, G // 2 - 1) as i:
                for b in range(2):
                    step(2 * i + b, b, True)
            for b in range(2):
                step(G - 2 + b, b, False)
            for b in range(2):
                sp.wait_ge(stored[b], 8 * G)

        @block.gpsimd
        def _(gp):
            gp.wait_ge(amax_local, 1)
            gp.partition_all_reduce(a2[:], a1[:], P, ABSMAX).then_inc(amax_all, 1)

        @block.scalar
        def _(act):
            act.wait_ge(scale_step, 4)

            def step(t, b, last):
                act.wait_ge(loaded[b], 8 * (t - b) + 16)
                wait(act, stored[b], 8 * (t - b))
                wait(act, hid_done, t - 1)
                nc.scalar.activation(n_u[:, b], up[:, b], ACT.Copy, scale=k_u[:, 0:1]).then_inc(up_int, 1)

            two_buffers(act, G, step)

        @block.vector
        def _(dve):
            v = nc.vector
            v.tensor_reduce(a1[:], amax_up[:], X, ALU.max).then_inc(amax_local, 1)
            dve.wait_ge(amax_all, 1)
            v.tensor_scalar(a3[:], a2[:], s_x[:, 0:1], 1.0 / QMAX, ALU.mult, ALU.mult).then_inc(scale_step, 1)
            dve.wait_ge(scale_step, 1)
            v.tensor_scalar(s_u[:], a3[:], TINY, None, ALU.max).then_inc(scale_step, 1)
            dve.wait_ge(scale_step, 2)
            v.reciprocal(r_u[:], s_u[:]).then_inc(scale_step, 1)
            dve.wait_ge(scale_step, 3)
            v.tensor_scalar(k_u[:], r_u[:], s_x[:, 0:1], None, ALU.mult).then_inc(scale_step, 1)
            v.tensor_tensor(s_hid[:], s_p[:], s_u[:], ALU.mult).then_inc(scale_step, 1)

            def step(t, b, last):
                wait(dve, hid_reduced, t)
                dve.wait_ge(up_int, t + 1)
                v.tensor_tensor(hid[:], n_p[:, bass.ds(t, 1)].rearrange("p o n -> p (o n)"), n_u[:, b], ALU.mult).then_inc(hid_done, 1)
                dve.wait_ge(hid_done, t + 1)
                v.tensor_reduce(amax_hid[:, bass.ds(t, 1)], hid[:], X, ALU.max, apply_absolute_value=True).then_inc(hid_reduced, 1)

            two_buffers(dve, G, step)


def down_products(nc, n_u_d, x1_d, g_ffn, n_p, wd, out, amax_hid, s_hid, G, IC):
    D = wd.shape[2]
    T = NB * P
    N = IC * T
    with ExitStack() as st:
        def sb(name, shape, dt=F32):
            return st.enter_context(nc.sbuf_tensor(name, shape, dt))

        def sem(name):
            return st.enter_context(nc.semaphore(name))

        n_u = sb("n_u5", [P, 2, N], I16)
        n_h = sb("n_h", [P, 2, N], I16)
        f_h = sb("f_h", [P, 2, IC, T])
        x1 = sb("x1_5", [P, 2, NB, D])
        res = sb("res", [P, 2, NB, D])
        tg = sb("tg5", [P, 1])
        a1 = sb("a1o", [P, 1])
        a2 = sb("a2o", [P, 1])
        a3 = sb("a3o", [P, 1])
        s_o = sb("s_o", [P, 1])
        r_o = sb("r_o", [P, 1])
        k_o = sb("k_o", [P, 1])
        y_scale = sb("y_scale", [P, 1])
        y = [st.enter_context(nc.psum_tensor(f"y5{b}", [P, NB, D], F32)) for b in range(2)]
        tg_loaded = sem("tg_loaded5")
        tg_ready = sem("tg_ready5")
        n_u_loaded = [sem(f"n_u_loaded{b}") for b in range(2)]
        x1_loaded = [sem(f"x1_loaded{b}") for b in range(2)]
        amax_local = sem("amax_local5")
        amax_all = sem("amax_all5")
        scale_step = sem("scale_step5")
        rounded = sem("rounded5")
        widened = sem("widened")
        y_done = sem("y_done5")
        res_done = sem("res_done")
        stored = [sem(f"out_stored{b}") for b in range(2)]
        block = st.enter_context(nc.Block())

        @block.sync
        def _(sp):
            sp.dma_start(tg[:], g_ffn.rearrange("(o n) -> o n", o=1).broadcast_to([P, 1])).then_inc(tg_loaded, 16)

            def load(t, b):
                sp.dma_start(n_u[:, b], n_u_d[:, t]).then_inc(n_u_loaded[b], 16)

            def load_x1(t, b):
                sp.dma_start(x1[:, b], x1_d[:, t]).then_inc(x1_loaded[b], 16)

            def step(t, b, more):
                if more:
                    sp.wait_ge(rounded, t + 1)
                    load(t + 2, b)
                sp.wait_ge(res_done, t + 1)
                sp.dma_start(out[bass.ds(t * NB, NB)].rearrange("b p d -> p b d"), res[:, b]).then_inc(stored[b], 16)
                if more:
                    load_x1(t + 2, b)

            for b in range(2):
                load(b, b)
                load_x1(b, b)
            with sp.Fori(0, G // 2 - 1) as i:
                for b in range(2):
                    step(2 * i + b, b, True)
            for b in range(2):
                step(G - 2 + b, b, False)
            for b in range(2):
                sp.wait_ge(stored[b], 8 * G)

        @block.gpsimd
        def _(gp):
            gp.wait_ge(amax_local, 1)
            gp.partition_all_reduce(a2[:], a1[:], P, ABSMAX).then_inc(amax_all, 1)

        @block.scalar
        def _(act):
            act.wait_ge(tg_loaded, 16)
            nc.scalar.activation(tg[:], tg[:], ACT.Tanh).then_inc(tg_ready, 1)

            def step(t, b=None):
                b = t % 2 if isinstance(t, int) else b
                act.wait_ge(rounded, t + 1)
                wait(act, y_done, t - 1)
                nc.scalar.activation(f_h[:, b].rearrange("p j n -> p (j n)"), n_h[:, b], ACT.Copy).then_inc(widened, 1)

            step(0)
            step(1)
            with act.Fori(1, G // 2) as i:
                step(2 * i, 0)
                step(2 * i + 1, 1)

        @block.vector
        def _(dve):
            v = nc.vector
            v.tensor_reduce(a1[:], amax_hid[:], X, ALU.max).then_inc(amax_local, 1)
            dve.wait_ge(amax_all, 1)
            v.tensor_scalar(a3[:], a2[:], s_hid[:, 0:1], 1.0 / QMAX, ALU.mult, ALU.mult).then_inc(scale_step, 1)
            dve.wait_ge(scale_step, 1)
            v.tensor_scalar(s_o[:], a3[:], TINY, None, ALU.max).then_inc(scale_step, 1)
            dve.wait_ge(scale_step, 2)
            v.reciprocal(r_o[:], s_o[:]).then_inc(scale_step, 1)
            dve.wait_ge(scale_step, 3)
            v.tensor_scalar(k_o[:], r_o[:], s_hid[:, 0:1], None, ALU.mult).then_inc(scale_step, 1)
            dve.wait_ge(tg_ready, 1)
            v.tensor_tensor(y_scale[:], s_o[:], tg[:], ALU.mult).then_inc(scale_step, 1)
            dve.wait_ge(scale_step, 5)

            def quantise(t, b):
                dve.wait_ge(n_u_loaded[b], 8 * (t - b) + 16)
                wait(dve, widened, t - 1)
                v.scalar_tensor_tensor(n_h[:, b], n_p[:, bass.ds(t, 1)].rearrange("p o n -> p (o n)"), k_o[:, 0:1], n_u[:, b],
                                       ALU.mult, ALU.mult).then_inc(rounded, 1)

            def step(t, b=None, last=False):
                b = t % 2 if isinstance(t, int) else b
                if not last:
                    quantise(t + 1, 1 - b)
                dve.wait_ge(y_done, t + 1)
                dve.wait_ge(x1_loaded[b], 8 * (t - b) + 16)
                wait(dve, stored[b], 8 * (t - b))
                for h in range(2):
                    rows = slice(h * NB // 2, (h + 1) * NB // 2)
                    last_op = v.scalar_tensor_tensor(res[:, b, rows], y[b][:, rows], y_scale[:, 0:1], x1[:, b, rows], ALU.mult, ALU.add)
                last_op.then_inc(res_done, 1)

            quantise(0, 0)
            step(0)
            step(1)
            with dve.Fori(1, G // 2 - 1) as i:
                step(2 * i, 0)
                step(2 * i + 1, 1)
            step(G - 2)
            step(G - 1, last=True)

        @block.tensor
        def _(pe):
            def step(t, b=None):
                b = t % 2 if isinstance(t, int) else b
                pe.wait_ge(widened, t + 1)
                wait(pe, res_done, t - 1)
                for e in range(NB):
                    for j in range(IC):
                        mm = nc.tensor.matmul(y[b][:, e, :], f_h[:, b, j, e * P:(e + 1) * P], wd[:, j, :],
                                              start=(j == 0), stop=(j == IC - 1))
                mm.then_inc(y_done, 1)

            step(0)
            step(1)
            with pe.Fori(1, G // 2) as i:
                step(2 * i, 0)
                step(2 * i + 1, 1)


def program(nc, x, ctx, mask, g_xattn, g_ffn, wq, wk, wv, wo, bo, w_gate, w_up, w_down, out):
    B, S, D = x.shape
    I = w_up.shape[0]
    G, IC, T = B // NB, I // P, NB * P
    assert G % 2 == 0 and G >= 6

    def dram(name, shape, dt=F32):
        return nc.dram_tensor(name, shape, dt, kind="Internal").ap()

    x1_d = dram("x1_d", (P, G, NB, D))
    xn2_d = dram("xn2_d", (P, G, NB, D))
    n_x_d = dram("n_x_d", (P, G, D // P, T), I16)
    up_d, gate_d = (dram(n, (P, G, IC, T)) for n in ("up_d", "gate_d"))
    n_u_d = dram("n_u_d", (P, G, IC * T), I16)

    with ExitStack() as st:
        def sb(name, shape, dt=F32):
            return st.enter_context(nc.sbuf_tensor(name, shape, dt))

        amax_x, amax_up, amax_hid = (sb(f"amax_{n}", [P, G]) for n in ("x", "up", "hid"))
        ext_gate = sb("ext_gate", [P, 2, G])
        s_x, s_g, k_g, s_p, k_p, s_hid = (sb(n, [P, 1]) for n in ("s_x", "s_g", "k_g", "s_p", "k_p", "s_hid"))
        attention(nc, x, ctx, mask, g_xattn, wq, wk, wv, wo, bo, x1_d, xn2_d, amax_x)
        wd = sb("wd", [P, IC, D])
        wup = [sb(f"wup_{n}", [P, D // P, I], F32R) for n in ("hi", "lo")]
        gate_products(nc, w_up, w_gate, w_down, xn2_d, n_x_d, gate_d, wup, wd, amax_x, ext_gate, s_x, G)
        gate_scales(nc, gate_d, ext_gate, s_x, s_g, k_g, k_p, s_p, G, IC * T)
        n_p = sb("n_p", [P, G, IC * T], I16)
        up_products(nc, n_x_d, gate_d, up_d, wup, n_p, amax_up, s_g, k_g, k_p, G, IC)
        hidden_max(nc, up_d, n_u_d, n_p, amax_up, amax_hid, s_x, s_p, s_hid, G, IC * T)
        down_products(nc, n_u_d, x1_d, g_ffn, n_p, wd, out, amax_hid, s_hid, G, IC)


INPUTS = ["x", "ctx_1024", "mask_BxS2_bf0", "g_xattn", "g_ffn", "L0_xattn_Wq", "L0_xattn_Wk", "L0_xattn_Wv", "L0_xattn_Wo",
          "L0_xattn_bo", "L0_ffn_w_gate", "L0_ffn_w_up", "L0_ffn_w_down"]


def kernel(**inputs):
    import numpy as np
    import concourse.bacc as bacc
    from concourse.bass_utils import run_bass_kernel_spmd

    nc = bacc.Bacc("TRN2", target_bir_lowering=False, num_devices=1)
    arrays, args = {}, []
    for name in INPUTS:
        a = np.ascontiguousarray(inputs[name])
        arrays[f"in_{name}"] = a
        args.append(nc.dram_tensor(f"in_{name}", a.shape, mybir.dt.from_np(a.dtype), kind="ExternalInput").ap())
    out = nc.dram_tensor("out_x", inputs["x"].shape, F32, kind="ExternalOutput").ap()
    program(nc, *args, out)
    r = run_bass_kernel_spmd(nc, [arrays], core_ids=[0])
    return np.asarray(r.results[0]["out_x"])
```

```python
from contextlib import ExitStack

import concourse.bass as bass
from concourse import mybir

ALU = mybir.AluOpType
ACT = mybir.ActivationFunctionType
F32 = mybir.dt.float32
F32R = mybir.dt.float32r
I16 = mybir.dt.int16
U16 = mybir.dt.uint16
U8 = mybir.dt.uint8
X = mybir.AxisListType.X
ABSMAX = bass.bass_isa.ReduceOp.absmax

P = 128
NB = 4
HD = 64
SCALE = HD ** -0.5
FMAX = 3.4028234663852886e38
EPS = 1e-5
QMAX = 32767.0
TINY = 1e-12
WBLOCK = 32
WQMAX = 7.0


def split(hi, lo):
    return [(hi, hi), (lo, hi), (hi, lo)]


def wait(eng, s, n):
    if not isinstance(n, int) or n > 0:
        eng.wait_ge(s, n)


def attention(nc, x, ctx, mask, g_xattn, wq, wk, wv, wo, bo, w_ffn, ident, x1_d, xn2_d, w_raw, amax_x):
    B, S, D = x.shape
    INNER = wq.shape[1]
    assert S == P and D == 2 * P and INNER % P == 0 and B % NB == 0
    KC = D // P
    NC = INNER // P
    G = B // NB
    U = G * NC
    T = NB * P
    VH = 512
    assert NC == 8 and INNER == 2 * VH

    YC = 3
    jobs = []
    for c in range(NC):
        jobs += [(c, "q", 0)]
        if c == NC - 1:
            jobs += [(c, "t", n) for n in range(KC)]
        jobs += [(c, "k", 0)]
        if c < 2:
            jobs += [(c, "v", 2 * c), (c, "v", 2 * c + 1)]
        elif c < 6:
            jobs += [(c, "v", NB + c - 2)]
        if c == YC:
            jobs += [(c, "y", 0), (c, "y", 1)]
    jobs += [(NC - 1, "t", n) for n in range(KC, 2 * KC)]
    NJ = len(jobs)
    FIRST = 2 * KC
    y_at = jobs.index((YC, "y", 0))
    last_k = jobs.index((NC - 1, "k", 0))
    assert NJ % 2 == 0 and FIRST % 2 == 0 and y_at % 2 == 0

    def first_job(n):
        return NJ - FIRST + n

    def jobs_of(c, kind):
        return [(i, n) for i, (cc, k, n) in enumerate(jobs) if cc == c and k == kind]

    def nth(g, i):
        if isinstance(g, int) and g == G:
            return i % 2, NJ // 2 * G - 1
        skipped = 0 if isinstance(g, int) and (g < 0 or (g == 0 and i < y_at)) else 1
        if isinstance(g, int) and g == G - 1 and i == last_k:
            skipped += KC // 2
        return i % 2, (FIRST + i) // 2 + (NJ // 2) * g - skipped

    with ExitStack() as st:
        def sb(name, shape, dt=F32):
            return st.enter_context(nc.sbuf_tensor(name, shape, dt))

        def sem(name):
            return st.enter_context(nc.semaphore(name))

        w_hi = [sb(f"w{n}_hi", [P, KC * INNER], F32R) for n in "qkvo"]
        w_lo = [sb(f"w{n}_lo", [P, KC * INNER], F32R) for n in "qkvo"]
        x_in = sb("x_in", [P, NB, D])
        ctx_in = sb("ctx_in", [P, NB, D])
        xn = sb("xn", [P, NB, D])
        xres = sb("xres", [P, NB, D])
        t_hi = [sb(f"t{n}_hi", [P, KC, T], F32R) for n in "xc"]
        t_lo = [sb(f"t{n}_lo", [P, KC, T], F32R) for n in "xc"]
        qT = sb("qT", [P, T])
        kT = sb("kT", [P, T])
        v_sb = sb("v_sb", [P, NB, INNER])
        masked = sb("masked", [P, 2, NB, P])
        prob = sb("prob", [P, 2, 2, NB, P])
        probT = sb("probT", [P, 2, NB, P])
        neg_max = sb("neg_max", [P, 2, NB])
        psums = sb("psums", [P, 2, NB])
        rsums = sb("rsums", [P, 2, NB])
        o_hi = sb("o_hi", [P, T], F32R)
        o_lo = sb("o_lo", [P, T], F32R)
        yT_sb = sb("yT_sb", [P, KC, T])
        mask_u8 = sb("mask_u8", [P, NB, P], U8)
        mask_add = sb("mask_add", [P, NB, P])
        causal = sb("causal", [P, P])
        x1 = sb("x1", [P, NB, D])
        xn2 = sb("xn2", [P, NB, D])
        bo_g = sb("bo_g", [P, D])
        tg = sb("tg", [P, 1])
        stats = sb("stats", [P, NB, 6])
        mean = sb("mean", [P, NB])
        stats2 = sb("stats2", [P, NB, 6])
        mean2 = sb("mean2", [P, NB])
        vare = sb("vare", [P, NB])
        vare2 = sb("vare2", [P, NB])
        m_sum, m_dif, v_sum, m_sq, v_eps = (sb(n, [P, NB]) for n in ("m_sum", "m_dif", "v_sum", "m_sq", "v_eps"))
        rstd = sb("rstd", [P, NB])
        rstd2 = sb("rstd2", [P, NB])
        mhalf = sb("mhalf", [P, NB])

        proj = [st.enter_context(nc.psum_tensor(f"proj{b}", [P, T], F32)) for b in range(2)]
        score = [st.enter_context(nc.psum_tensor(f"score{h}", [P, NB, P], F32)) for h in range(2)]
        trans = st.enter_context(nc.psum_tensor("trans", [P, NB, P], F32))
        pv = st.enter_context(nc.psum_tensor("pv", [P, NB, P], F32))
        yT = [st.enter_context(nc.psum_tensor(f"yT{n}", [P, T], F32)) for n in range(KC)]

        w_loaded = [sem(f"w{n}_loaded") for n in "qkvo"]
        w_high = sem("w_high")
        w_ready = sem("w_ready")
        small_loaded = sem("small_loaded")
        x_loaded = sem("x_loaded")
        ctx_loaded = sem("ctx_loaded")
        mask_loaded = sem("mask_loaded")
        ident_zero = sem("ident_zero")
        consts = sem("consts")
        gate_ready = sem("gate_ready")
        bo_ready = sem("bo_ready")
        stats_done = sem("stats_done")
        var_ready = sem("var_ready")
        rstd_ready = sem("rstd_ready")
        xn_ready = sem("xn_ready")
        xres_ready = sem("xres_ready")
        mask_ready = sem("mask_ready")
        projected = [sem(f"projected{b}") for b in range(2)]
        copied = [sem(f"copied{b}") for b in range(2)]
        high_done = sem("high_done")
        scored = sem("scored")
        masked_done = sem("masked_done")
        max_done = sem("max_done")
        exp_done = sem("exp_done")
        recip_done = sem("recip_done")
        normed = sem("normed")
        transposed = sem("transposed")
        probT_copied = [sem(f"probT_copied{h}") for h in range(2)]
        pv_done = sem("pv_done")
        out_high = sem("out_high")
        out_split = sem("out_split")
        yT_copied = sem("yT_copied")
        wo_done = sem("wo_done")
        stats2_done = sem("stats2_done")
        var2_ready = sem("var2_ready")
        rstd2_ready = sem("rstd2_ready")
        xn2_ready = sem("xn2_ready")
        x1_stored = sem("x1_stored")
        xn2_stored = sem("xn2_stored")
        W1 = w_raw.shape[1] // 3
        NBLK = W1 // WBLOCK
        w_int = sb("w_int", [P, W1], I16)
        w_max = sb("w_max", [P, NBLK])
        w_scale = sb("w_scale", [P, NBLK])
        w_inv = sb("w_inv", [P, NBLK])
        ffn_loaded = sem("ffn_loaded")
        dequantised = sem("dequantised")

        def wait_x1(eng, g):
            if isinstance(g, int) and g == 0:
                return
            for i, n in jobs_of(YC, "y"):
                b, before = nth(g, i)
                eng.wait_ge(copied[b], before + 1)

        def drive(eng, step):
            for c in range(NC):
                step(0, c)
            with eng.Fori(1, G - 1) as i:
                for c in range(NC):
                    step(i, c)
            for c in range(NC):
                step(G - 1, c)
            for c in range(3):
                step(G, c)

        def parts(g, c):
            u = g * NC + c
            if not isinstance(g, int):
                return u, True, True, True, True
            return u, u < U, 0 < u <= U, 2 <= u < U + 2, g < G - 1

        def w_stage(n):
            return w_raw[:, (n % 2) * KC * INNER:(n % 2 + 1) * KC * INNER]

        block = st.enter_context(nc.Block())

        @block.sync
        def _(sp):
            def load_ctx(g):
                sp.dma_start(ctx_in[:], ctx[bass.ds(g * NB, NB)].rearrange("b p d -> p b d")).then_inc(ctx_loaded, 16)

            def load_x(g):
                sp.dma_start(x_in[:], x[bass.ds(g * NB, NB)].rearrange("b p d -> p b d")).then_inc(x_loaded, 16)

            def load_mask(g):
                rows = mask[bass.ds(g * NB, NB)].rearrange("(o b) k -> o b k", o=1)
                sp.dma_start(mask_u8[:], rows.broadcast_to([P, NB, P])).then_inc(mask_loaded, 16)

            def load_w(n):
                w = (wq, wk, wv, wo)[n]
                sp.dma_start(w_stage(n).rearrange("p (c n) -> p c n", n=w.shape[1]),
                             w.rearrange("(c p) n -> p c n", p=P)).then_inc(w_loaded[n], 16)

            load_x(0)
            load_w(0)
            load_ctx(0)
            load_w(1)
            sp.dma_start(tg[:], g_xattn.rearrange("(o n) -> o n", o=1).broadcast_to([P, 1])).then_inc(small_loaded, 16)
            sp.dma_start(bo_g[:], bo.rearrange("(o n) -> o n", o=1).broadcast_to([P, D])).then_inc(small_loaded, 16)
            load_mask(0)
            for n in (2, 3):
                sp.wait_ge(w_ready, n - 1)
                load_w(n)

            def store(g):
                wait_x1(sp, g + 1)
                sp.dma_start(x1_d[:, g], x1[:]).then_inc(x1_stored, 16)
                sp.wait_ge(xn2_ready, NB * (g + 1))
                sp.dma_start(xn2_d[:, g], xn2[:]).then_inc(xn2_stored, 16)

            def load_next(g):
                sp.wait_ge(mask_ready, g + 1)
                sp.wait_ge(projected[1], nth(g, 1)[1])
                load_ctx(g + 1)
                load_mask(g + 1)
                sp.wait_ge(xn_ready, g + 1)
                sp.wait_ge(xres_ready, g + 1)
                load_x(g + 1)

            sp.wait_ge(w_ready, 4)
            for n, w in enumerate(w_ffn):
                sp.dma_start(w_raw[:, n * W1:(n + 1) * W1].rearrange("p (c n) -> p c n", n=w.shape[1]),
                             w.rearrange("(c p) n -> p c n", p=P)).then_inc(ffn_loaded, 16)
            load_next(0)
            with sp.Fori(1, G - 1) as i:
                load_next(i)
                store(i - 1)
            store(G - 2)
            store(G - 1)
            sp.wait_ge(x1_stored, 16 * G)
            sp.wait_ge(xn2_stored, 16 * G)

        @block.gpsimd
        def _(gp):
            gp.memset(ident[:], 0.0).then_inc(ident_zero, 1)
            gp.memset(causal[:], 0.0).then_inc(ident_zero, 1)
            gp.wait_ge(ident_zero, 2)
            gp.affine_select(out=ident[:], in_=ident[:], compare_op=ALU.not_equal, fill=1.0, base=0,
                             pattern=[[-1, P]], channel_multiplier=1).then_inc(consts, 1)
            gp.affine_select(out=causal[:], in_=causal[:], compare_op=ALU.is_ge, fill=-FMAX, base=0,
                             pattern=[[-1, P]], channel_multiplier=1).then_inc(consts, 1)
            gp.memset(mhalf[:], -0.5).then_inc(consts, 1)
            gp.wait_ge(consts, 3)

            def make_rstd(g):
                gp.wait_ge(var_ready, g + 1)
                gp.tensor_tensor(rstd[:], vare[:], mhalf[:], ALU.pow).then_inc(rstd_ready, 1)

            def make_rstd2(g):
                gp.wait_ge(var2_ready, g + 1)
                gp.tensor_tensor(rstd2[:], vare2[:], mhalf[:], ALU.pow).then_inc(rstd2_ready, 1)

            def step(g, c):
                u, new, soft, old, more = parts(g, c)
                if soft:
                    for h in range(2):
                        gp.wait_ge(recip_done, 2 * (u - 1) + h + 1)
                        pr = prob[:, (c + 1) % 2, h]
                        gp.tensor_tensor(pr, pr, rsums[:, h, :].rearrange("p (b o) -> p b o", o=1).broadcast_to([P, NB, P]),
                                         ALU.mult).then_inc(normed, 1)
                if c == YC and new:
                    gp.wait_ge(x_loaded, 16 * (g + 1))
                    wait_x1(gp, g)
                    gp.tensor_tensor(xres[:], x_in[:], bo_g[:].rearrange("p (o n) -> p o n", o=1).broadcast_to([P, NB, D]),
                                     ALU.add).then_inc(xres_ready, 1)
                if c == YC + 1 and new and not (isinstance(g, int) and g == 0):
                    make_rstd2(g - 1)
                if c == 5 and new and more:
                    make_rstd(g + 1)

            make_rstd(0)
            gp.wait_ge(gate_ready, 1)
            gp.tensor_scalar(bo_g[:], bo_g[:], tg[:, 0:1], None, ALU.mult).then_inc(bo_ready, 1)
            gp.wait_ge(bo_ready, 1)
            drive(gp, step)
            make_rstd2(G - 1)

        @block.scalar
        def _(act):
            def w_high_part(n):
                act.wait_ge(w_loaded[n], 16)
                nc.scalar.activation(w_hi[n][:], w_stage(n), ACT.Copy).then_inc(w_high, 1)

            def high(g, i, n):
                b, before = nth(g, i)
                act.wait_ge(projected[b], before + 1)
                nc.scalar.activation(t_hi[n // KC][:, n % KC, :], proj[b][:], ACT.Copy).then_inc(high_done, 1)

            def exps(u, c, h):
                wait(act, transposed, 2 * (u - 2) + h + 1)
                act.wait_ge(max_done, 2 * u + h + 1)
                wait(act, normed, 2 * (u - 1) + h + 1)
                for b in range(NB):
                    nc.scalar.activation(prob[:, c % 2, h, b, :], masked[:, h, b, :], ACT.Exp,
                                         bias=neg_max[:, h, b:b + 1],
                                         accum_out=psums[:, h, b:b + 1]).then_inc(exp_done, 1)

            def step(g, c):
                u, new, soft, old, more = parts(g, c)
                if new:
                    (i, _), = jobs_of(c, "q")
                    b, before = nth(g, i)
                    act.wait_ge(projected[b], before + 1)
                    wait(act, scored, 2 * u)
                    nc.scalar.activation(qT[:], proj[b][:], ACT.Copy, scale=SCALE).then_inc(copied[b], 1)
                nxt = c == NC - 1 and new and more
                ts = jobs_of(c, "t")
                if nxt:
                    for i, n in ts[:KC]:
                        high(g, i, n)
                if old:
                    act.wait_ge(transposed, 2 * (u - 2) + 1)
                    wait(act, pv_done, u - 2)
                    nc.scalar.activation(probT[:, 0], trans[:], ACT.Copy).then_inc(probT_copied[0], 1)
                if c == 2 and not (isinstance(g, int) and g == 0):
                    copy_y(g - 1)
                if soft:
                    exps(u - 1, c + 1, 0)
                if new:
                    (i, _), = jobs_of(c, "k")
                    b, before = nth(g, i)
                    act.wait_ge(projected[b], before + 1)
                    wait(act, scored, 2 * u)
                    nc.scalar.activation(kT[:], proj[b][:], ACT.Copy).then_inc(copied[b], 1)
                if nxt:
                    high(g, *ts[KC])
                if soft:
                    exps(u - 1, c + 1, 1)
                if nxt:
                    high(g, *ts[KC + 1])
                if old:
                    act.wait_ge(pv_done, u - 1)
                    wait(act, wo_done, u - 2)
                    nc.scalar.activation(o_hi[:], pv[:], ACT.Copy).then_inc(out_high, 1)

            def copy_y(g):
                act.wait_ge(wo_done, NC * (g + 1))
                wait_x1(act, g)
                for k in range(KC):
                    nc.scalar.activation(yT_sb[:, k, :], yT[k][:], ACT.Copy).then_inc(yT_copied, 1)

            w_high_part(0)
            w_high_part(1)
            for n in range(2 * KC):
                high(-1, first_job(n), n)
            w_high_part(2)
            act.wait_ge(small_loaded, 32)
            nc.scalar.activation(tg[:], tg[:], ACT.Tanh).then_inc(gate_ready, 1)
            w_high_part(3)
            drive(act, step)

        @block.vector
        def _(dve):
            def w_low_part(n):
                dve.wait_ge(w_high, n + 1)
                nc.vector.tensor_tensor(w_lo[n][:], w_stage(n), w_hi[n][:].bitcast(F32), ALU.subtract).then_inc(w_ready, 1)

            MOMENTS = NB + 6

            def moments(stats, mean, var_eps, done, n, ready):
                v = nc.vector
                dve.wait_ge(done, n)
                v.tensor_tensor(m_sum[:], stats[:, :, 1], stats[:, :, 4], ALU.add).then_inc(done, 1)
                v.tensor_tensor(m_dif[:], stats[:, :, 1], stats[:, :, 4], ALU.subtract).then_inc(done, 1)
                v.tensor_tensor(v_sum[:], stats[:, :, 2], stats[:, :, 5], ALU.add).then_inc(done, 1)
                dve.wait_ge(done, n + 3)
                v.tensor_scalar(mean[:], m_sum[:], 0.5, None, ALU.mult).then_inc(done, 1)
                v.tensor_tensor(m_sq[:], m_dif[:], m_dif[:], ALU.mult).then_inc(done, 1)
                v.tensor_scalar(v_eps[:], v_sum[:], 1.0 / D, EPS, ALU.mult, ALU.add).then_inc(done, 1)
                dve.wait_ge(done, n + 6)
                v.scalar_tensor_tensor(var_eps[:], m_sq[:], 0.25, v_eps[:], ALU.mult, ALU.add).then_inc(ready, 1)

            def layernorm_stats(g):
                dve.wait_ge(x_loaded, 16 * (g + 1))
                for b in range(NB):
                    nc.vector.bn_stats(stats[:, b, :], x_in[:, b, :]).then_inc(stats_done, 1)

            def layernorm_moments(g):
                moments(stats, mean, vare, stats_done, MOMENTS * g + NB, var_ready)

            def normalise(g):
                dve.wait_ge(rstd_ready, g + 1)
                for b in range(NB):
                    last = nc.vector.tensor_scalar(xn[:, b, :], x_in[:, b, :], mean[:, b:b + 1], rstd[:, b:b + 1],
                                                   ALU.subtract, ALU.mult)
                last.then_inc(xn_ready, 1)

            def low(g, i, n, high_before):
                b, before = nth(g, i)
                dve.wait_ge(high_done, high_before + 1)
                nc.vector.tensor_tensor(t_lo[n // KC][:, n % KC, :], proj[b][:], t_hi[n // KC][:, n % KC, :].bitcast(F32),
                                        ALU.subtract).then_inc(copied[b], 1)

            def step(g, c):
                u, new, soft, old, more = parts(g, c)
                nxt = c == NC - 1 and new and more
                if soft:
                    for h in range(2):
                        n = 2 * (u - 1) + h + 1
                        dve.wait_ge(scored, n)
                        wait(dve, exp_done, NB * (n - 2))
                        nc.vector.tensor_tensor(masked[:, h], score[h][:], mask_add[:], ALU.add).then_inc(masked_done, 1)
                        dve.wait_ge(masked_done, n)
                        nc.vector.tensor_reduce(neg_max[:, h, :], masked[:, h], X, ALU.max, negate=True).then_inc(max_done, 1)
                        if nxt:
                            low(g, *jobs_of(c, "t")[h], 2 * KC * (g + 1) + h)
                if c == 0 and new:
                    dve.wait_ge(mask_loaded, 16 * (g + 1))
                    if isinstance(g, int) and g == 0:
                        dve.wait_ge(consts, 2)
                    nc.vector.scalar_tensor_tensor(mask_add[:], mask_u8[:], -FMAX,
                                                   causal[:].rearrange("p (o k) -> p o k", o=1).broadcast_to([P, NB, P]),
                                                   ALU.mult, ALU.min).then_inc(mask_ready, 1)
                    dve.wait_ge(mask_ready, g + 1)
                if old:
                    dve.wait_ge(transposed, 2 * (u - 2) + 2)
                    wait(dve, pv_done, u - 2)
                    nc.vector.tensor_copy(probT[:, 1], trans[:]).then_inc(probT_copied[1], 1)
                if new:
                    for i, n in jobs_of(c, "v"):
                        b, before = nth(g, i)
                        dve.wait_ge(projected[b], before + 1)
                        cols = slice((n // NB) * VH, (n // NB + 1) * VH)
                        nc.vector.tensor_copy(v_sb[:, n % NB, cols], proj[b][:]).then_inc(copied[b], 1)
                if nxt:
                    low(g, *jobs_of(c, "t")[KC], 2 * KC * (g + 1) + KC)
                if c == 6 and new and more:
                    layernorm_moments(g + 1)
                ys = c == YC and new and not (isinstance(g, int) and g == 0)
                if ys:
                    residual(g, 0)
                if soft:
                    for h in range(2):
                        n = 2 * (u - 1) + h + 1
                        dve.wait_ge(exp_done, NB * n)
                        wait(dve, normed, n - 2)
                        nc.vector.reciprocal(rsums[:, h, :], psums[:, h, :]).then_inc(recip_done, 1)
                if nxt:
                    low(g, *jobs_of(c, "t")[KC + 1], 2 * KC * (g + 1) + KC + 1)
                if old:
                    dve.wait_ge(out_high, u - 1)
                    wait(dve, wo_done, u - 2)
                    nc.vector.tensor_tensor(o_lo[:], pv[:].rearrange("p b q -> p (b q)"), o_hi[:].bitcast(F32), ALU.subtract).then_inc(out_split, 1)
                if isinstance(g, int):
                    for work, n in beside.get((g, c), []):
                        work(n)
                if ys:
                    residual(g, 1)
                if c == YC + 1 and new and not (isinstance(g, int) and g == 0):
                    second_stats(g - 1)
                if c == 5 and new and more:
                    layernorm_stats(g + 1)
                if c == 6 and new and more:
                    normalise(g + 1)
                if c == YC + 3 and new and not (isinstance(g, int) and g == 0):
                    second_norm(g - 1)
                if c == NC - 1 and new and not (isinstance(g, int) and g == 0):
                    second_max(g - 1)

            def wide(a):
                return a[:].rearrange("p (a o) -> p a o", o=1).broadcast_to([P, NBLK, WBLOCK])

            def blocks(n):
                return w_raw[:, n * W1:(n + 1) * W1].rearrange("p (a b) -> p a b", b=WBLOCK)

            ints = w_int[:].rearrange("p (a b) -> p a b", b=WBLOCK)

            def weight_scales(n):
                dve.wait_ge(ffn_loaded, 48)
                wait(dve, dequantised, 5 * n)
                nc.vector.tensor_reduce(w_max[:], blocks(n), X, ALU.max, apply_absolute_value=True).then_inc(dequantised, 1)
                dve.wait_ge(dequantised, 5 * n + 1)
                nc.vector.tensor_scalar(w_scale[:], w_max[:], 1.0 / WQMAX, TINY, ALU.mult, ALU.max).then_inc(dequantised, 1)
                dve.wait_ge(dequantised, 5 * n + 2)
                nc.vector.reciprocal(w_inv[:], w_scale[:]).then_inc(dequantised, 1)

            def weight_ints(n):
                dve.wait_ge(dequantised, 5 * n + 3)
                nc.vector.tensor_tensor(ints, blocks(n), wide(w_inv), ALU.mult).then_inc(dequantised, 1)

            def weight_values(n):
                dve.wait_ge(dequantised, 5 * n + 4)
                nc.vector.tensor_tensor(blocks(n), ints, wide(w_scale), ALU.mult).then_inc(dequantised, 1)

            beside = {(0, 4): [(weight_scales, 0), (weight_ints, 0)],
                      (0, 6): [(weight_values, 0)],
                      (G - 1, 0): [(weight_scales, 1), (weight_ints, 1)],
                      (G - 1, 1): [(weight_values, 1)],
                      (G - 1, 2): [(weight_scales, 2)],
                      (G - 1, 5): [(weight_ints, 2)],
                      (G, 2): [(weight_values, 2)]}

            def residual(g, n):
                dve.wait_ge(xres_ready, g)
                wait(dve, x1_stored, 16 * (g - 1))
                i, _ = jobs_of(YC, "y")[n]
                b, before = nth(g, i)
                dve.wait_ge(projected[b], before + 1)
                rows = slice(n * NB // 2, (n + 1) * NB // 2)
                nc.vector.scalar_tensor_tensor(x1[:, rows], proj[b][:].rearrange("p (b d) -> p b d", d=D), tg[:, 0:1],
                                               xres[:, rows], ALU.mult, ALU.add).then_inc(copied[b], 1)

            def second_stats(g):
                wait_x1(dve, g + 1)
                for b in range(NB):
                    nc.vector.bn_stats(stats2[:, b, :], x1[:, b, :]).then_inc(stats2_done, 1)
                moments(stats2, mean2, vare2, stats2_done, MOMENTS * g + NB, var2_ready)

            def second_norm(g):
                dve.wait_ge(rstd2_ready, g + 1)
                wait(dve, xn2_stored, 16 * g)
                for b in range(NB):
                    nc.vector.tensor_scalar(xn2[:, b, :], x1[:, b, :], mean2[:, b:b + 1], rstd2[:, b:b + 1],
                                            ALU.subtract, ALU.mult).then_inc(xn2_ready, 1)

            def second_max(g):
                dve.wait_ge(xn2_ready, NB * (g + 1))
                nc.vector.tensor_reduce(amax_x[:, bass.ds(g, 1)],
                                        xn2[:].rearrange("p b d -> p (b d)"), X, ALU.max, apply_absolute_value=True)

            layernorm_stats(0)
            layernorm_moments(0)
            w_low_part(0)
            normalise(0)
            w_low_part(1)
            for n in range(2 * KC):
                low(-1, first_job(n), n, n)
            w_low_part(2)
            w_low_part(3)
            drive(dve, step)
            residual(G, 0)
            residual(G, 1)
            second_stats(G - 1)
            second_norm(G - 1)
            second_max(G - 1)

        @block.tensor
        def _(pe):
            pe.wait_ge(consts, 1)

            def product(b, before, stat, mov, n=KC):
                wait(pe, copied[b], before)
                passes = [(k, s, m) for k in range(n) for s, m in split(0, 1)]
                for j, (k, s, m) in enumerate(passes):
                    last = nc.tensor.matmul(proj[b][:], stat(s, k), mov(m, k), start=(j == 0), stop=(j == len(passes) - 1))
                last.then_inc(projected[b], 1)

            def weights_left(g, c, i, n):
                b, before = nth(g, i)
                w, t = (w_hi[n], w_lo[n]), (t_hi[n], t_lo[n])
                product(b, before, lambda s, k: w[s][:, k * INNER + c * P:k * INNER + (c + 1) * P], lambda m, k: t[m][:, k, :])

            def value(g, i, n):
                b, before = nth(g, i)
                e, half = n % NB, n // NB
                t, w = (t_hi[1], t_lo[1]), (w_hi[2], w_lo[2])
                product(b, before, lambda s, k: t[s][:, k, e * P:(e + 1) * P], 
                        lambda m, k: w[m][:, k * INNER + half * VH:k * INNER + (half + 1) * VH])

            def transpose_in(g, i, n):
                b, before = nth(g, i)
                if n == 0:
                    pe.wait_ge(xn_ready, g + 2)
                if n == KC:
                    pe.wait_ge(ctx_loaded, 16 * (g + 2))
                wait(pe, copied[b], before)
                src = (xn, ctx_in)[n // KC]
                for e in range(NB):
                    last = nc.tensor.transpose(proj[b][:, e * P:(e + 1) * P], src[:, e, (n % KC) * P:(n % KC + 1) * P], ident[:])
                last.then_inc(projected[b], 1)

            def transpose_prob(u, c, h):
                pe.wait_ge(normed, 2 * u + h + 1)
                wait(pe, probT_copied[1 - h], u + h)
                for b in range(NB):
                    last = nc.tensor.transpose(trans[:, b, :], prob[:, c % 2, h, b, :], ident[:])
                last.then_inc(transposed, 1)

            def times_v(u, c):
                for h in range(2):
                    pe.wait_ge(probT_copied[h], u + 1)
                wait(pe, out_split, u)
                for b in range(NB):
                    for h in range(2):
                        last = nc.tensor.matmul(pv[h * HD:(h + 1) * HD, b, :], v_sb[:, b, c * P + h * HD:c * P + (h + 1) * HD],
                                                probT[:, h, b, :], start=True, stop=True)
                last.then_inc(pv_done, 1)

            def scores(g, c, u):
                for kind in "qk":
                    (i, _), = jobs_of(c, kind)
                    b, before = nth(g, i)
                    pe.wait_ge(copied[b], before + 1)
                for h in range(2):
                    wait(pe, masked_done, 2 * (u - 1) + h + 1)
                rows = [slice(h * HD, (h + 1) * HD) for h in range(2)]
                for b in range(NB):
                    for h in range(2):
                        last = nc.tensor.matmul(score[h][:, b, :], qT[rows[h], b * P:(b + 1) * P], kT[rows[h], b * P:(b + 1) * P],
                                                start=True, stop=True)
                        if b == NB - 1:
                            last.then_inc(scored, 1)

            def out_product(u, c):
                pe.wait_ge(out_split, u + 1)
                w, o = (w_hi[3], w_lo[3]), (o_hi, o_lo)
                for k in range(KC):
                    for j, (s, m) in enumerate(split(0, 1)):
                        at = c * D + k * P
                        last = nc.tensor.matmul(yT[k][:], w[s][:, at:at + P], o[m][:], start=(c == 0 and j == 0),
                                                stop=(c == NC - 1 and j == 2), skip_group_check=True)
                last.then_inc(wo_done, 1)

            def transpose_y(g, i, n):
                b, before = nth(g, i)
                pe.wait_ge(yT_copied, KC * g)
                wait(pe, copied[b], before)
                for e in range(2):
                    for k in range(KC):
                        last = nc.tensor.transpose(proj[b][:, (e * KC + k) * P:(e * KC + k + 1) * P],
                                                   yT_sb[:, k, (2 * n + e) * P:(2 * n + e + 1) * P], ident[:])
                last.then_inc(projected[b], 1)

            def step(g, c):
                u, new, soft, old, more = parts(g, c)
                co = (c - 2) % NC
                nxt = c == NC - 1 and new and more
                ts = jobs_of(c, "t")
                first = isinstance(g, int) and g == 0 and c == 0
                oldest = not isinstance(g, int) or 3 <= u < U + 3
                if first:
                    pe.wait_ge(w_ready, 1)
                if new:
                    weights_left(g, c, jobs_of(c, "q")[0][0], 0)
                if nxt:
                    transpose_in(g, *ts[0])
                if oldest and c != NC - 2:
                    if isinstance(g, int) and u == 3:
                        pe.wait_ge(w_ready, 4)
                    if c == 3:
                        wait(pe, yT_copied, KC * g)
                    out_product(u - 3, (c - 3) % NC)
                if nxt:
                    transpose_in(g, *ts[1])
                if old:
                    transpose_prob(u - 2, co, 0)
                if first:
                    pe.wait_ge(w_ready, 2)
                if new:
                    weights_left(g, c, jobs_of(c, "k")[0][0], 1)
                if old:
                    transpose_prob(u - 2, co, 1)
                if nxt:
                    transpose_in(g, *ts[2])
                if oldest and c == NC - 2:
                    out_product(u - 3, (c - 3) % NC)
                if first:
                    pe.wait_ge(w_ready, 3)
                if new:
                    for i, n in jobs_of(c, "v"):
                        value(g, i, n)
                ys = jobs_of(c, "y") if new and not (isinstance(g, int) and g == 0) else []
                if nxt:
                    transpose_in(g, *ts[3])
                if ys:
                    transpose_y(g, *ys[0])
                if old:
                    times_v(u - 2, co)
                if ys:
                    transpose_y(g, *ys[1])
                if new:
                    scores(g, c, u)

            for n in range(2 * KC):
                transpose_in(-1, first_job(n), n)
            drive(pe, step)
            for i, n in jobs_of(YC, "y"):
                transpose_y(G, i, n)


def two_buffers(eng, G, step):
    step(0, 0, False)
    step(1, 1, False)
    with eng.Fori(1, G // 2 - 1) as i:
        step(2 * i, 0, False)
        step(2 * i + 1, 1, False)
    step(G - 2, 0, False)
    step(G - 1, 1, True)


def skip_two(eng, G, step):
    step(2, 0, False)
    step(3, 1, False)
    with eng.Fori(2, G // 2 - 1) as i:
        step(2 * i, 0, False)
        step(2 * i + 1, 1, False)
    step(G - 2, 0, False)
    step(G - 1, 1, True)


def product(nc, bank, stat, mov, KC):
    passes = [(k, s, m) for k in range(KC) for s, m in split(0, 1)]
    for j, (k, s, m) in enumerate(passes):
        last = nc.tensor.matmul(bank, stat(s, k), mov(m, k), start=(j == 0), stop=(j == len(passes) - 1))
    return last


def gate_products(nc, w_raw, ident, xn2_d, n_x_d, gate_d, wup, wd, n_x, xT, stage, amax_x, ext_gate, s_x, G):
    I, KC = wup[0].shape[2], wup[0].shape[1]
    D = KC * P
    IC, T = I // P, NB * P
    RING = IC
    W1 = IC * D
    with ExitStack() as st:
        def sb(name, shape, dt=F32):
            return st.enter_context(nc.sbuf_tensor(name, shape, dt))

        def sem(name):
            return st.enter_context(nc.semaphore(name))

        wgate = [sb(f"wgate_{n}", [P, KC, I], F32R) for n in ("hi", "lo")]
        xin = sb("xin", [P, 2, NB, D])
        a1 = sb("a1", [P, 1])
        a2 = sb("a2", [P, 1])
        inv_x = sb("inv_x", [P, 1])
        ring = [st.enter_context(nc.psum_tensor(f"ring{n}", [P, T], F32)) for n in range(RING)]
        tr = [st.enter_context(nc.psum_tensor(f"tr{k}", [P, T], F32)) for k in range(KC)]

        w_transposed = sem("w_transposed")
        w_high = sem("w_high2")
        w_copied = sem("w_copied")
        amax_local = sem("amax_local")
        amax_all = sem("amax_all")
        scale_step = sem("scale_step")
        x_loaded = [sem(f"xn2_loaded{b}") for b in range(2)]
        x_transposed = sem("x_transposed")
        x_int = sem("x_int")
        x_high = sem("x_high")
        x_ready = sem("x_ready")
        product_done = sem("product_done")
        staged = sem("staged")
        reduced = sem("reduced")
        n_x_stored = [sem(f"n_x_stored{b}") for b in range(2)]
        stored = [sem(f"gate_stored{b}") for b in range(2)]
        block = st.enter_context(nc.Block())

        HI = IC // 2
        targets = (wup, wgate)
        w_jobs = [("ug", m, k, h) for m in (1, 0) for k in range(KC) for h in range(2)] + [("d", i, 0, 0) for i in range(HI)]

        def weights(n, part):
            kind, m, k, h = w_jobs[n]
            if kind == "ug":
                return targets[m][part][:, k, h * HI * P:(h + 1) * HI * P], ring[n % RING][:, 0:HI * P]
            return wd[part][:, 2 * m * D:(2 * m + 2) * D], ring[n % RING][:]

        @block.sync
        def _(sp):
            def load(t, b):
                sp.dma_start(xin[:, b], xn2_d[:, t]).then_inc(x_loaded[b], 16)

            def step(t, b, more):
                if more:
                    sp.wait_ge(x_transposed, KC * (t + 1))
                    load(t + 2, b)
                last = isinstance(t, int) and t == G - 1
                sp.wait_ge(x_int, KC * (t + 1))
                sp.dma_start(n_x_d[:, 0] if last else n_x_d[:, 1:][:, t], n_x[:, b]).then_inc(n_x_stored[b], 16)
                if last:
                    return
                sp.wait_ge(staged, IC * (t + 1))
                sp.dma_start(gate_d[:, t], stage[b][:]).then_inc(stored[b], 16)

            load(0, 0)
            load(1, 1)
            with sp.Fori(0, G // 2 - 1) as i:
                for b in range(2):
                    step(2 * i + b, b, True)
            for b in range(2):
                step(G - 2 + b, b, False)
            for b in range(2):
                sp.wait_ge(stored[b], 8 * G - 16 * b)
                sp.wait_ge(n_x_stored[b], 8 * G)

        @block.gpsimd
        def _(gp):
            gp.wait_ge(amax_local, 1)
            gp.partition_all_reduce(a2[:], a1[:], P, ABSMAX).then_inc(amax_all, 1)

        @block.scalar
        def _(act):
            for n in range(len(w_jobs)):
                act.wait_ge(w_transposed, n + 1)
                to, bank = weights(n, 0)
                nc.scalar.activation(to, bank, ACT.Copy).then_inc(w_high, 1)

            def quantise_x(t, b):
                wait(act, n_x_stored[b], 8 * (t - b))
                wait(act, x_ready, KC * (t - 1))
                for k in range(KC):
                    act.wait_ge(x_transposed, KC * t + k + 1)
                    nc.scalar.activation(n_x[:, b, k, :], tr[k][:], ACT.Copy, scale=inv_x[:, 0:1]).then_inc(x_int, 1)
                wait(act, product_done, IC * (t - 1))
                for k in range(KC):
                    act.wait_ge(x_int, KC * t + k + 1)
                    nc.scalar.activation(xT[b][0][:, k, :], n_x[:, b, k, :], ACT.Copy).then_inc(x_high, 1)

            def step(t, b, last):
                if not last:
                    quantise_x(t + 1, 1 - b)
                for n in range(IC):
                    act.wait_ge(product_done, IC * t + n + 1)
                    if n == 0:
                        wait(act, reduced, 4 * (t - 1))
                        wait(act, stored[b], 8 * (t - b))
                    nc.scalar.activation(stage[b][:, n * T:(n + 1) * T], ring[n][:], ACT.Copy).then_inc(staged, 1)

            act.wait_ge(scale_step, 2)
            quantise_x(0, 0)
            two_buffers(act, G, step)

        @block.vector
        def _(dve):
            v = nc.vector
            v.tensor_reduce(a1[:], amax_x[:], X, ALU.max).then_inc(amax_local, 1)
            dve.wait_ge(amax_all, 1)
            v.tensor_scalar(s_x[:], a2[:], 1.0 / QMAX, TINY, ALU.mult, ALU.max).then_inc(scale_step, 1)
            dve.wait_ge(scale_step, 1)
            v.reciprocal(inv_x[:], s_x[:]).then_inc(scale_step, 1)
            dve.wait_ge(scale_step, 2)
            for n in range(len(w_jobs)):
                dve.wait_ge(w_high, n + 1)
                to, bank = weights(n, 1)
                v.tensor_tensor(to, bank, weights(n, 0)[0].bitcast(F32), ALU.subtract).then_inc(w_copied, 1)

            def low(t, b):
                wait(dve, product_done, IC * (t - 1))
                for k in range(KC):
                    dve.wait_ge(x_high, KC * t + k + 1)
                    v.tensor_tensor(xT[b][1][:, k, :], n_x[:, b, k, :], xT[b][0][:, k, :].bitcast(F32), ALU.subtract).then_inc(x_ready, 1)

            def extremes(t, b, h):
                dve.wait_ge(staged, IC * t + (h + 1) * HI)
                for e, op in enumerate((ALU.max, ALU.min)):
                    v.tensor_reduce(ext_gate[:, e, bass.ds(2 * t + h, 1)], stage[b][:, h * HI * T:(h + 1) * HI * T],
                                    X, op).then_inc(reduced, 1)

            def step(t, b, last):
                if not last:
                    low(t + 1, 1 - b)
                extremes(t, b, 0)
                extremes(t, b, 1)

            low(0, 0)
            two_buffers(dve, G, step)

        @block.tensor
        def _(pe):
            for n, (kind, m, k, h) in enumerate(w_jobs):
                if n >= RING:
                    pe.wait_ge(w_copied, n - RING + 1)
                for e in range(HI if kind == "ug" else 4):
                    if kind == "ug":
                        at = m * W1 + (h * HI + e) * D + k * P
                    else:
                        at = 2 * W1 + (e % 2) * I + (2 * m + e // 2) * P
                    last = nc.tensor.transpose(ring[n % RING][:, e * P:(e + 1) * P], w_raw[:, at:at + P], ident[:])
                last.then_inc(w_transposed, 1)

            def transpose_x(t, b):
                pe.wait_ge(x_loaded[b], 8 * (t - b) + 16)
                for k in range(KC):
                    wait(pe, x_int, KC * (t - 1) + k + 1)
                    for e in range(NB):
                        last = nc.tensor.transpose(tr[k][:, e * P:(e + 1) * P], xin[:, b, e, k * P:(k + 1) * P], ident[:])
                    last.then_inc(x_transposed, 1)

            def step(t, b, last):
                if not last:
                    transpose_x(t + 1, 1 - b)
                pe.wait_ge(x_ready, KC * (t + 1))
                for n in range(IC):
                    wait(pe, staged, IC * (t - 1) + n + 1)
                    product(nc, ring[n][:], lambda s, k: wgate[s][:, k, n * P:(n + 1) * P],
                            lambda m, k: xT[b][m][:, k, :], KC).then_inc(product_done, 1)

            transpose_x(0, 0)
            pe.wait_ge(w_copied, len(w_jobs))
            two_buffers(pe, G, step)


NEGATIVE_SILU = 0.279


def gate_scales(nc, gate_d, last_gate, ext_gate, s_x, s_g, k_g, k_p, s_p, G, N):
    with ExitStack() as st:
        def sb(name, shape, dt=F32):
            return st.enter_context(nc.sbuf_tensor(name, shape, dt))

        def sem(name):
            return st.enter_context(nc.semaphore(name))

        a1 = sb("a1g", [P, 2])
        a2 = sb("a2g", [P, 2])
        a3 = sb("a3g", [P, 1])
        a4 = sb("a4g", [P, 1])
        inv_g = sb("inv_g", [P, 1])
        unit_p = sb("unit_p", [P, 1])
        n_top = sb("n_top", [P, 1], I16)
        sig_top = sb("sig_top", [P, 1])
        n_sig_top = sb("n_sig_top", [P, 1], U16)
        p_top = sb("p_top", [P, 1])
        silu_top = sb("silu_top", [P, 1])
        slow = sb("slow", [P, 1], mybir.dt.int32)
        local = sem("local3")
        overall = sem("overall3")
        step_done = sem("step_done3")
        top_sig = sem("top_sig")
        slow_known = sem("slow_known")

        with ExitStack() as st1:
            block = st1.enter_context(nc.Block())

            @block.gpsimd
            def _(gp):
                gp.wait_ge(local, 2)
                gp.partition_all_reduce(a2[:], a1[:], P, bass.bass_isa.ReduceOp.max).then_inc(overall, 1)

            @block.scalar
            def _(act):
                act.wait_ge(step_done, 7)
                nc.scalar.activation(sig_top[:], n_top[:], ACT.Sigmoid, scale=s_g[:, 0:1]).then_inc(top_sig, 1)

            @block.vector
            def _(dve):
                v = nc.vector
                n = [0]

                def chain(ins):
                    n[0] += 1
                    ins.then_inc(step_done, 1)
                    dve.wait_ge(step_done, n[0])

                v.tensor_reduce(a1[:, 0:1], ext_gate[:, 0, :], X, ALU.max).then_inc(local, 1)
                v.tensor_reduce(a1[:, 1:2], ext_gate[:, 1, :], X, ALU.min, negate=True).then_inc(local, 1)
                dve.wait_ge(overall, 1)
                chain(v.tensor_tensor(a3[:], a2[:, 0:1], a2[:, 1:2], ALU.max))
                chain(v.tensor_scalar(a4[:], a3[:], s_x[:, 0:1], 1.0 / QMAX, ALU.mult, ALU.mult))
                chain(v.tensor_scalar(s_g[:], a4[:], TINY, None, ALU.max))
                chain(v.reciprocal(inv_g[:], s_g[:]))
                chain(v.tensor_scalar(k_g[:], inv_g[:], s_x[:, 0:1], None, ALU.mult))
                chain(v.tensor_scalar(unit_p[:], s_g[:], 1.0 / 65536.0, None, ALU.mult))
                chain(v.tensor_scalar(n_top[:], a2[:, 0:1], k_g[:, 0:1], None, ALU.mult))
                dve.wait_ge(top_sig, 1)
                chain(v.tensor_scalar(n_sig_top[:], sig_top[:], 65536.0, 65535.0, ALU.mult, ALU.min))
                chain(v.tensor_tensor(p_top[:], n_top[:], n_sig_top[:], ALU.mult))
                chain(v.tensor_scalar(silu_top[:], p_top[:], unit_p[:, 0:1], None, ALU.mult))
                v.tensor_scalar(slow[:], silu_top[:], NEGATIVE_SILU, None, ALU.is_lt).then_inc(slow_known, 1)

        with ExitStack() as st2:
            gate = st2.enter_context(nc.sbuf_tensor("gate_all", [P, N], F32))
            n_g = st2.enter_context(nc.sbuf_tensor("n_g_all", [P, N], I16))
            sig = st2.enter_context(nc.sbuf_tensor("sig_all", [P, N], F32))
            n_s = st2.enter_context(nc.sbuf_tensor("n_s_all", [P, N], U16))
            prod = st2.enter_context(nc.sbuf_tensor("prod_all", [P, N], F32))
            amax = st2.enter_context(nc.sbuf_tensor("amax_prod", [P, G], F32))
            am1 = st2.enter_context(nc.sbuf_tensor("am1", [P, 1], F32))
            loaded, rounded, sig_done, sig_int, prod_done, reduced, am_local, am_all = (
                st2.enter_context(nc.semaphore(n)) for n in
                ("gate_all_loaded", "gate_all_rounded", "sig_all_done", "sig_all_int", "prod_all_done", "prod_reduced", "am_local", "am_all"))
            block = st2.enter_context(nc.Block())

            def if_slow(eng):
                return eng.If(eng.value_load(slow[0:1, 0:1], min_val=0, max_val=1) == 1)

            @block.sync
            def _(sp):
                sp.wait_ge(slow_known, 1)
                with if_slow(sp):
                    with sp.Fori(0, G - 1) as t:
                        sp.wait_ge(prod_done, t + 1)
                        sp.dma_start(gate[:], gate_d[:, t]).then_inc(loaded, 16)
                    sp.wait_ge(prod_done, G)
                    sp.dma_start(gate[:], last_gate[:]).then_inc(loaded, 16)

            @block.gpsimd
            def _(gp):
                gp.wait_ge(slow_known, 1)
                with if_slow(gp):
                    gp.wait_ge(am_local, 1)
                    gp.partition_all_reduce(p_top[:], am1[:], P, ABSMAX).then_inc(am_all, 1)

            @block.scalar
            def _(act):
                act.wait_ge(slow_known, 1)
                with if_slow(act):
                    with act.Fori(0, G) as t:
                        act.wait_ge(loaded, 16 * t + 16)
                        nc.scalar.activation(n_g[:], gate[:], ACT.Copy, scale=k_g[:, 0:1]).then_inc(rounded, 1)
                        act.wait_ge(rounded, t + 1)
                        nc.scalar.activation(sig[:], n_g[:], ACT.Sigmoid, scale=s_g[:, 0:1]).then_inc(sig_done, 1)

            @block.vector
            def _(dve):
                v = nc.vector
                dve.wait_ge(slow_known, 1)
                with if_slow(dve):
                    v.memset(prod[:], 0.0).then_inc(prod_done, 1)
                    with dve.Fori(0, G) as t:
                        dve.wait_ge(sig_done, t + 1)
                        v.tensor_scalar(n_s[:], sig[:], 65536.0, 65535.0, ALU.mult, ALU.min).then_inc(sig_int, 1)
                        dve.wait_ge(sig_int, t + 1)
                        v.tensor_tensor(prod[:], n_g[:], n_s[:], ALU.mult).then_inc(prod_done, 1)
                        dve.wait_ge(prod_done, t + 2)
                        v.tensor_reduce(amax[:, bass.ds(t, 1)], prod[:], X, ALU.max, apply_absolute_value=True).then_inc(reduced, 1)
                    dve.wait_ge(reduced, G)
                    v.tensor_reduce(am1[:], amax[:], X, ALU.max).then_inc(am_local, 1)
                    dve.wait_ge(am_all, 1)
                n = [10]

                def chain(ins):
                    n[0] += 1
                    ins.then_inc(step_done, 1)
                    dve.wait_ge(step_done, n[0])

                chain(v.tensor_scalar(a3[:], p_top[:], unit_p[:, 0:1], 1.0 / QMAX, ALU.mult, ALU.mult))
                chain(v.tensor_scalar(s_p[:], a3[:], TINY, None, ALU.max))
                chain(v.reciprocal(a4[:], s_p[:]))
                chain(v.tensor_scalar(k_p[:], a4[:], unit_p[:, 0:1], None, ALU.mult))


PAIRS = 3


def up_product(nc, pe, pair, wup, xT, reads, done):
    KC, T = wup[0].shape[1], NB * P
    for i in range(PAIRS):
        reads(i)
        for e in range(2):
            n = 2 * i + e
            last = product(nc, pair[i][:, e * T:(e + 1) * T], lambda s, k: wup[s][:, k, n * P:(n + 1) * P],
                           lambda m, k: xT[m][:, k, :], KC)
        last.then_inc(done, 1)


class Ahead:

    def __init__(self, nc, st):
        self.loaded = [st.enter_context(nc.semaphore(f"x_ahead_loaded{b}")) for b in range(2)]
        self.widened, self.high, self.ready = (st.enter_context(nc.semaphore(f"x_ahead_{n}")) for n in ("widened", "high", "ready"))


def up_products(nc, n_x_d, gate_d, wup, n_x, xT, x_wide, gate, sig, stage, n_p, ahead, amax_up, s_g, k_g, k_p, G, IC):
    T = NB * P
    KC = wup[0].shape[1]
    H = IC * T // 2
    PN = 2 * T
    assert IC == 2 * PAIRS
    with ExitStack() as st:
        def sb(name, shape, dt=F32):
            return st.enter_context(nc.sbuf_tensor(name, shape, dt))

        def sem(name):
            return st.enter_context(nc.semaphore(name))

        n_g = sb("n_g2", [P, 2, H], I16)
        n_s = sb("n_s2", [P, 2, H], U16)
        pair = [st.enter_context(nc.psum_tensor(f"pair{n}", [P, PN], F32)) for n in range(PAIRS)]
        x_loaded = [sem(f"n_x_loaded{b}") for b in range(2)]
        gate_loaded = [sem(f"gate_loaded{h}") for h in range(2)]
        x_widened = sem("x_widened")
        x_high = sem("x_high2")
        x_ready = sem("x_ready2")
        product_done = sem("product_done2")
        staged = sem("staged2")
        reduced = sem("reduced2")
        rounded = [sem(f"gate_rounded{h}") for h in range(2)]
        sig_done = [sem(f"sig_done{h}") for h in range(2)]
        sig_int = [sem(f"sig_int{h}") for h in range(2)]
        silu_int = [sem(f"silu_int{h}") for h in range(2)]
        block = st.enter_context(nc.Block())

        def kept(t):
            return isinstance(t, int) and t >= G - 2

        @block.sync
        def _(sp):
            def load_x(t, b):
                sp.dma_start(n_x[:, 1 - b], n_x_d[:, t]).then_inc(x_loaded[b], 16)

            def load_gate(t, h):
                sp.dma_start(gate[:, h], gate_d[:, t - 1, h * H:(h + 1) * H]).then_inc(gate_loaded[h], 16)

            def step(t, b, more):
                if more:
                    wait(sp, x_high, KC * t)
                    load_x(t + 2, b)
                for h in range(2):
                    sp.wait_ge(rounded[h], t + 1)
                    load_gate(t + 1, h)

            load_x(1, 1)
            with sp.Fori(0, G // 2 - 1) as i:
                for b in range(2):
                    step(2 * i + b, b, True)
            step(G - 2, 0, False)
            for b in range(2):
                sp.wait_ge(x_high, KC * (G - 2 + b))
                sp.dma_start(n_x[:, 1 - b], n_x_d[:, b]).then_inc(ahead.loaded[b], 16)

        @block.gpsimd
        def _(gp):
            def step(t, b, last):
                if isinstance(t, int) and t == 0:
                    return
                gp.wait_ge(x_widened, t)
                for k in range(KC):
                    gp.wait_ge(x_high, KC * (t - 1) + k + 1)
                    gp.tensor_tensor(xT[1 - b][1][:, k, :], x_wide[:, k, :], xT[1 - b][0][:, k, :].bitcast(F32), ALU.subtract).then_inc(x_ready, 1)

            two_buffers(gp, G, step)
            gp.wait_ge(ahead.widened, 1)
            for k in range(KC):
                gp.wait_ge(ahead.high, k + 1)
                gp.tensor_tensor(xT[1][1][:, k, :], x_wide[:, k, :], xT[1][0][:, k, :].bitcast(F32), ALU.subtract).then_inc(ahead.ready, 1)

        @block.scalar
        def _(act):
            def high(t, b):
                act.wait_ge(x_loaded[b], 8 * t + 8 * b)
                wait(act, x_ready, KC * (t - 1))
                nc.scalar.activation(x_wide[:], n_x[:, 1 - b], ACT.Copy).then_inc(x_widened, 1)
                wait(act, product_done, PAIRS * (t - 1))
                for k in range(KC):
                    nc.scalar.activation(xT[1 - b][0][:, k, :], n_x[:, 1 - b, k, :], ACT.Copy).then_inc(x_high, 1)

            def round_gate(t, h):
                wait(act, gate_loaded[h], 16 * t)
                wait(act, silu_int[h], t)
                nc.scalar.activation(n_g[:, h], gate[:, h], ACT.Copy, scale=k_g[:, 0:1]).then_inc(rounded[h], 1)

            def sigmoid(t, h):
                act.wait_ge(rounded[h], t + 1)
                wait(act, sig_int[h], t)
                nc.scalar.activation(sig[:, h], n_g[:, h], ACT.Sigmoid, scale=s_g[:, 0:1]).then_inc(sig_done[h], 1)

            def step(t, b, last):
                for h in range(2):
                    round_gate(t, h)
                    sigmoid(t, h)
                if not last:
                    high(t + 1, 1 - b)
                else:
                    act.wait_ge(ahead.loaded[0], 16)
                    act.wait_ge(x_ready, KC * (G - 1))
                    nc.scalar.activation(x_wide[:], n_x[:, 1], ACT.Copy).then_inc(ahead.widened, 1)
                    act.wait_ge(product_done, PAIRS * (G - 1))
                    for k in range(KC):
                        nc.scalar.activation(xT[1][0][:, k, :], n_x[:, 1, k, :], ACT.Copy).then_inc(ahead.high, 1)
                if kept(t):
                    for i in range(PAIRS):
                        act.wait_ge(product_done, PAIRS * t + i + 1)
                        nc.scalar.activation(stage[b][:, i * PN:(i + 1) * PN], pair[i][:], ACT.Copy).then_inc(staged, 1)

            two_buffers(act, G, step)

        @block.vector
        def _(dve):
            v = nc.vector

            def silu(t, h):
                dve.wait_ge(sig_done[h], t + 1)
                wait(dve, silu_int[h], t)
                v.tensor_scalar(n_s[:, h], sig[:, h], 65536.0, 65535.0, ALU.mult, ALU.min).then_inc(sig_int[h], 1)
                dve.wait_ge(sig_int[h], t + 1)
                v.scalar_tensor_tensor(n_p[:, bass.ds(t, 1), h * H:(h + 1) * H].rearrange("p o n -> p (o n)"), n_g[:, h], k_p[:, 0:1],
                                       n_s[:, h], ALU.mult, ALU.mult).then_inc(silu_int[h], 1)

            def maximum(t, b, i):
                if kept(t):
                    dve.wait_ge(staged, PAIRS * (t - (G - 2)) + i + 1)
                    up = stage[b][:, i * PN:(i + 1) * PN]
                else:
                    dve.wait_ge(product_done, PAIRS * t + i + 1)
                    up = pair[i][:]
                v.tensor_reduce(amax_up[:, bass.ds(PAIRS * t + i, 1)], up, X, ALU.max, apply_absolute_value=True).then_inc(reduced, 1)

            def step(t, b, last):
                silu(t, 0)
                maximum(t, b, 0)
                silu(t, 1)
                maximum(t, b, 1)
                maximum(t, b, 2)

            two_buffers(dve, G, step)

        @block.tensor
        def _(pe):
            def step(t, b, last):
                wait(pe, x_ready, KC * t)
                up_product(nc, pe, pair, wup, xT[1 - b], lambda i: wait(pe, reduced, PAIRS * (t - 1) + i + 1), product_done)

            two_buffers(pe, G, step)


def hidden_max(nc, n_x_d, n_u_d, wup, n_x, xT, x_wide, up, n_u, hid, n_p, ahead, prefetch, amax_up, amax_hid, s_x, s_p, s_hid, G, N):
    KC, T = wup[0].shape[1], NB * P
    PN = 2 * T
    x_loaded, x_widened, x_high, x_ready = ahead.loaded, ahead.widened, ahead.high, ahead.ready
    with ExitStack() as st:
        def sb(name, shape, dt=F32):
            return st.enter_context(nc.sbuf_tensor(name, shape, dt))

        def sem(name):
            return st.enter_context(nc.semaphore(name))

        a1 = sb("a1h", [P, 1])
        a2 = sb("a2h", [P, 1])
        a3 = sb("a3h", [P, 1])
        s_u = sb("s_u", [P, 1])
        r_u = sb("r_u", [P, 1])
        k_u = sb("k_u", [P, 1])
        pair = [st.enter_context(nc.psum_tensor(f"pair4{n}", [P, PN], F32)) for n in range(PAIRS)]
        amax_local = sem("amax_local4")
        amax_all = sem("amax_all4")
        scale_step = sem("scale_step4")
        product_done = sem("product_done4")
        up_int = sem("up_int")
        hid_done = sem("hid_done")
        hid_reduced = sem("hid_reduced")
        stored = [sem(f"n_u_stored{b}") for b in range(2)]

        def slot(t):
            return G - 2 + t if isinstance(t, int) and t < 2 else t - 2

        def on_chip(t):
            return isinstance(t, int) and t < 2

        block = st.enter_context(nc.Block())

        @block.sync
        def _(sp):
            def load_x(t, b):
                sp.dma_start(n_x[:, 1 - b], n_x_d[:, slot(t)]).then_inc(x_loaded[b], 16)

            def step(t, b, more):
                if more and not on_chip(t):
                    sp.wait_ge(x_high, KC * (t - 1))
                    load_x(t + 2, b)
                sp.wait_ge(up_int, PAIRS * (t + 1))
                sp.dma_start(n_u_d[:, slot(t)], n_u[:, b]).then_inc(stored[b], 16)

            for b in range(2):
                step(b, b, True)
            with sp.Fori(1, G // 2 - 1) as i:
                for b in range(2):
                    step(2 * i + b, b, True)
            for b in range(2):
                sp.wait_ge(stored[b], 32)
            prefetch(sp)
            for b in range(2):
                step(G - 2 + b, b, False)
            for b in range(2):
                sp.wait_ge(stored[b], 8 * G)

        @block.gpsimd
        def _(gp):
            gp.wait_ge(amax_local, 1)
            gp.partition_all_reduce(a2[:], a1[:], P, ABSMAX).then_inc(amax_all, 1)

            def step(t, b, last):
                if isinstance(t, int) and t <= 2:
                    return
                gp.wait_ge(x_widened, t - 1)
                for k in range(KC):
                    gp.wait_ge(x_high, KC * (t - 2) + k + 1)
                    gp.tensor_tensor(xT[1 - b][1][:, k, :], x_wide[:, k, :], xT[1 - b][0][:, k, :].bitcast(F32), ALU.subtract).then_inc(x_ready, 1)

            skip_two(gp, G, step)

        @block.scalar
        def _(act):
            def high(t, b):
                act.wait_ge(x_loaded[b], 8 * (t - b))
                wait(act, x_ready, KC * (t - 2))
                nc.scalar.activation(x_wide[:], n_x[:, 1 - b], ACT.Copy).then_inc(x_widened, 1)
                wait(act, product_done, PAIRS * (t - 3))
                for k in range(KC):
                    nc.scalar.activation(xT[1 - b][0][:, k, :], n_x[:, 1 - b, k, :], ACT.Copy).then_inc(x_high, 1)

            def step(t, b, last):
                wait(act, stored[b], 8 * (t - b))
                wait(act, hid_done, PAIRS * (t - 1))
                for i in range(PAIRS):
                    part = slice(i * PN, (i + 1) * PN)
                    if on_chip(t):
                        source = up[b][:, part]
                    else:
                        act.wait_ge(product_done, PAIRS * (t - 2) + i + 1)
                        source = pair[i][:]
                    nc.scalar.activation(n_u[:, b, part], source, ACT.Copy, scale=k_u[:, 0:1]).then_inc(up_int, 1)
                if not (isinstance(t, int) and (t == 0 or t >= G - 2)):
                    high(t + 2, b)

            act.wait_ge(scale_step, 4)
            two_buffers(act, G, step)

        @block.vector
        def _(dve):
            v = nc.vector
            v.tensor_reduce(a1[:], amax_up[:], X, ALU.max).then_inc(amax_local, 1)
            dve.wait_ge(amax_all, 1)
            v.tensor_scalar(a3[:], a2[:], s_x[:, 0:1], 1.0 / QMAX, ALU.mult, ALU.mult).then_inc(scale_step, 1)
            dve.wait_ge(scale_step, 1)
            v.tensor_scalar(s_u[:], a3[:], TINY, None, ALU.max).then_inc(scale_step, 1)
            dve.wait_ge(scale_step, 2)
            v.reciprocal(r_u[:], s_u[:]).then_inc(scale_step, 1)
            dve.wait_ge(scale_step, 3)
            v.tensor_scalar(k_u[:], r_u[:], s_x[:, 0:1], None, ALU.mult).then_inc(scale_step, 1)
            v.tensor_tensor(s_hid[:], s_p[:], s_u[:], ALU.mult).then_inc(scale_step, 1)

            def step(t, b, last):
                def part(i):
                    return slice(i * PN, (i + 1) * PN)

                def times(i):
                    n = PAIRS * t + i
                    wait(dve, hid_reduced, n - PAIRS + 1)
                    dve.wait_ge(up_int, n + 1)
                    v.tensor_tensor(hid[:, part(i)], n_p[:, bass.ds(slot(t), 1), part(i)].rearrange("p o n -> p (o n)"),
                                    n_u[:, b, part(i)], ALU.mult).then_inc(hid_done, 1)

                def largest(i):
                    n = PAIRS * t + i
                    dve.wait_ge(hid_done, n + 1)
                    v.tensor_reduce(amax_hid[:, bass.ds(n, 1)], hid[:, part(i)], X, ALU.max,
                                    apply_absolute_value=True).then_inc(hid_reduced, 1)

                times(0)
                for i in range(1, PAIRS):
                    times(i)
                    largest(i - 1)
                largest(PAIRS - 1)

            two_buffers(dve, G, step)

        @block.tensor
        def _(pe):
            def step(t, b, last):
                pe.wait_ge(x_ready, KC * (t - 1))

                def pair_read(i):
                    if not (isinstance(t, int) and t == 2):
                        pe.wait_ge(up_int, PAIRS * (t - 1) + i + 1)

                up_product(nc, pe, pair, wup, xT[1 - b], pair_read, product_done)

            skip_two(pe, G, step)


def group(t, G):
    return G - 1 if isinstance(t, int) and t == 0 else t - 1


def down_loads(nc, st, n_u_d, x1_d, n_u, x1, G):
    n_u_loaded = [st.enter_context(nc.semaphore(f"n_u_loaded{b}")) for b in range(2)]
    x1_loaded = [st.enter_context(nc.semaphore(f"x1_loaded{b}")) for b in range(2)]

    def load(sp, t, b):
        sp.dma_start(n_u[b], n_u_d[:, t]).then_inc(n_u_loaded[b], 16)

    def load_x1(sp, t, b):
        sp.dma_start(x1[b], x1_d[:, group(t, G)]).then_inc(x1_loaded[b], 16)

    return n_u, x1, n_u_loaded, x1_loaded, load, load_x1


def down_products(nc, loads, g_ffn, ident, n_h, yT_sb, res, n_p, wd, out, amax_hid, s_hid, G, IC):
    D = wd[0].shape[1] // IC
    KC, T = D // P, NB * P
    HJ = IC // 2
    H = HJ * T
    n_u, x1, n_u_loaded, x1_loaded, load, load_x1 = loads
    with ExitStack() as st:
        def sb(name, shape, dt=F32):
            return st.enter_context(nc.sbuf_tensor(name, shape, dt))

        def sem(name):
            return st.enter_context(nc.semaphore(name))

        h_hi = sb("h_hi", [P, 2, H], F32R)
        h_lo = sb("h_lo", [P, 2, H], F32R)
        tg = sb("tg5", [P, 1])
        a1 = sb("a1o", [P, 1])
        a2 = sb("a2o", [P, 1])
        a3 = sb("a3o", [P, 1])
        s_o = sb("s_o", [P, 1])
        r_o = sb("r_o", [P, 1])
        k_o = sb("k_o", [P, 1])
        y_scale = sb("y_scale", [P, 1])
        yT = [[st.enter_context(nc.psum_tensor(f"yT5{b}{k}", [P, T], F32)) for k in range(KC)] for b in range(2)]
        y = [st.enter_context(nc.psum_tensor(f"y5{b}", [P, NB, D], F32)) for b in range(2)]
        tg_loaded = sem("tg_loaded5")
        tg_ready = sem("tg_ready5")
        amax_local = sem("amax_local5")
        amax_all = sem("amax_all5")
        scale_step = sem("scale_step5")
        rounded = sem("rounded5")
        high_done = sem("high_done5")
        low_done = sem("low_done5")
        half_done = sem("half_done5")
        yT_copied = sem("yT_copied5")
        transposed = sem("transposed5")
        res_done = sem("res_done")
        stored = [sem(f"out_stored{b}") for b in range(2)]
        block = st.enter_context(nc.Block())

        @block.sync
        def _(sp):
            sp.dma_start(tg[:], g_ffn.rearrange("(o n) -> o n", o=1).broadcast_to([P, 1])).then_inc(tg_loaded, 16)

            def store(t, b):
                sp.wait_ge(res_done, t + 1)
                sp.dma_start(out[bass.ds(group(t, G) * NB, NB)].rearrange("b p d -> p b d"), res[b][:]).then_inc(stored[b], 16)

            def step(t, b, more):
                if more:
                    sp.wait_ge(rounded, 2 * (t + 1))
                    load(sp, t + 2, b)
                if not (isinstance(t, int) and t == 0):
                    store(t - 1, 1 - b)
                    if not (isinstance(t, int) and t == G - 1):
                        load_x1(sp, t + 1, 1 - b)

            for b in range(2):
                step(b, b, True)
            with sp.Fori(1, G // 2 - 1) as i:
                for b in range(2):
                    step(2 * i + b, b, True)
            for b in range(2):
                step(G - 2 + b, b, False)
            store(G - 1, 1)
            for b in range(2):
                sp.wait_ge(stored[b], 8 * G)

        @block.gpsimd
        def _(gp):
            gp.wait_ge(amax_local, 1)
            gp.partition_all_reduce(a2[:], a1[:], P, ABSMAX).then_inc(amax_all, 1)

        @block.scalar
        def _(act):
            act.wait_ge(tg_loaded, 16)
            nc.scalar.activation(tg[:], tg[:], ACT.Tanh).then_inc(tg_ready, 1)

            def high(t, h):
                act.wait_ge(rounded, 2 * t + h + 1)
                wait(act, half_done, 2 * (t - 1) + h + 1)
                nc.scalar.activation(h_hi[:, h], n_h[:, h], ACT.Copy).then_inc(high_done, 1)

            def copy_y(t, b):
                act.wait_ge(half_done, 2 * t + 2)
                wait(act, transposed, t)
                for k in range(KC):
                    nc.scalar.activation(yT_sb[:, k, :], yT[b][k][:], ACT.Copy).then_inc(yT_copied, 1)

            def step(t, b, last):
                high(t, 1)
                if not (isinstance(t, int) and t == 0):
                    copy_y(t - 1, 1 - b)
                if not last:
                    high(t + 1, 0)

            high(0, 0)
            two_buffers(act, G, step)
            copy_y(G - 1, 1)

        @block.vector
        def _(dve):
            v = nc.vector
            v.tensor_reduce(a1[:], amax_hid[:], X, ALU.max).then_inc(amax_local, 1)
            dve.wait_ge(amax_all, 1)
            v.tensor_scalar(a3[:], a2[:], s_hid[:, 0:1], 1.0 / QMAX, ALU.mult, ALU.mult).then_inc(scale_step, 1)
            dve.wait_ge(scale_step, 1)
            v.tensor_scalar(s_o[:], a3[:], TINY, None, ALU.max).then_inc(scale_step, 1)
            dve.wait_ge(scale_step, 2)
            v.reciprocal(r_o[:], s_o[:]).then_inc(scale_step, 1)
            dve.wait_ge(scale_step, 3)
            v.tensor_scalar(k_o[:], r_o[:], s_hid[:, 0:1], None, ALU.mult).then_inc(scale_step, 1)
            dve.wait_ge(scale_step, 4)

            def quantise(t, b, h):
                dve.wait_ge(n_u_loaded[b], 8 * (t - b) + 16)
                wait(dve, high_done, 2 * (t - 1) + h + 1)
                wait(dve, low_done, 2 * (t - 1) + h + 1)
                v.scalar_tensor_tensor(n_h[:, h], n_p[:, bass.ds(t, 1), h * H:(h + 1) * H].rearrange("p o n -> p (o n)"), k_o[:, 0:1],
                                       n_u[b][:, h * H:(h + 1) * H], ALU.mult, ALU.mult).then_inc(rounded, 1)

            def low(t, h):
                dve.wait_ge(high_done, 2 * t + h + 1)
                v.tensor_tensor(h_lo[:, h], n_h[:, h], h_hi[:, h].bitcast(F32), ALU.subtract).then_inc(low_done, 1)

            def result(t, b):
                dve.wait_ge(transposed, t + 1)
                dve.wait_ge(x1_loaded[b], 8 * (t - b) + 16)
                wait(dve, stored[b], 8 * (t - b))
                for h in range(2):
                    rows = slice(h * NB // 2, (h + 1) * NB // 2)
                    last_op = v.scalar_tensor_tensor(res[b][:, rows], y[b][:, rows], y_scale[:, 0:1], x1[b][:, rows], ALU.mult, ALU.add)
                last_op.then_inc(res_done, 1)

            def step(t, b, last):
                if not last:
                    quantise(t + 1, 1 - b, 0)
                low(t, 1)
                if not last:
                    quantise(t + 1, 1 - b, 1)
                if not (isinstance(t, int) and t == 0):
                    result(t - 1, 1 - b)
                if not last:
                    low(t + 1, 0)

            quantise(0, 0, 0)
            quantise(0, 0, 1)
            low(0, 0)
            dve.wait_ge(tg_ready, 1)
            v.tensor_tensor(y_scale[:], s_o[:], tg[:], ALU.mult).then_inc(scale_step, 1)
            dve.wait_ge(scale_step, 5)
            two_buffers(dve, G, step)
            result(G - 1, 1)

        @block.tensor
        def _(pe):
            def half(t, b, h):
                pe.wait_ge(low_done, 2 * t + h + 1)
                if h == 0:
                    wait(pe, yT_copied, KC * (t - 1))
                parts = (h_hi, h_lo)
                for k in range(KC):
                    for j in range(HJ):
                        for n, (w, m) in enumerate(split(0, 1)):
                            at = (h * HJ + j) * D + k * P
                            last = nc.tensor.matmul(yT[b][k][:], wd[w][:, at:at + P], parts[m][:, h, j * T:(j + 1) * T],
                                                    start=(h == 0 and j == 0 and n == 0), stop=(h == 1 and j == HJ - 1 and n == 2),
                                                    skip_group_check=True)
                last.then_inc(half_done, 1)

            def transpose_y(t, b):
                pe.wait_ge(yT_copied, KC * (t + 1))
                wait(pe, res_done, t - 1)
                for e in range(NB):
                    for k in range(KC):
                        last = nc.tensor.transpose(y[b][:, e, k * P:(k + 1) * P], yT_sb[:, k, e * P:(e + 1) * P], ident[:])
                last.then_inc(transposed, 1)

            def step(t, b, last):
                half(t, b, 0)
                if not (isinstance(t, int) and t == 0):
                    transpose_y(t - 1, 1 - b)
                half(t, b, 1)

            two_buffers(pe, G, step)
            transpose_y(G - 1, 1)


def program(nc, x, ctx, mask, g_xattn, g_ffn, wq, wk, wv, wo, bo, w_gate, w_up, w_down, out):
    B, S, D = x.shape
    I = w_up.shape[0]
    G, IC, KC, T = B // NB, I // P, D // P, NB * P
    N = IC * T
    assert G % 2 == 0 and G >= 8

    def dram(name, shape, dt=F32):
        return nc.dram_tensor(name, shape, dt, kind="Internal").ap()

    x1_d = dram("x1_d", (P, G, NB, D))
    xn2_d = dram("xn2_d", (P, G, NB, D))
    n_x_d = dram("n_x_d", (P, G, D // P, T), I16)
    gate_d = dram("gate_d", (P, G, N))
    n_u_d = dram("n_u_d", (P, G, IC * T), I16)

    with ExitStack() as st:
        def sb(name, shape, dt=F32):
            return st.enter_context(nc.sbuf_tensor(name, shape, dt))

        amax_x = sb("amax_x", [P, G])
        amax_up, amax_hid = (sb(f"amax_{n}", [P, PAIRS * G]) for n in ("up", "hid"))
        ext_gate = sb("ext_gate", [P, 2, 2 * G])
        s_x, s_g, k_g, s_p, k_p, s_hid = (sb(n, [P, 1]) for n in ("s_x", "s_g", "k_g", "s_p", "k_p", "s_hid"))
        ident = sb("ident", [P, P])
        wd = [sb(f"wd_{n}", [P, IC * D], F32R) for n in ("hi", "lo")]
        w_raw = sb("w_raw", [P, 3 * IC * D])
        attention(nc, x, ctx, mask, g_xattn, wq, wk, wv, wo, bo, (w_up, w_gate, w_down), ident, x1_d, xn2_d, w_raw, amax_x)

        gate = sb("gate", [P, N])
        stage = [sb(f"stage{b}", [P, N]) for b in range(2)]
        with ExitStack() as st1:
            def sb1(name, shape, dt=F32, side="left"):
                return st1.enter_context(nc.sbuf_tensor(name, shape, dt, side=side))

            wup = [sb1(f"wup_{n}", [P, KC, I], F32R) for n in ("hi", "lo")]
            n_x = sb1("n_x", [P, 2, KC, T], I16)
            xT = [[sb1(f"xT{n}{b}", [P, KC, T], F32R) for n in ("hi", "lo")] for b in range(2)]
            gate_products(nc, w_raw, ident, xn2_d, n_x_d, gate_d, wup, wd, n_x, xT, [stage[0], gate], amax_x, ext_gate, s_x, G)
            gate_scales(nc, gate_d, gate, ext_gate, s_x, s_g, k_g, k_p, s_p, G, N)
            n_p = st.enter_context(nc.sbuf_tensor("n_p", [P, G, N], I16, side="right"))
            sig = w_raw[:, 0:N].rearrange("p (h n) -> p h n", h=2)
            x_wide = w_raw[:, N:N + KC * T].rearrange("p (k n) -> p k n", k=KC)
            ahead = Ahead(nc, st1)
            up_products(nc, n_x_d, gate_d, wup, n_x, xT, x_wide, gate[:].rearrange("p (h n) -> p h n", h=2), sig, stage,
                        n_p, ahead, amax_up, s_g, k_g, k_p, G, IC)

            half = N // 2
            n_u_last = [a[:, 0:half].bitcast(I16) for a in stage]
            x1 = [a[:, half:half + NB * D].rearrange("p (b d) -> p b d", d=D) for a in stage]
            loads = down_loads(nc, st, n_u_d, x1_d, n_u_last, x1, G)

            def prefetch(sp):
                for b in range(2):
                    loads[4](sp, b, b)
                    loads[5](sp, b, b)

            n_u = w_raw[:, 0:N].bitcast(I16).rearrange("p (b n) -> p b n", b=2)
            hidden_max(nc, n_x_d, n_u_d, wup, n_x, xT, x_wide, stage, n_u, gate, n_p, ahead, prefetch, amax_up, amax_hid,
                       s_x, s_p, s_hid, G, N)
        yT_sb = w_raw[:, 0:KC * T].rearrange("p (k n) -> p k n", k=KC)
        n_h = gate[:, 0:N // 2].bitcast(I16).rearrange("p (h n) -> p h n", h=2)
        res = [sb(f"res{b}", [P, NB, D]) for b in range(2)]
        down_products(nc, loads, g_ffn, ident, n_h, yT_sb, res, n_p, wd, out, amax_hid, s_hid, G, IC)


INPUTS = ["x", "ctx_1024", "mask_BxS2_bf0", "g_xattn", "g_ffn", "L0_xattn_Wq", "L0_xattn_Wk", "L0_xattn_Wv", "L0_xattn_Wo",
          "L0_xattn_bo", "L0_ffn_w_gate", "L0_ffn_w_up", "L0_ffn_w_down"]


def kernel(**inputs):
    import numpy as np
    import concourse.bacc as bacc
    from concourse.bass_utils import run_bass_kernel_spmd

    nc = bacc.Bacc("TRN2", target_bir_lowering=False, num_devices=1)
    arrays, args = {}, []
    for name in INPUTS:
        a = np.ascontiguousarray(inputs[name])
        arrays[f"in_{name}"] = a
        args.append(nc.dram_tensor(f"in_{name}", a.shape, mybir.dt.from_np(a.dtype), kind="ExternalInput").ap())
    out = nc.dram_tensor("out_x", inputs["x"].shape, F32, kind="ExternalOutput").ap()
    program(nc, *args, out)
    r = run_bass_kernel_spmd(nc, [arrays], core_ids=[0])
    return np.asarray(r.results[0]["out_x"])
```
